# Optimizing a Trainium2 kernel written in Bass

```python
import numpy as np
import jax
import jax.numpy as jnp

def _softmax(x, axis=-1):
    return jax.nn.softmax(x, axis=axis)

def _gelu(x):
    return jax.nn.gelu(x, approximate=True)

def _silu(x):
    return jax.nn.silu(x)

def _sigmoid(x):
    return jax.nn.sigmoid(x)

def _layernorm(x, axis=-1, eps=1e-05):
    m = jnp.mean(x, axis=axis, keepdims=True)
    v = jnp.var(x, axis=axis, keepdims=True)
    return (x - m) / jnp.sqrt(v + eps)

def _scatter_add(tgt, idx, src, axis=0):
    return tgt.at[idx].add(src)

def _segment_sum(src, seg, n):
    return jax.ops.segment_sum(src, seg, n)
kernel_name = 'mk_adaln_attn_ffn_d1_seqx_r4_f68725'

def setup_inputs(seed: int=0):
    np.random.seed(seed)
    _w = jnp.asarray

    def _rec_inputs():
        import jax
        import jax.numpy as jnp
        _rk = jax.random.key(seed)
        x = -1.394e-06 + 0.9999 * jax.random.normal(jax.random.fold_in(_rk, 1), (32, 64, 512), jnp.float32)
        _lenS = 64 - jax.random.randint(jax.random.fold_in(_rk, 7), (32,), 0, max(1, 64 // 4) + 1, jnp.int32)
        _lenS2 = 64 - jax.random.randint(jax.random.fold_in(_rk, 8), (32,), 0, max(1, 64 // 4) + 1, jnp.int32)
        cond_2048 = -0.00499425 + 1.0058 * jax.random.normal(jax.random.fold_in(_rk, 11), (32, 512), jnp.float32)
        return (x, cond_2048)
    x, cond_2048 = _rec_inputs()

    def _L0_cond_setup():
        import jax, jax.numpy as jnp
        import numpy as np
        B, T, D = (16, 128, 512)
        key = jax.random.key(seed)
        k0, k1, k2, k3 = jax.random.split(key, 4)
        scale = 1.0 / np.sqrt(D)
        return {'initial_state': jax.random.normal(k0, (B, D), jnp.float32), 'inputs': jax.random.normal(k1, (B, T, D), jnp.float32), 'W_ih': jax.random.normal(k2, (D, 3 * D), jnp.float32) * scale, 'W_hh': jax.random.normal(k3, (D, 3 * D), jnp.float32) * scale, 'b_ih': jnp.zeros((3 * D,), jnp.float32), 'b_hh': jnp.zeros((3 * D,), jnp.float32)}
    _L0_cond_all = _L0_cond_setup()
    _L0_cond_in = {k: v for k, v in _L0_cond_all.items() if k in ('W_ih', 'W_hh', 'b_ih', 'b_hh')}
    del _L0_cond_all

    def _L0_attn_setup():
        import jax, jax.numpy as jnp
        import numpy as np
        DIM = 512
        DIM_HEAD = 128
        HEADS = 16
        EPS = 1e-05

        def _rotate_half(t):
            d2 = t.shape[-1] // 2
            x1, x2 = (t[..., :d2], t[..., d2:])
            return jnp.concatenate([-x2, x1], axis=-1)

        def _rotary_pos(n, dim_head, dtype):
            inv_freq = 1.0 / 10000.0 ** (jnp.arange(0, dim_head, 2, dtype=jnp.float32) / dim_head)
            freqs = jnp.arange(n, dtype=jnp.float32)[:, None] * inv_freq[None, :]
            return jnp.concatenate([freqs, freqs], axis=-1).astype(dtype)
        key = jax.random.key(seed)
        ks = jax.random.split(key, 4)
        b, n = (2, 512)
        x = jax.random.normal(ks[0], (b, n, DIM), dtype=jnp.float32)
        gamma = jnp.ones((DIM,), dtype=jnp.float32)
        Wq = jax.random.normal(ks[1], (DIM, HEADS * DIM_HEAD), dtype=jnp.float32) * DIM ** (-0.5)
        Wkv = jax.random.normal(ks[2], (DIM, 2 * DIM_HEAD), dtype=jnp.float32) * DIM ** (-0.5)
        Wo = jax.random.normal(ks[3], (HEADS * DIM_HEAD, DIM), dtype=jnp.float32) * (HEADS * DIM_HEAD) ** (-0.5)
        return {'x': x, 'gamma': gamma, 'Wq': Wq, 'Wkv': Wkv, 'Wo': Wo}
    _L0_attn_all = _L0_attn_setup()
    _L0_attn_in = {k: v for k, v in _L0_attn_all.items() if k in ('gamma', 'Wq', 'Wkv', 'Wo')}
    del _L0_attn_all

    def _L0_cond2_setup():
        import jax, jax.numpy as jnp
        import numpy as np
        DT = 0.01
        EPSILON = 0.08
        ALPHA = 0.7
        BETA = 0.8
        CLAMP = 20.0
        B, T, N = (64, 128, 512)

        def _derivative(q, p, drive, coupling, bias):
            i_couple = jnp.tanh(q) @ coupling.T
            dq = q - q ** 3 / 3.0 - p + drive + i_couple + bias
            dp = EPSILON * (q + ALPHA - BETA * p)
            return (dq, dp)

        def _rk4_step(q, p, drive, coupling, bias):
            dq1, dp1 = _derivative(q, p, drive, coupling, bias)
            dq2, dp2 = _derivative(q + 0.5 * DT * dq1, p + 0.5 * DT * dp1, drive, coupling, bias)
            dq3, dp3 = _derivative(q + 0.5 * DT * dq2, p + 0.5 * DT * dp2, drive, coupling, bias)
            dq4, dp4 = _derivative(q + DT * dq3, p + DT * dp3, drive, coupling, bias)
            q_next = q + DT / 6.0 * (dq1 + 2 * dq2 + 2 * dq3 + dq4)
            p_next = p + DT / 6.0 * (dp1 + 2 * dp2 + 2 * dp3 + dp4)
            q_next = jnp.clip(q_next, -CLAMP, CLAMP)
            p_next = jnp.clip(p_next, -CLAMP, CLAMP)
            return (q_next, p_next)
        key = jax.random.key(seed)
        k1, k2, k3, k4 = jax.random.split(key, 4)
        return {'q0': jax.random.normal(k1, (B, N), dtype=jnp.float32), 'p0': jax.random.normal(k2, (B, N), dtype=jnp.float32), 'input_drive_seq': jax.random.normal(k3, (B, T, N), dtype=jnp.float32), 'coupling': jax.random.normal(k4, (N, N), dtype=jnp.float32) * 0.01, 'bias': jnp.zeros((N,), dtype=jnp.float32)}
    _L0_cond2_all = _L0_cond2_setup()
    _L0_cond2_in = {k: v for k, v in _L0_cond2_all.items() if k in ('coupling', 'bias')}
    del _L0_cond2_all

    def _L0_ffn_setup():
        import jax, jax.numpy as jnp
        import numpy as np
        FP8_MAX = 448.0
        GLOBAL_DIV = 448.0 * 6.0

        def _fp8(x):
            return x.astype(jnp.float8_e4m3fn).astype(jnp.float32)

        def _reorder_quantize_x(x, idx):
            scale = jnp.max(jnp.abs(x)) / GLOBAL_DIV
            xr = (x / scale)[:, idx]
            scale_x = jnp.max(jnp.abs(xr), axis=1, keepdims=True) / FP8_MAX
            qx = _fp8(xr / scale_x)
            return (qx, scale_x, scale)

        def _qlinear(qx, scale_x, scale, W, idx, out_idx=None):
            Wr = W[:, idx]
            w_scale = jnp.max(jnp.abs(Wr), axis=1, keepdims=True) / FP8_MAX
            qw = _fp8(Wr / w_scale)
            y = qx * scale_x @ (qw * w_scale).T * scale
            if out_idx is not None:
                y = y[:, out_idx]
            return y
        key = jax.random.key(seed)
        ks = jax.random.split(key, 6)
        B, S, H, I = (2, 256, 512, 1408)
        return {'x': jax.random.normal(ks[0], (B, S, H), jnp.float32), 'w_gate': jax.random.normal(ks[1], (I, H), jnp.float32) * 0.02, 'w_up': jax.random.normal(ks[2], (I, H), jnp.float32) * 0.02, 'w_down': jax.random.normal(ks[3], (H, I), jnp.float32) * 0.02, 'up_reorder_index': jax.random.permutation(ks[4], jnp.arange(H, dtype=jnp.int64)), 'down_reorder_index': jax.random.permutation(ks[5], jnp.arange(I, dtype=jnp.int64))}
    _L0_ffn_all = _L0_ffn_setup()
    _L0_ffn_in = {k: v for k, v in _L0_ffn_all.items() if k in ('w_gate', 'w_up', 'w_down', 'up_reorder_index', 'down_reorder_index')}
    del _L0_ffn_all
    return {'x': x, 'cond_2048': cond_2048, 'L0_cond_W_ih': _L0_cond_in['W_ih'], 'L0_cond_W_hh': _L0_cond_in['W_hh'], 'L0_cond_b_ih': _L0_cond_in['b_ih'], 'L0_cond_b_hh': _L0_cond_in['b_hh'], 'L0_attn_gamma': _L0_attn_in['gamma'], 'L0_attn_Wq': _L0_attn_in['Wq'], 'L0_attn_Wkv': _L0_attn_in['Wkv'], 'L0_attn_Wo': _L0_attn_in['Wo'], 'L0_cond2_coupling': _L0_cond2_in['coupling'], 'L0_cond2_bias': _L0_cond2_in['bias'], 'L0_ffn_w_gate': _L0_ffn_in['w_gate'], 'L0_ffn_w_up': _L0_ffn_in['w_up'], 'L0_ffn_w_down': _L0_ffn_in['w_down'], 'L0_ffn_up_reorder_index': _L0_ffn_in['up_reorder_index'], 'L0_ffn_down_reorder_index': _L0_ffn_in['down_reorder_index']}

def reference(x, cond_2048, L0_cond_W_ih, L0_cond_W_hh, L0_cond_b_ih, L0_cond_b_hh, L0_attn_gamma, L0_attn_Wq, L0_attn_Wkv, L0_attn_Wo, L0_cond2_coupling, L0_cond2_bias, L0_ffn_w_gate, L0_ffn_w_up, L0_ffn_w_down, L0_ffn_up_reorder_index, L0_ffn_down_reorder_index):
    import jax
    import jax.numpy as jnp

    def _L0_cond_ref(initial_state, inputs, W_ih, W_hh, b_ih, b_hh):
        import jax, jax.numpy as jnp
        import numpy as np
        B, T, D = (16, 128, 512)
        "ScanOverTime(GRU cell): sequential per-timestep module call with\n            dict-state passing; merge_dict_trees stacks the per-step\n            'state_predicted' tensors along axis=1 -> [B, T, D]."

        def cell(h, x):
            gi = x @ W_ih + b_ih
            gh = h @ W_hh + b_hh
            i_r, i_z, i_n = jnp.split(gi, 3, axis=-1)
            h_r, h_z, h_n = jnp.split(gh, 3, axis=-1)
            r = jax.nn.sigmoid(i_r + h_r)
            z = jax.nn.sigmoid(i_z + h_z)
            n = jnp.tanh(i_n + r * h_n)
            h_new = (1.0 - z) * n + z * h
            return (h_new, h_new)
        xs = jnp.swapaxes(inputs, 0, 1)
        _, hs = jax.lax.scan(cell, initial_state, xs)
        return jnp.swapaxes(hs, 0, 1)

    def _L0_attn_ref(x, gamma, Wq, Wkv, Wo):
        import jax, jax.numpy as jnp
        import numpy as np
        DIM = 512
        DIM_HEAD = 128
        HEADS = 16
        EPS = 1e-05

        def _rotate_half(t):
            d2 = t.shape[-1] // 2
            x1, x2 = (t[..., :d2], t[..., d2:])
            return jnp.concatenate([-x2, x1], axis=-1)

        def _rotary_pos(n, dim_head, dtype):
            inv_freq = 1.0 / 10000.0 ** (jnp.arange(0, dim_head, 2, dtype=jnp.float32) / dim_head)
            freqs = jnp.arange(n, dtype=jnp.float32)[:, None] * inv_freq[None, :]
            return jnp.concatenate([freqs, freqs], axis=-1).astype(dtype)
        b, n, dim = x.shape
        h, dh = (HEADS, DIM_HEAD)
        scale = dh ** (-0.5)
        mu = jnp.mean(x, axis=-1, keepdims=True)
        var = jnp.var(x, axis=-1, keepdims=True)
        xn = (x - mu) * jax.lax.rsqrt(var + EPS) * gamma
        q = (xn @ Wq).reshape(b, n, h, dh).transpose(0, 2, 1, 3)
        kv = xn @ Wkv
        k, v = (kv[..., :dh], kv[..., dh:])
        pos = _rotary_pos(n, dh, x.dtype)
        cos, sin = (jnp.cos(pos), jnp.sin(pos))
        q = q * cos + _rotate_half(q) * sin
        k = k * cos + _rotate_half(k) * sin
        q = q * scale
        sim = jnp.einsum('bhid,bjd->bhij', q, k)
        causal = jnp.triu(jnp.ones((n, n), dtype=bool), k=1)
        neg = -jnp.finfo(sim.dtype).max
        sim = jnp.where(causal, neg, sim)
        sim = sim - jax.lax.stop_gradient(jnp.max(sim, axis=-1, keepdims=True))
        attn = jax.nn.softmax(sim, axis=-1)
        out = jnp.einsum('bhij,bjd->bhid', attn, v)
        out = out.transpose(0, 2, 1, 3).reshape(b, n, h * dh)
        return out @ Wo

    def _L0_cond2_ref(q0, p0, input_drive_seq, coupling, bias):
        import jax, jax.numpy as jnp
        import numpy as np
        DT = 0.01
        EPSILON = 0.08
        ALPHA = 0.7
        BETA = 0.8
        CLAMP = 20.0
        B, T, N = (64, 128, 512)

        def _derivative(q, p, drive, coupling, bias):
            i_couple = jnp.tanh(q) @ coupling.T
            dq = q - q ** 3 / 3.0 - p + drive + i_couple + bias
            dp = EPSILON * (q + ALPHA - BETA * p)
            return (dq, dp)

        def _rk4_step(q, p, drive, coupling, bias):
            dq1, dp1 = _derivative(q, p, drive, coupling, bias)
            dq2, dp2 = _derivative(q + 0.5 * DT * dq1, p + 0.5 * DT * dp1, drive, coupling, bias)
            dq3, dp3 = _derivative(q + 0.5 * DT * dq2, p + 0.5 * DT * dp2, drive, coupling, bias)
            dq4, dp4 = _derivative(q + DT * dq3, p + DT * dp3, drive, coupling, bias)
            q_next = q + DT / 6.0 * (dq1 + 2 * dq2 + 2 * dq3 + dq4)
            p_next = p + DT / 6.0 * (dp1 + 2 * dp2 + 2 * dp3 + dp4)
            q_next = jnp.clip(q_next, -CLAMP, CLAMP)
            p_next = jnp.clip(p_next, -CLAMP, CLAMP)
            return (q_next, p_next)
        drive_tbn = jnp.swapaxes(input_drive_seq, 0, 1)

        def scan_fn(carry, drive):
            q, p = carry
            q, p = _rk4_step(q, p, drive, coupling, bias)
            return ((q, p), q)
        (_, _), q_trace_tbn = jax.lax.scan(scan_fn, (q0, p0), drive_tbn)
        return jnp.swapaxes(q_trace_tbn, 0, 1)

    def _L0_ffn_ref(x, w_gate, w_up, w_down, up_reorder_index, down_reorder_index):
        import jax, jax.numpy as jnp
        import numpy as np
        FP8_MAX = 448.0
        GLOBAL_DIV = 448.0 * 6.0

        def _fp8(x):
            return x.astype(jnp.float8_e4m3fn).astype(jnp.float32)

        def _reorder_quantize_x(x, idx):
            scale = jnp.max(jnp.abs(x)) / GLOBAL_DIV
            xr = (x / scale)[:, idx]
            scale_x = jnp.max(jnp.abs(xr), axis=1, keepdims=True) / FP8_MAX
            qx = _fp8(xr / scale_x)
            return (qx, scale_x, scale)

        def _qlinear(qx, scale_x, scale, W, idx, out_idx=None):
            Wr = W[:, idx]
            w_scale = jnp.max(jnp.abs(Wr), axis=1, keepdims=True) / FP8_MAX
            qw = _fp8(Wr / w_scale)
            y = qx * scale_x @ (qw * w_scale).T * scale
            if out_idx is not None:
                y = y[:, out_idx]
            return y
        B, S, H = x.shape
        xf = x.reshape(B * S, H)
        qx, sx, sc = _reorder_quantize_x(xf, up_reorder_index)
        g = _qlinear(qx, sx, sc, w_gate, up_reorder_index, out_idx=down_reorder_index)
        u = _qlinear(qx, sx, sc, w_up, up_reorder_index, out_idx=down_reorder_index)
        t = jax.nn.silu(g) * u
        qt, st, sct = _reorder_quantize_x(t, down_reorder_index)
        y = _qlinear(qt, st, sct, w_down, down_reorder_index)
        return y.reshape(B, S, H)
    x = x + _L0_attn_ref(_L0_cond_ref(cond_2048, x, L0_cond_W_ih, L0_cond_W_hh, L0_cond_b_ih, L0_cond_b_hh), L0_attn_gamma, L0_attn_Wq, L0_attn_Wkv, L0_attn_Wo)
    x = x + _L0_ffn_ref(_L0_cond2_ref(cond_2048, cond_2048, x, L0_cond2_coupling, L0_cond2_bias), L0_ffn_w_gate, L0_ffn_w_up, L0_ffn_w_down, L0_ffn_up_reorder_index, L0_ffn_down_reorder_index)
    return x

_drawn_inputs = setup_inputs


def setup_inputs(seed=0):
    import zlib

    import numpy as np

    out = dict(_drawn_inputs(seed))
    spreads = {'L0_cond_b_ih': (0.0, 0.1),
     'L0_cond_b_hh': (0.0, 0.1),
     'L0_attn_gamma': (1.0, 0.2),
     'L0_cond2_bias': (0.0, 0.8)}
    factors = {'L0_cond2_coupling': 8.0}
    for name, (base, spread) in spreads.items():
        noise = np.random.default_rng([zlib.crc32(name.encode()), seed]).standard_normal(out[name].shape)
        drawn = base * np.exp(spread * noise) if base else spread * noise
        out[name] = jnp.asarray(drawn.astype(out[name].dtype))
    for name, factor in factors.items():
        out[name] = (out[name] * factor).astype(out[name].dtype)
    return out
```

```python
from contextlib import ExitStack

import concourse.bass as bass
from concourse import mybir

ALU = mybir.AluOpType
ACT = mybir.ActivationFunctionType
AX = mybir.AxisListType
F32 = mybir.dt.float32
BF16 = mybir.dt.bfloat16
U32 = mybir.dt.uint32
I32 = mybir.dt.int32

P = 128
B, T, D = 32, 64, 512
NC = D // P
GATES = 3
HEADS, DH = 16, 128
HP = HEADS // 2
TOK = B * T
BLK_B = 4
BLK = BLK_B * T
NBLK = B // BLK_B
PAIRS = BLK_B // 2
LN_TOK = 512
NLN = TOK // LN_TOK
INNER = 1408
IC = INNER // P
GU_N = 352
GU_T = INNER // GU_N
TILE_T = P // B
NTILE = T // TILE_T
PV_BANKS = (5, 2, 3)
LN_EPS = 1e-5
DT, EPS, ALPHA, BETA, CLAMP = 0.01, 0.08, 0.7, 0.8, 20.0
FP8_MAX = 448.0
FP8_TINY = 2.0 ** -6
ROUND_AT = 1.5 * 2.0 ** 20
EXP_BITS = 0x7F800000
WORDS = 48 * 1024 - 256


class Steps:

    def __init__(self, eng, sem, base):
        self.eng, self.sem, self.base, self.n = eng, sem, base, 0

    def did(self, ins):
        ins.then_inc(self.sem, 1)
        self.n += 1
        return self.n

    def need(self, n):
        self.eng.wait_ge(self.sem, self.base + n)


class Words:

    def __init__(self, at, end):
        self.at, self.end = at, end

    def take(self, n):
        a = self.at
        self.at += n
        assert self.at <= self.end, (self.at, self.end)
        return a


def gru_attn_rk4_ffn(nc, xT, x, cond_quad, cond_T, W_ih, W_hh, bias_ih, bias_hh, sel, gamma, Wq, Wkv, Wo,
                     couplingT, bias_quad, w_gate, w_up, w_down, down_idx, ident, ones, rot, trig, mask,
                     x1_scr, q_scr, out):
    with ExitStack() as ctx:
        mem = ctx.enter_context(nc.sbuf_tensor("mem", [P, WORDS], F32))
        ps = ctx.enter_context(nc.psum_tensor("ps", [P, 8, 512], F32))

        def sem(name):
            return ctx.enter_context(nc.semaphore(name))

        def f32(a, *dims):
            n = 1
            for d in dims:
                n *= d
            v = mem[:, a:a + n]
            if len(dims) == 2:
                v = v.rearrange("p (a b) -> p a b", a=dims[0])
            if len(dims) == 3:
                v = v.rearrange("p (a b c) -> p a b c", a=dims[0], b=dims[1])
            return v

        def bf16(a, *dims):
            n = 1
            for d in dims:
                n *= d
            v = mem[:, a:a + n // 2].bitcast(BF16)
            if len(dims) == 2:
                v = v.rearrange("p (a b) -> p a b", a=dims[0])
            return v

        w = Words(0, WORDS)
        a_hs = w.take(NC * TOK)
        hsT = f32(a_hs, NC, TOK)
        a_ih = w.take(NC * GATES * D)
        a_hh = w.take(NC * GATES * D)
        wih = f32(a_ih, NC, GATES * D)
        whh = f32(a_hh, NC, GATES * D)
        wq = f32(w.take(NC * HEADS * DH), NC, HEADS * DH)
        wo = f32(w.take(HEADS * D), HEADS, D)
        wkv = f32(w.take(NC * 2 * DH), NC, 2 * DH)
        a_p2 = w.at
        q_cos = f32(a_ih, BLK_B, HEADS * T)
        q_sin = f32(a_ih + HEADS * BLK, BLK_B, HEADS * T)
        aoT = f32(a_ih + 2 * HEADS * BLK, HEADS, BLK)
        rstd = f32(w.take(TOK), TOK)
        xnb = f32(w.take(NC * BLK), NC, BLK)
        probs = f32(w.take(PAIRS * HP * P), PAIRS, HP * P)
        pT = f32(w.take(HP * P), HP * P)
        xres = f32(w.take(PAIRS * D), PAIRS, D)
        a_k = w.take(3 * BLK)
        kc, kraw, kr, krr = f32(a_k, BLK), f32(a_k + BLK, BLK), f32(a_k + 2 * BLK, BLK), f32(w.take(BLK), BLK)
        vtok = f32(w.take(PAIRS * DH), PAIRS, DH)
        smax = f32(w.take(PAIRS * 2 * HP), PAIRS * 2, HP)
        ssum = f32(w.take(PAIRS * 2 * HP), PAIRS * 2, HP)
        gam = f32(w.take(NC), NC)
        a_const = w.take(P + P + 2 * P + 4 * T + T)
        identf = f32(a_const, P)
        mean_w = f32(a_const + P, P)
        rots = f32(a_const + 2 * P, 2, P)
        trigs = f32(a_const + 4 * P, 4, T)
        masks = f32(a_const + 4 * P + 4 * T, T)
        g = Words(a_p2, w.at)
        xt = [f32(g.take(NC * B), NC, B) for _ in range(2)]
        hT = [f32(g.take(NC * B), NC, B) for _ in range(2)]
        h_q = [f32(g.take(P), P) for _ in range(2)]
        rz = [f32(g.take(2 * P), 2, P) for _ in range(2)]
        rh, npre, nval, zh, omz, nz = (f32(g.take(P), P) for _ in range(6))
        a_bg = g.take(512 + 256 + 256 + 256 + 512 + 256)
        assert g.at <= a_const
        bg = f32(a_bg, 512)
        bres = f32(a_bg + 512 + 256 + 256 + 256, 512)
        bparts = [bf16(a_bg + 512 + 256 * i, 512) for i in range(3)]
        sel_f = f32(a_bg + 512 + 3 * 256 + 512, P)
        sel_b = bf16(a_bg + 512 + 3 * 256 + 512 + P, P)
        sq = f32(a_ih, NC, LN_TOK)
        var = f32(a_ih + NC * LN_TOK, LN_TOK)
        root = f32(a_ih + NC * LN_TOK + LN_TOK, LN_TOK)
        newt = f32(a_ih + NC * LN_TOK + 2 * LN_TOK, LN_TOK)

        w = Words(0, a_const)
        ct = f32(w.take(NC * D), NC, D)
        wgT = bf16(w.take(NC * INNER // 2), NC, INNER)
        wuT = bf16(w.take(NC * INNER // 2), NC, INNER)
        wdT = bf16(w.take(IC * D // 2), IC, D)
        gs_row, us_row, ds_row = f32(w.take(INNER), INNER), f32(w.take(INNER), INNER), f32(w.take(D), D)
        id_b = bf16(w.take(P // 2), P)
        ones_sb = f32(w.take(P), P)
        biasq = f32(w.take(P), P)
        drive = [f32(w.take(P), P) for _ in range(4)]
        qn = [f32(w.take(P), P) for _ in range(4)]
        pn = [f32(w.take(P), P) for _ in range(2)]
        qst = [f32(w.take(P), P) for _ in range(3)]
        pst = [f32(w.take(P), P) for _ in range(3)]
        qsT = f32(w.take(P), NC, B)
        thT = f32(w.take(P), NC, B)
        (cube, ebuf, gbuf, dsum, hA, hA2, nq, a1, a2, a3, xfin, qpre, ubuf, pcA, pcA2, np_, p1, p2, p3, p4, p5, d6) = (
            f32(w.take(P), P) for _ in range(22))
        a_f = w.at
        wraw = f32(w.take(2 * D), 2, D)
        wv = f32(w.take(INNER), INNER)
        wexp = f32(w.take(INNER), INNER)
        wround = f32(w.take(INNER), INNER)
        wq8 = bf16(w.take(INNER // 2), INNER)
        diag = f32(w.take(P), P)
        wdraw = f32(w.take(INNER), INNER)
        idx = f32(w.take(1), 1)
        am, sx, rs = (f32(w.take(2), 2) for _ in range(3))
        f = Words(a_f + 8192, a_const)
        qt = f32(f.take(D), D)
        x1t = f32(f.take(D), D)
        qx8 = bf16(f.take(D // 2), D)
        qxT = bf16(f.take(D // 2), NC, P)
        gsc = [f32(f.take(GU_N), GU_N) for _ in range(2)]
        usc = [f32(f.take(GU_N), GU_N) for _ in range(2)]
        sig = [f32(f.take(GU_N), GU_N) for _ in range(2)]
        tt = f32(f.take(INNER), INNER)
        t8 = bf16(f.take(INNER // 2), INNER)
        t8T = bf16(f.take(INNER // 2), IC, P)
        ysc = f32(f.take(D), D)
        yout = f32(f.take(D), D)
        tam, tsx, trs, xam, xsx, xrs = (f32(f.take(1), 1) for _ in range(6))
        f.take(16)

        (w_gru, w_att, c_ld, xt_ld0, xt_ld1, h0_ld, st_ld, wraw_ld, idx_ld, wd_ld, x_ld, x1_wr, q_ld, x1_ld,
         o_wr, ct_ld) = (sem(n) for n in (
             "w_gru", "w_att", "c_ld", "xt_ld0", "xt_ld1", "h0_ld", "st_ld", "wraw_ld", "idx_ld", "wd_ld", "x_ld",
             "x1_wr", "q_ld", "x1_ld", "o_wr", "ct_ld"))
        xt_ld = [xt_ld0, xt_ld1]
        q_wr = [sem(f"q_wr{i}") for i in range(4)]
        drive_ld = [sem(f"drive_ld{i}") for i in range(4)]
        bias_split, gx_mm, gates_mm, rz_done, rh_done, npre_done, n_done, zh_done, omz_done, nz_done, h_done, hT_done, hs_cp = (
            sem(n) for n in ("bias_split", "gx_mm", "gates_mm", "rz_done", "rh_done", "npre_done", "n_done",
                             "zh_done", "omz_done", "nz_done", "h_done", "hT_done", "hs_cp"))
        mean_mm, xc_done, sq_done, var_mm, ve_done, root_done, ln_v = (
            sem(n) for n in ("mean_mm", "xc_done", "sq_done", "var_mm", "ve_done", "root_done", "ln_v"))
        (xn_done, k_mm, v_mm, q_mm, rot_mm, rot2_mm, kraw_cp, kc_done, ks_done, kr_done, krr_cp, v_cp, q_ev, s_mm,
         masked, max_done, shifted, exp_done, sum_done, inv_done, p_done, pT_mm, pT_cp, pv_mm, ao_cp, wo_mm,
         x1_done) = (sem(n) for n in (
             "xn_done", "k_mm", "v_mm", "q_mm", "rot_mm", "rot2_mm", "kraw_cp", "kc_done", "ks_done", "kr_done",
             "krr_cp", "v_cp", "q_ev", "s_mm", "masked", "max_done", "shifted", "exp_done", "sum_done", "inv_done",
             "p_done", "pT_mm", "pT_cp", "pv_mm", "ao_cp", "wo_mm", "x1_done"))
        w_v, w_scaled, w_q8, w_diag, w_tr, w_bc, w_cp, idb_done, gather_go = (
            sem(n) for n in ("w_v", "w_scaled", "w_q8", "w_diag", "w_tr", "w_bc", "w_cp", "idb_done", "gather_go"))
        (rk_qT, rk_th, rk_mm, rk_sq, rk_v, rk_q) = (sem(n) for n in ("rk_qT", "rk_th", "rk_mm", "rk_sq", "rk_v", "rk_q"))
        (f_v, f_q8, f_qT, f_qTcp, f_gu, f_scaled, f_sig, f_gated, f_t8, f_tT, f_tTcp, f_y, f_out) = (
            sem(n) for n in ("f_v", "f_q8", "f_qT", "f_qTcp", "f_gu", "f_scaled", "f_sig", "f_gated", "f_t8",
                             "f_tT", "f_tTcp", "f_y", "f_out"))

        PRIMED = 1
        block = ctx.enter_context(nc.Block())
        N_CONST = 10

        @block.sync
        def _(sp):
            sp.dma_start(wih, W_ih.rearrange("p (c n) -> p c n", c=NC)).then_inc(w_gru, 16)
            gate_of = lambda a, lo, hi: a[lo:hi].rearrange("g j n -> j g n")
            sp.dma_start(bg[0:NC, 0:P], bias_ih[2]).then_inc(c_ld, 16)
            sp.dma_start(bg[0:NC, P:3 * P].rearrange("j (g n) -> j g n", g=2), gate_of(bias_ih, 0, 2)).then_inc(c_ld, 16)
            sp.dma_start(bg[0:NC, 3 * P:], bias_hh[2]).then_inc(c_ld, 16)
            sp.dma_start(bres[0:NC, 0:2 * P].rearrange("j (g n) -> j g n", g=2), gate_of(bias_hh, 0, 2)).then_inc(c_ld, 16)
            sp.dma_start(sel_f[0:NC, :], sel).then_inc(c_ld, 16)
            sp.dma_start(xt[0], xT[0].rearrange("p (c b) -> p c b", c=NC)).then_inc(xt_ld[0], 16)
            sp.dma_start(xt[1], xT[1].rearrange("p (c b) -> p c b", c=NC)).then_inc(xt_ld[1], 16)
            sp.dma_start(hT[1], cond_T.rearrange("p (c b) -> p c b", c=NC)).then_inc(h0_ld, 16)
            sp.dma_start(h_q[1], cond_quad).then_inc(h0_ld, 16)
            sp.dma_start(whh, W_hh.rearrange("p (c n) -> p c n", c=NC)).then_inc(w_gru, 16)
            sp.dma_start(identf, ident).then_inc(c_ld, 16)
            sp.dma_start(mean_w, ones[0]).then_inc(c_ld, 16)
            sp.dma_start(rots, rot.rearrange("r p m -> p r m")).then_inc(c_ld, 16)
            sp.dma_start(trigs, trig.rearrange("r p m -> p r m")).then_inc(c_ld, 16)
            sp.dma_start(masks, mask).then_inc(c_ld, 16)
            sp.dma_start(wq, Wq.rearrange("p (c n) -> p c n", c=NC)).then_inc(w_att, 16)
            sp.dma_start(wkv, Wkv.rearrange("p (c n) -> p c n", c=NC)).then_inc(w_att, 16)
            sp.dma_start(wo, Wo.rearrange("p (h n) -> p h n", h=HEADS)).then_inc(w_att, 16)
            with sp.Fori(1, T // 2) as i:
                for par in range(2):
                    sp.wait_ge(gx_mm, 2 * i + par - 1)
                    sp.dma_start(xt[par], xT[bass.ds(2 * i + par, 1)].rearrange("a p (c b) -> p (a c) b", c=NC)).then_inc(xt_ld[par], 16)
            sp.wait_ge(hs_cp, PRIMED + T)
            sp.dma_start(gam, gamma).then_inc(st_ld, 16)

            def x_rows(blk):
                for pr in range(PAIRS):
                    src = x[bass.ds(blk * BLK + pr * P, P), :]
                    sp.dma_start(xres[:, pr, :], src).then_inc(x_ld, 16)

            def x1_rows(blk):
                for pr in range(PAIRS):
                    sp.wait_ge(x1_done, PRIMED + PAIRS * blk + pr + 1)
                    for b2 in range(2):
                        dst = x1_scr[:, :, bass.ds(blk * BLK_B + 2 * pr + b2, 1), :]
                        src = xres[64 * b2:64 * b2 + 64, pr, :].rearrange("p (j a n) -> p j a n", j=NC, a=1)
                        sp.dma_start(dst, src).then_inc(x1_wr, 16)
            x_rows(0)
            with sp.Fori(0, NBLK - 1) as blk:
                x1_rows(blk)
                sp.wait_ge(x1_wr, 16 * 2 * PAIRS * (blk + 1))
                x_rows(blk + 1)
            x1_rows(NBLK - 1)
            sp.dma_start(ct, couplingT.rearrange("p (c n) -> p c n", c=NC)).then_inc(ct_ld, 16)
            sp.dma_start(ones_sb, ones[1]).then_inc(ct_ld, 16)
            sp.dma_start(biasq, bias_quad).then_inc(ct_ld, 16)
            sp.dma_start(qn[3], cond_quad).then_inc(ct_ld, 16)
            sp.dma_start(pn[1], cond_quad).then_inc(ct_ld, 16)
            sp.dma_start(idx.bitcast(I32), down_idx[0:P, :]).then_inc(idx_ld, 16)
            sp.dma_start(wdraw, w_down[0:P, :]).then_inc(wd_ld, 16)
            with sp.Fori(1, IC) as i:
                sp.wait_ge(wraw_ld, 32 * i)
                sp.dma_start(idx.bitcast(I32), down_idx[bass.ds(i * P, P), :]).then_inc(idx_ld, 16)
            with sp.Fori(1, NC) as i:
                sp.wait_ge(w_scaled, PRIMED + 2 * IC + i)
                sp.dma_start(wdraw, w_down[bass.ds(i * P, P), :]).then_inc(wd_ld, 16)

            sp.wait_ge(x1_wr, 16 * B)
            for s in range(4):
                sp.dma_start(drive[s], x1_scr[s].rearrange("j b n -> (j b) n")).then_inc(drive_ld[s], 16)

            def q_store(i, s):
                sp.wait_ge(rk_q, 4 * i + s + 1)
                sp.dma_start(q_scr[bass.ds(4 * i + s, 1)].rearrange("a j b n -> (a j b) n"), qn[s]).then_inc(q_wr[s], 16)
            with sp.Fori(0, T // 4 - 1) as i:
                for s in range(4):
                    q_store(i, s)
                    sp.dma_start(drive[s], x1_scr[bass.ds(4 * i + 4 + s, 1)].rearrange("a j b n -> (a j b) n")).then_inc(drive_ld[s], 16)
            for s in range(4):
                q_store(T // 4 - 1, s)
            for s in range(4):
                sp.wait_ge(q_wr[s], PRIMED + 16 * T // 4)
            with sp.Fori(0, NTILE) as i:
                sp.wait_ge(f_q8, PRIMED + i)
                for s in range(TILE_T):
                    sp.dma_start(qt[32 * s:32 * s + 32, :].rearrange("p (j n) -> p j n", j=NC),
                                 q_scr[bass.ds(i * TILE_T + s, 1)].rearrange("a j b n -> (a b) j n")).then_inc(q_ld, 16)
                sp.wait_ge(f_out, PRIMED + i)
                for s in range(TILE_T):
                    sp.dma_start(x1t[32 * s:32 * s + 32, :].rearrange("p (j n) -> p j n", j=NC),
                                 x1_scr[bass.ds(i * TILE_T + s, 1)].rearrange("a j b n -> (a b) j n")).then_inc(x1_ld, 16)
                sp.wait_ge(f_out, PRIMED + i + 1)
                for s in range(TILE_T):
                    sp.dma_start(out[:, bass.ds(i * TILE_T + s, 1), :].rearrange("b a n -> (b a) n"),
                                 yout[32 * s:32 * s + 32, :]).then_inc(o_wr, 16)
            sp.wait_ge(o_wr, PRIMED + 16 * TILE_T * NTILE)

        @block.gpsimd
        def _(pool):
            for s_ in (hs_cp, x1_done, f_q8, f_out, w_tr, w_bc, w_scaled, o_wr, *q_wr):
                pool.sem_inc(s_, PRIMED)
            with pool.Fori(0, T // 2) as i:
                for par in range(2):
                    t = 2 * i + par
                    pool.wait_ge(hT_done, t + 1)
                    pool.tensor_copy(hsT.rearrange("p c (b t) -> p c b t", t=T)[:, :, :, bass.ds(t, 1)],
                                     hT[par].rearrange("p c (b a) -> p c b a", a=1)).then_inc(hs_cp, 1)
            pool.wait_ge(x1_wr, 16 * B)
            with pool.Fori(0, IC) as i:
                pool.wait_ge(idx_ld, 16 * (i + 1))
                pool.wait_ge(w_scaled, PRIMED + 2 * i)
                pool.sem_inc(gather_go, 1)
                for k, src in enumerate((w_gate, w_up)):
                    pool.indirect_dma_start(out=wraw[:, k, :], out_offset=None, in_=src,
                                            in_offset=bass.IndirectOffsetOnAxis(ap=idx.bitcast(U32), axis=0)).then_inc(wraw_ld, 16)

        @block.tensor
        def _(pe):
            pe.wait_ge(bias_split, 6)
            pe.wait_ge(w_gru, 16 * 2)

            def x_part(t, par, prev):
                pe.wait_ge(xt_ld[par], 8 * (t - par) + 16)
                if prev:
                    pe.wait_ge(npre_done, t - 1)
                for k in range(3):
                    pe.matmul(ps[:, par, :], sel_b[0:NC, :], bparts[k][0:NC, :], start=(k == 0), stop=False,
                              skip_group_check=True)
                for c in range(NC):
                    for j in range(NC):
                        mm = pe.matmul(ps[32 * j:32 * j + 32, par, 0:3 * P].rearrange("p (g n) -> p g n", g=3), xt[par][:, c, :],
                                       wih[:, c, :].rearrange("p (g j n) -> p g j n", g=3, j=NC)[:, :, j, :],
                                       start=False, stop=False, skip_group_check=True, tile_position=(0, 32 * j))
                mm.then_inc(gx_mm, 1)

            def h_part(t, par):
                for c in range(NC):
                    for j in range(NC):
                        mm = pe.matmul(ps[32 * j:32 * j + 32, par, P:4 * P].rearrange("p (g n) -> p g n", g=3), hT[1 - par][:, c, :],
                                       whh[:, c, :].rearrange("p (g j n) -> p g j n", g=3, j=NC)[:, :, j, :],
                                       start=False, stop=(c == NC - 1), skip_group_check=True, tile_position=(0, 32 * j))
                mm.then_inc(gates_mm, 1)
            x_part(0, 0, False)
            x_part(1, 1, False)
            pe.wait_ge(h0_ld, 32)
            h_part(0, 0)
            with pe.Fori(1, T // 2) as i:
                x_part(2 * i, 0, True)
                pe.wait_ge(hT_done, 2 * i - 1)
                h_part(2 * i - 1, 1)
                x_part(2 * i + 1, 1, True)
                pe.wait_ge(hT_done, 2 * i)
                h_part(2 * i, 0)
            pe.wait_ge(hT_done, T - 1)
            h_part(T - 1, 1)

            pe.wait_ge(hs_cp, PRIMED + T)
            pe.wait_ge(c_ld, 16 * N_CONST)
            with pe.Fori(0, NLN) as i:
                for c in range(NC):
                    mm = pe.matmul(ps[:, 0, :], mean_w, hsT[:, c, bass.ds(i * LN_TOK, LN_TOK)], start=(c == 0), stop=(c == NC - 1))
                mm.then_inc(mean_mm, 1)
                pe.wait_ge(sq_done, i + 1)
                for c in range(NC):
                    mm = pe.matmul(ps[:, 1, :], mean_w, sq[:, c, :], start=(c == 0), stop=(c == NC - 1))
                mm.then_inc(var_mm, 1)
                pe.wait_ge(ve_done, i + 1)

            def out_proj(blk):
                pe.wait_ge(x1_done, PRIMED + PAIRS * blk)
                for pr in range(PAIRS):
                    pe.wait_ge(ao_cp, 4 * (PAIRS * blk + pr + 1))
                    for h in range(HEADS):
                        mm = pe.matmul(ps[:, 6 + pr, :], aoT[:, h, pr * P:pr * P + P], wo[:, h, :], start=(h == 0), stop=(h == HEADS - 1))
                    mm.then_inc(wo_mm, 1)

            def q_heads(blk, h0, h1):
                for h in range(h0, h1):
                    bank = h % 2
                    if h >= 2:
                        pe.wait_ge(q_ev, 2 * (HEADS * blk + h - 1))
                    for c in range(NC):
                        mm = pe.matmul(ps[:, bank, 0:BLK], wq[:, c, h * DH:(h + 1) * DH], xnb[:, c, :], start=(c == 0), stop=(c == NC - 1))
                    mm.then_inc(q_mm, 1)

            def attn_block(blk, first):
                pe.wait_ge(xn_done, blk + 1)
                if not first:
                    pe.wait_ge(x1_done, PRIMED + PAIRS * (blk - 1))
                    pe.wait_ge(pT_cp, 2 * PAIRS * blk)
                    pe.wait_ge(ao_cp, 4 * PAIRS * blk)
                for c in range(NC):
                    mm = pe.matmul(ps[:, 7, 0:BLK], wkv[:, c, 0:DH], xnb[:, c, :], start=(c == 0), stop=(c == NC - 1))
                mm.then_inc(k_mm, 1)
                for pr in range(PAIRS):
                    for c in range(NC):
                        mm = pe.matmul(ps[:, 5, pr * DH:(pr + 1) * DH], xnb[:, c, pr * P:pr * P + P], wkv[:, c, DH:], start=(c == 0), stop=(c == NC - 1))
                mm.then_inc(v_mm, 1)
                q_heads(blk, 0, 6)
                pe.wait_ge(kraw_cp, blk + 1)
                pe.matmul(ps[:, 7, 0:BLK], rots[:, 0, :], kraw, start=True, stop=True).then_inc(rot_mm, 1)
                q_heads(blk, 6, 12)
                pe.wait_ge(kr_done, blk + 1)
                pe.matmul(ps[:, 7, BLK:2 * BLK], rots[:, 1, :], kr, start=True, stop=True).then_inc(rot2_mm, 1)
                q_heads(blk, 12, HEADS)
                pe.wait_ge(krr_cp, blk + 1)
                pe.wait_ge(q_ev, 2 * HEADS * (blk + 1))
                for pr in range(PAIRS):
                    if pr:
                        pe.wait_ge(masked, 2 * PAIRS * blk + 2 * pr)
                    for b2 in range(2):
                        b = 2 * pr + b2
                        for hp in range(HP):
                            o = ps[:, 2 + b2, hp * T:(hp + 1) * T]
                            pe.matmul(o, q_cos[:, b, hp * P:(hp + 1) * P], kr[:, b * T:(b + 1) * T], start=True, stop=False)
                            mm = pe.matmul(o, q_sin[:, b, hp * P:(hp + 1) * P], krr[:, b * T:(b + 1) * T], start=False, stop=True)
                        mm.then_inc(s_mm, 1)
                if not first:
                    out_proj(blk - 1)
                pe.wait_ge(v_cp, blk + 1)
                for pr in range(PAIRS):
                    pe.wait_ge(p_done, 2 * (PAIRS * blk + pr + 1))
                    for half in range(2):
                        n = 2 * pr + half
                        if n >= 2:
                            pe.wait_ge(pT_cp, 2 * PAIRS * blk + n - 1)
                        for hp in range(4 * half, 4 * half + 4):
                            mm = pe.transpose(ps[:, 4 - 4 * half, (hp % 4) * P:(hp % 4 + 1) * P], probs[:, pr, hp * P:(hp + 1) * P], identf)
                        mm.then_inc(pT_mm, 1)
                    pe.wait_ge(pT_cp, 2 * PAIRS * blk + 2 * pr + 2)
                    for half in range(2):
                        for b2 in range(2):
                            n = 4 * pr + 2 * half + b2
                            if n >= 3:
                                pe.wait_ge(ao_cp, 4 * PAIRS * blk + n - 2)
                            pe.matmul(ps[:, PV_BANKS[n % 3], :], vtok[64 * b2:64 * b2 + 64, pr, :], pT[64 * b2:64 * b2 + 64, half * 512:(half + 1) * 512],
                                      start=True, stop=True).then_inc(pv_mm, 1)
            pe.wait_ge(w_att, 48)
            attn_block(0, True)
            with pe.Fori(1, NBLK) as blk:
                attn_block(blk, False)
            out_proj(NBLK - 1)

            pe.wait_ge(ct_ld, 16 * 5)
            pe.wait_ge(idb_done, 1)
            with pe.Fori(0, IC) as i:
                for k in range(2):
                    n = 2 * i + k
                    pe.wait_ge(w_q8, n + 1)
                    if k:
                        pe.wait_ge(w_cp, 2 * n)
                    for c in range(NC):
                        mm = pe.transpose(ps[:, 0, 0:2 * P].bitcast(BF16)[:, c * P:(c + 1) * P], wq8[:, c * P:(c + 1) * P], id_b)
                    mm.then_inc(w_tr, 1)
                    pe.wait_ge(w_diag, n + 1)
                    pe.matmul(ps[:, 1, 0:P], ones_sb, diag, start=True, stop=True).then_inc(w_bc, 1)
                pe.wait_ge(w_cp, 4 * (i + 1))
            with pe.Fori(0, NC) as i:
                pe.wait_ge(w_q8, 2 * IC + i + 1)
                for c in range(IC):
                    mm = pe.transpose(ps[:, c // 8, :].bitcast(BF16)[:, (c % 8) * P:(c % 8 + 1) * P], wq8[:, c * P:(c + 1) * P], id_b)
                mm.then_inc(w_tr, 1)
                pe.wait_ge(w_diag, 2 * IC + i + 1)
                pe.matmul(ps[:, 2, 0:P], ones_sb, diag, start=True, stop=True).then_inc(w_bc, 1)
                pe.wait_ge(w_cp, 4 * IC + 2 * i + 2)

            with pe.Fori(0, 4 * T) as n:
                pe.wait_ge(rk_th, n + 1)
                for c in range(NC):
                    for j in range(NC):
                        mm = pe.matmul(ps[32 * j:32 * j + 32, 0, 0:P], thT[:, c, :], ct[:, c, j * P:(j + 1) * P],
                                       start=(c == 0), stop=(c == NC - 1), skip_group_check=True, tile_position=(0, 32 * j))
                mm.then_inc(rk_mm, 1)

            with pe.Fori(0, NTILE) as i:
                pe.wait_ge(f_q8, PRIMED + i + 1)
                for c in range(NC):
                    mm = pe.transpose(ps[:, 1, 0:2 * P].bitcast(BF16)[:, c * P:(c + 1) * P], qx8[:, c * P:(c + 1) * P], id_b)
                mm.then_inc(f_qT, 1)
                pe.wait_ge(f_qTcp, i + 1)
                for m in range(GU_T):
                    if m >= 2:
                        pe.wait_ge(f_scaled, 2 * (GU_T * i + m - 1))
                    for k, wt in enumerate((wgT, wuT)):
                        for c in range(NC):
                            mm = pe.matmul(ps[:, 2 + 2 * (m % 2) + k, 0:GU_N], qxT[:, c, :], wt[:, c, m * GU_N:(m + 1) * GU_N],
                                           start=(c == 0), stop=(c == NC - 1))
                    mm.then_inc(f_gu, 1)
                pe.wait_ge(f_t8, i + 1)
                for c in range(IC):
                    mm = pe.transpose(ps[:, 6 + c // 8, :].bitcast(BF16)[:, (c % 8) * P:(c % 8 + 1) * P], t8[:, c * P:(c + 1) * P], id_b)
                mm.then_inc(f_tT, 1)
                pe.wait_ge(f_tTcp, 2 * i + 2)
                for c in range(IC):
                    mm = pe.matmul(ps[:, 1, :], t8T[:, c, :], wdT[:, c, :], start=(c == 0), stop=(c == IC - 1))
                mm.then_inc(f_y, 1)
                pe.wait_ge(f_out, PRIMED + i + 1)

        @block.scalar
        def _(act):
            def gru_step(t, par):
                act.wait_ge(gates_mm, t + 1)
                act.activation(rz[par], ps[:, par, P:3 * P].rearrange("p (g n) -> p g n", g=2), ACT.Sigmoid).then_inc(rz_done, 1)
                act.wait_ge(npre_done, t + 1)
                act.activation(nval, npre, ACT.Tanh).then_inc(n_done, 1)
            with act.Fori(0, T // 2) as i:
                for par in range(2):
                    gru_step(2 * i + par, par)

            with act.Fori(0, NLN) as i:
                act.wait_ge(xc_done, i + 1)
                act.activation(sq, hsT[:, :, bass.ds(i * LN_TOK, LN_TOK)], ACT.Square).then_inc(sq_done, 1)
                act.wait_ge(ve_done, i + 1)
                act.activation(root, var, ACT.Sqrt).then_inc(root_done, 1)

            def attn_block(blk):
                act.wait_ge(k_mm, blk + 1)
                act.activation(kraw, ps[:, 7, 0:BLK], ACT.Copy).then_inc(kraw_cp, 1)
                act.wait_ge(v_mm, blk + 1)
                act.activation(vtok, ps[:, 5, 0:PAIRS * DH].rearrange("p (a n) -> p a n", a=PAIRS), ACT.Copy).then_inc(v_cp, 1)
                act.wait_ge(rot2_mm, blk + 1)
                act.activation(krr, ps[:, 7, BLK:2 * BLK], ACT.Copy).then_inc(krr_cp, 1)
                for n in range(2 * PAIRS):
                    act.wait_ge(shifted, 2 * PAIRS * blk + n + 1)
                    pb = probs[:, n // 2, :].rearrange("p (h b j) -> p h b j", h=HP, b=2)[:, :, n % 2, :]
                    act.activation(pb, pb, ACT.Exp).then_inc(exp_done, 1)
                for pr in range(PAIRS):
                    for half in range(2):
                        act.wait_ge(pT_mm, 2 * (PAIRS * blk + pr) + half + 1)
                        if pr and half == 0:
                            act.wait_ge(pv_mm, 4 * (PAIRS * blk + pr))
                        act.activation(pT[:, half * 512:(half + 1) * 512], ps[:, 4 - 4 * half, :], ACT.Copy).then_inc(pT_cp, 1)
                    for half in range(2):
                        for b2 in range(2):
                            act.wait_ge(pv_mm, 4 * (PAIRS * blk + pr) + 2 * half + b2 + 1)
                            tk = (2 * pr + b2) * T
                            act.activation(aoT[:, 8 * half:8 * half + 8, tk:tk + T],
                                           ps[:, PV_BANKS[(4 * pr + 2 * half + b2) % 3], :].rearrange("p (h t) -> p h t", h=8), ACT.Copy).then_inc(ao_cp, 1)
            with act.Fori(0, NBLK) as blk:
                attn_block(blk)

            act.wait_ge(c_ld, 16 * N_CONST)
            act.wait_ge(x1_wr, 16 * B)
            act.activation(id_b, identf, ACT.Copy).then_inc(idb_done, 1)
            with act.Fori(0, IC) as i:
                for k, (wt, row) in enumerate(((wgT, gs_row), (wuT, us_row))):
                    act.wait_ge(w_tr, PRIMED + 2 * i + k + 1)
                    act.activation(wt[:, :, bass.ds(i * P, P)], ps[:, 0, 0:2 * P].bitcast(BF16).rearrange("p (c n) -> p c n", c=NC),
                                   ACT.Copy).then_inc(w_cp, 1)
                    act.wait_ge(w_bc, PRIMED + 2 * i + k + 1)
                    act.activation(row[:, bass.ds(i * P, P)], ps[:, 1, 0:P], ACT.Copy).then_inc(w_cp, 1)
            with act.Fori(0, NC) as i:
                act.wait_ge(w_tr, PRIMED + 2 * IC + i + 1)
                act.activation(wdT[:, 0:8, bass.ds(i * P, P)], ps[:, 0, :].bitcast(BF16).rearrange("p (c n) -> p c n", c=8), ACT.Copy)
                act.activation(wdT[:, 8:IC, bass.ds(i * P, P)],
                               ps[:, 1, :].bitcast(BF16)[:, 0:(IC - 8) * P].rearrange("p (c n) -> p c n", c=IC - 8), ACT.Copy).then_inc(w_cp, 1)
                act.wait_ge(w_bc, PRIMED + 2 * IC + i + 1)
                act.activation(ds_row[:, bass.ds(i * P, P)], ps[:, 2, 0:P], ACT.Copy).then_inc(w_cp, 1)

            with act.Fori(0, T // 4) as i:
                for s in range(4):
                    for st in range(4):
                        n = 4 * (4 * i + s) + st
                        act.wait_ge(rk_qT, n + 1)
                        act.activation(thT, qsT, ACT.Tanh).then_inc(rk_th, 1)
                        src = qn[(s - 1) % 4] if st == 0 else qst[st - 1]
                        act.activation(cube, src, ACT.Square, scale=3.0 ** -0.5).then_inc(rk_sq, 1)

            with act.Fori(0, NTILE) as i:
                act.wait_ge(f_qT, i + 1)
                act.activation(qxT, ps[:, 1, 0:2 * P].bitcast(BF16).rearrange("p (c n) -> p c n", c=NC), ACT.Copy).then_inc(f_qTcp, 1)
                for m in range(GU_T):
                    act.wait_ge(f_scaled, 2 * (GU_T * i + m) + 1)
                    if m >= 2:
                        act.wait_ge(f_gated, GU_T * i + m - 1)
                    act.activation(sig[m % 2], gsc[m % 2], ACT.Sigmoid).then_inc(f_sig, 1)
                act.wait_ge(f_tT, i + 1)
                act.activation(t8T[:, 0:8, :], ps[:, 6, :].bitcast(BF16).rearrange("p (c n) -> p c n", c=8), ACT.Copy).then_inc(f_tTcp, 1)
                act.activation(t8T[:, 8:IC, :], ps[:, 7, :].bitcast(BF16)[:, 0:(IC - 8) * P].rearrange("p (c n) -> p c n", c=IC - 8),
                               ACT.Copy).then_inc(f_tTcp, 1)

        @block.vector
        def _(dve):
            def bcast(row, nb):
                return row.unsqueeze(1).to_broadcast([P, nb, T])

            dve.wait_ge(c_ld, 16 * N_CONST)
            b4, r4 = bg[0:NC, :], bres[0:NC, :]
            dve.tensor_copy(sel_b[0:NC, :], sel_f[0:NC, :]).then_inc(bias_split, 1)
            dve.tensor_tensor(b4[:, P:3 * P], b4[:, P:3 * P], r4[:, 0:2 * P], ALU.add).then_inc(bias_split, 1)
            dve.wait_ge(bias_split, 2)
            dve.tensor_copy(bparts[0][0:NC, :], b4).then_inc(bias_split, 1)
            dve.wait_ge(bias_split, 3)
            dve.tensor_tensor(r4, b4, bparts[0][0:NC, :], ALU.subtract).then_inc(bias_split, 1)
            dve.wait_ge(bias_split, 4)
            dve.tensor_copy(bparts[1][0:NC, :], r4).then_inc(bias_split, 1)
            dve.wait_ge(bias_split, 5)
            dve.tensor_tensor(bparts[2][0:NC, :], r4, bparts[1][0:NC, :], ALU.subtract).then_inc(bias_split, 1)

            dve.wait_ge(h0_ld, 32)
            with dve.Fori(0, T // 2) as i:
                for par in range(2):
                    t = 2 * i + par
                    r, z = rz[par][:, 0, :], rz[par][:, 1, :]
                    dve.wait_ge(rz_done, t + 1)
                    dve.tensor_tensor(rh, r, ps[:, par, 3 * P:4 * P], ALU.mult).then_inc(rh_done, 1)
                    dve.wait_ge(rh_done, t + 1)
                    dve.tensor_tensor(npre, rh, ps[:, par, 0:P], ALU.add).then_inc(npre_done, 1)
                    dve.tensor_tensor(zh, z, h_q[1 - par], ALU.mult).then_inc(zh_done, 1)
                    dve.tensor_scalar(omz, z, -1.0, 1.0, ALU.mult, ALU.add).then_inc(omz_done, 1)
                    dve.wait_ge(n_done, t + 1)
                    dve.wait_ge(omz_done, t + 1)
                    dve.tensor_tensor(nz, omz, nval, ALU.mult).then_inc(nz_done, 1)
                    dve.wait_ge(zh_done, t + 1)
                    dve.wait_ge(nz_done, t + 1)
                    dve.tensor_tensor(h_q[par], nz, zh, ALU.add).then_inc(h_done, 1)
                    dve.wait_ge(h_done, t + 1)
                    dve.wait_ge(hs_cp, PRIMED + t)
                    dve.transpose(hT[par].rearrange("p c b -> p (c b)"), h_q[par]).then_inc(hT_done, 1)

            with dve.Fori(0, NLN) as i:
                v = Steps(dve, ln_v, 5 * i)
                dve.wait_ge(mean_mm, i + 1)
                for c in range(NC):
                    one = hsT[:, c, bass.ds(i * LN_TOK, LN_TOK)]
                    mm = dve.tensor_tensor(one, one, ps[:, 0, :], ALU.subtract)
                mm.then_inc(xc_done, 1)
                dve.wait_ge(var_mm, i + 1)
                dve.tensor_scalar(var, ps[:, 1, :], LN_EPS, None, ALU.add).then_inc(ve_done, 1)
                dve.wait_ge(root_done, i + 1)
                v.need(v.did(dve.reciprocal(newt, root)))
                v.need(v.did(dve.tensor_tensor(root, newt, newt, ALU.mult)))
                v.need(v.did(dve.tensor_tensor(root, root, var, ALU.mult)))
                v.need(v.did(dve.tensor_scalar(root, root, -0.5, 1.5, ALU.mult, ALU.add)))
                v.did(dve.tensor_tensor(rstd[:, bass.ds(i * LN_TOK, LN_TOK)], newt, root, ALU.mult))
                assert v.n == 5

            def norm(blk):
                for c in range(NC):
                    mm = dve.scalar_tensor_tensor(out=xnb[:, c, :], in0=hsT[:, c, bass.ds(blk * BLK, BLK)], scalar=gam[:, c:c + 1],
                                                  in1=rstd[:, bass.ds(blk * BLK, BLK)], op0=ALU.mult, op1=ALU.mult)
                mm.then_inc(xn_done, 1)

            def by_time(a):
                return a.rearrange("p (b t) -> p b t", t=T)

            def q_out(blk, h0, h1):
                for h in range(h0, h1):
                    dve.wait_ge(q_mm, HEADS * blk + h + 1)
                    for dst, tr in ((q_cos, 0), (q_sin, 1)):
                        dve.tensor_tensor(dst[:, :, h * T:(h + 1) * T], by_time(ps[:, h % 2, 0:BLK]), bcast(trigs[:, tr, :], BLK_B),
                                          ALU.mult).then_inc(q_ev, 1)

            def softmax(blk, pr):
                def of(n):
                    return probs[:, pr, :].rearrange("p (h b j) -> p h b j", h=HP, b=2)[:, :, n % 2, :]

                def row(a, n):
                    return a[:, n, :].unsqueeze(2).to_broadcast([P, HP, T])

                def at(n):
                    return 2 * PAIRS * blk + n + 1
                two = (2 * pr, 2 * pr + 1)
                for n in two:
                    dve.wait_ge(s_mm, at(n))
                    dve.tensor_tensor(of(n), ps[:, 2 + n % 2, :].rearrange("p (h j) -> p h j", h=HP), bcast(masks, HP),
                                      ALU.add).then_inc(masked, 1)
                for n in two:
                    dve.wait_ge(masked, at(n))
                    dve.tensor_reduce(smax[:, n, :], of(n), AX.X, ALU.max).then_inc(max_done, 1)
                for n in two:
                    dve.wait_ge(max_done, at(n))
                    dve.tensor_tensor(of(n), of(n), row(smax, n), ALU.subtract).then_inc(shifted, 1)
                for n in two:
                    dve.wait_ge(exp_done, at(n))
                    dve.tensor_reduce(ssum[:, n, :], of(n), AX.X, ALU.add).then_inc(sum_done, 1)
                for n in two:
                    dve.wait_ge(sum_done, at(n))
                    dve.reciprocal(ssum[:, n, :], ssum[:, n, :]).then_inc(inv_done, 1)
                for n in two:
                    dve.wait_ge(inv_done, at(n))
                    dve.tensor_tensor(of(n), of(n), row(ssum, n), ALU.mult).then_inc(p_done, 1)

            def residual(blk):
                for pr in range(PAIRS):
                    dve.wait_ge(wo_mm, PAIRS * blk + pr + 1)
                    dve.wait_ge(x_ld, 16 * PAIRS * (blk + 1))
                    dve.tensor_tensor(xres[:, pr, :], ps[:, 6 + pr, :], xres[:, pr, :], ALU.add).then_inc(x1_done, 1)

            def attn_block(blk, first, last):
                dve.wait_ge(kraw_cp, blk + 1)
                dve.tensor_tensor(by_time(kc), by_time(kraw), bcast(trigs[:, 2, :], BLK_B), ALU.mult).then_inc(kc_done, 1)
                q_out(blk, 0, 6)
                dve.wait_ge(rot_mm, blk + 1)
                dve.tensor_tensor(by_time(kr), by_time(ps[:, 7, 0:BLK]), bcast(trigs[:, 3, :], BLK_B), ALU.mult).then_inc(ks_done, 1)
                dve.wait_ge(kc_done, blk + 1)
                dve.wait_ge(ks_done, blk + 1)
                dve.tensor_tensor(kr, kr, kc, ALU.add).then_inc(kr_done, 1)
                q_out(blk, 6, HEADS)
                for pr in range(PAIRS):
                    softmax(blk, pr)
                if not last:
                    norm(blk + 1)
                if not first:
                    residual(blk - 1)
            dve.wait_ge(st_ld, 16)
            dve.wait_ge(ln_v, 5 * NLN)
            norm(0)
            attn_block(0, True, False)
            with dve.Fori(1, NBLK - 1) as blk:
                attn_block(blk, False, False)
            attn_block(NBLK - 1, False, True)
            residual(NBLK - 1)

            def scale_of(v, src, a, s, r):
                v.need(v.did(dve.tensor_reduce(a, src, AX.X, ALU.max, apply_absolute_value=True)))
                v.need(v.did(dve.tensor_scalar(s, a, 1.0 / FP8_MAX, None, ALU.mult)))
                v.need(v.did(dve.reciprocal(r, s)))

            def rounded(v, x_, e, w_, dst):
                v.need(v.did(dve.tensor_scalar(e.bitcast(U32), x_.bitcast(U32), EXP_BITS, None, ALU.bitwise_and)))
                v.need(v.did(dve.tensor_scalar(e, e, FP8_TINY, ROUND_AT, ALU.max, ALU.mult)))
                v.need(v.did(dve.tensor_tensor(w_, x_, e, ALU.add)))
                return dve.tensor_tensor(dst, w_, e, ALU.subtract)

            W_STEPS = 6
            dve.wait_ge(x1_wr, 16 * B)
            dve.wait_ge(ct_ld, 16 * 5)

            def weight_rows(src, n, width):
                v = Steps(dve, w_v, W_STEPS * n)
                scale_of(v, src, am[:, 0:1], sx[:, 0:1], rs[:, 0:1])
                dve.tensor_scalar(wv[:, 0:width], src, rs[:, 0:1], None, ALU.mult).then_inc(w_scaled, 1)
                dve.wait_ge(w_scaled, PRIMED + n + 1)
                dve.wait_ge(w_bc, PRIMED + n)
                dve.wait_ge(w_tr, PRIMED + n)
                dve.tensor_scalar(diag, identf, sx[:, 0:1], None, ALU.mult).then_inc(w_diag, 1)
                rounded(v, wv[:, 0:width], wexp[:, 0:width], wround[:, 0:width], wq8[:, 0:width]).then_inc(w_q8, 1)
                assert v.n == W_STEPS

            with dve.Fori(0, IC) as i:
                dve.wait_ge(wraw_ld, 32 * (i + 1))
                for k in range(2):
                    weight_rows(wraw[:, k, :], 2 * i + k, D)
            with dve.Fori(0, NC) as i:
                dve.wait_ge(wd_ld, 16 * (i + 1))
                weight_rows(wdraw, 2 * IC + i, INNER)

            def drives(v, s):
                v.need(v.did(dve.tensor_tensor(dsum, drive[s], biasq, ALU.add)))
                return v.did(dve.tensor_scalar(d6, dsum, DT / 6, None, ALU.mult))

            def turn(v, src):
                dve.transpose(qsT.rearrange("p c b -> p (c b)"), src).then_inc(rk_qT, 1)

            def stage(v, t, s, st, next_drive):
                n = 4 * t + st
                q, p = qn[(s - 1) % 4], pn[(s - 1) % 2]
                qs = q if st == 0 else qst[st - 1]
                pp = p if st == 0 else pst[st - 1]
                a = (DT / 2, DT / 2, DT, DT / 6)[st]
                stt = dve.scalar_tensor_tensor
                u = v.did(stt(out=ubuf, in0=pp, scalar=-BETA, in1=qs, op0=ALU.mult, op1=ALU.add))
                if st == 0:
                    u = v.did(dve.tensor_scalar(pcA, p, DT / 2 * EPS * ALPHA, None, ALU.add))
                    v.did(stt(out=hA, in0=dsum, scalar=DT / 2, in1=q, op0=ALU.mult, op1=ALU.add))
                if st == 1:
                    v.did(dve.tensor_scalar(np_, p, -1.0 / 3, DT / 6 * EPS * ALPHA, ALU.mult, ALU.add))
                    v.did(stt(out=nq, in0=q, scalar=-1.0 / 3, in1=d6, op0=ALU.mult, op1=ALU.add))
                    v.did(stt(out=hA2, in0=dsum, scalar=DT, in1=q, op0=ALU.mult, op1=ALU.add))
                    k = v.did(dve.tensor_scalar(pcA2, p, DT * EPS * ALPHA, None, ALU.add))
                dve.wait_ge(rk_sq, n + 1)
                e = v.did(stt(out=ebuf, in0=cube, scalar=1.0, in1=qs, op0=ALU.subtract, op1=ALU.mult))
                if st < 3:
                    v.need(u)
                    v.did(stt(out=pst[st], in0=ubuf, scalar=a * EPS, in1=(pcA, pcA, pcA2)[st], op0=ALU.mult, op1=ALU.add))
                if st == 1:
                    v.need(k)
                if st >= 1:
                    w3 = (0, 1.0 / 3, 2.0 / 3, 1.0 / 3)[st]
                    psum = v.did(stt(out=(p1, p2, p3)[st - 1], in0=pp, scalar=w3, in1=(np_, p1, p2)[st - 1], op0=ALU.mult, op1=ALU.add))
                v.need(e)
                e2 = v.did(dve.tensor_tensor(gbuf, ebuf, pp, ALU.add))
                if st >= 1:
                    qsum = v.did(stt(out=(a1, a2, a3)[st - 1], in0=qs, scalar=w3, in1=(nq, a1, a2)[st - 1], op0=ALU.mult, op1=ALU.add))
                if st == 3:
                    v.need(qsum)
                    v.did(stt(out=p4, in0=ubuf, scalar=DT / 6 * EPS, in1=p3, op0=ALU.mult, op1=ALU.add))
                v.need(e2)
                last = v.did(stt(out=xfin, in0=gbuf, scalar=-a, in1=(hA, hA, hA2, a3)[st], op0=ALU.mult, op1=ALU.add))
                if st == 3:
                    v.need(last)
                    v.did(dve.tensor_scalar(pn[s % 2], p4, CLAMP, -CLAMP, ALU.min, ALU.max))
                    next_drive(v)
                else:
                    v.need(last)
                dve.wait_ge(rk_mm, n + 1)
                if st < 3:
                    v.need(v.did(stt(out=qst[st], in0=ps[:, 0, 0:P], scalar=a, in1=xfin, op0=ALU.mult, op1=ALU.add)))
                    turn(v, qst[st])
                else:
                    v.need(v.did(stt(out=qpre, in0=ps[:, 0, 0:P], scalar=a, in1=xfin, op0=ALU.mult, op1=ALU.add)))

            def step(v, i, s, next_drive, last):
                t = 4 * i + s
                for st in range(4):
                    stage(v, t, s, st, next_drive)
                dve.wait_ge(q_wr[s], PRIMED + 16 * i)
                dve.tensor_scalar(qn[s], qpre, CLAMP, -CLAMP, ALU.min, ALU.max).then_inc(rk_q, 1)
                dve.wait_ge(rk_q, t + 1)
                if not last:
                    turn(v, qn[s])

            v = Steps(dve, rk_v, 0)
            dve.wait_ge(drive_ld[0], 16)
            v.need(drives(v, 0))
            turn(v, qn[3])

            def group(i, v, last):
                for s in range(4):
                    def next_drive(v, s=s):
                        if last and s == 3:
                            return
                        dve.wait_ge(drive_ld[(s + 1) % 4], 16 * (i + 1 + (s == 3)))
                        v.need(drives(v, (s + 1) % 4))
                    step(v, i, s, next_drive, last and s == 3)
            RK_STEPS = 4 * 39
            with dve.Fori(0, T // 4 - 1) as i:
                v = Steps(dve, rk_v, 2 + RK_STEPS * i)
                group(i, v, False)
                assert v.n == RK_STEPS, v.n
            v = Steps(dve, rk_v, 2 + RK_STEPS * (T // 4 - 1))
            group(T // 4 - 1, v, True)

            F_STEPS = 6 + 1 + 6 + 1 + GU_T + 1
            with dve.Fori(0, NTILE) as i:
                v = Steps(dve, f_v, F_STEPS * i)
                dve.wait_ge(q_ld, 16 * TILE_T * (i + 1))
                scale_of(v, qt, xam, xsx, xrs)
                wx, wr_ = wv[:, 0:D], wround[:, 0:D]
                v.need(v.did(dve.tensor_scalar(wx, qt, xrs, None, ALU.mult)))
                rounded(v, wx, wexp[:, 0:D], wr_, qx8).then_inc(f_q8, 1)
                for m in range(GU_T):
                    b = m % 2
                    dve.wait_ge(f_gu, GU_T * i + m + 1)
                    for k, (dst, row) in enumerate(((gsc[b], gs_row), (usc[b], us_row))):
                        dve.scalar_tensor_tensor(out=dst, in0=ps[:, 2 + 2 * b + k, 0:GU_N], scalar=xsx, in1=row[:, m * GU_N:(m + 1) * GU_N],
                                                 op0=ALU.mult, op1=ALU.mult).then_inc(f_scaled, 1)
                    dve.wait_ge(f_scaled, 2 * (GU_T * i + m + 1))
                    v.need(v.did(dve.tensor_tensor(usc[b], gsc[b], usc[b], ALU.mult)))
                    dve.wait_ge(f_sig, GU_T * i + m + 1)
                    dve.tensor_tensor(tt[:, m * GU_N:(m + 1) * GU_N], sig[b], usc[b], ALU.mult).then_inc(f_gated, 1)
                dve.wait_ge(f_gated, GU_T * (i + 1))
                scale_of(v, tt, tam, tsx, trs)
                v.need(v.did(dve.tensor_scalar(wv, tt, trs, None, ALU.mult)))
                rounded(v, wv, wexp, wround, t8).then_inc(f_t8, 1)
                dve.wait_ge(f_y, i + 1)
                v.need(v.did(dve.scalar_tensor_tensor(out=ysc, in0=ps[:, 1, :], scalar=tsx, in1=ds_row, op0=ALU.mult, op1=ALU.mult)))
                dve.wait_ge(x1_ld, 16 * TILE_T * (i + 1))
                dve.wait_ge(o_wr, PRIMED + 16 * TILE_T * i)
                dve.tensor_tensor(yout, ysc, x1t, ALU.add).then_inc(f_out, 1)
                assert v.n == F_STEPS, v.n


def kernel(**inputs):
    import numpy as np
    import concourse.bacc as bacc
    from concourse.bass_utils import run_bass_kernel_spmd

    a = {k: np.asarray(v) for k, v in inputs.items()}

    def by_block(w_):
        return w_.reshape(NC, NC, 32, -1).transpose(0, 2, 1, 3).reshape(P, -1)

    def quad(m):
        return m.reshape(B, NC, P).transpose(1, 0, 2).reshape(P, P)

    wih = a["L0_cond_W_ih"].reshape(D, GATES, D)[:, [2, 0, 1]].reshape(D, -1)
    b_ih, b_hh = a["L0_cond_b_ih"], a["L0_cond_b_hh"]
    x_ = a["x"]
    trig, mask, rot, sel, ones = constants(np)
    arrays = {
        "xT": x_.reshape(B, T, NC, P).transpose(1, 3, 2, 0).reshape(T, P, NC * B),
        "x": x_.reshape(TOK, D),
        "cond_quad": quad(a["cond_2048"]),
        "cond_T": by_block(a["cond_2048"].T),
        "W_ih": wih.reshape(NC, P, -1).transpose(1, 0, 2).reshape(P, -1),
        "W_hh": by_block(a["L0_cond_W_hh"]),
        "bias_ih": b_ih.reshape(GATES, NC, P), "bias_hh": b_hh.reshape(GATES, NC, P),
        "sel": sel,
        "gamma": by_block(a["L0_attn_gamma"][:, None]),
        "Wq": by_block(a["L0_attn_Wq"]), "Wkv": by_block(a["L0_attn_Wkv"]),
        "Wo": a["L0_attn_Wo"].reshape(HEADS, DH, D).transpose(1, 0, 2).reshape(P, -1),
        "couplingT": by_block(a["L0_cond2_coupling"].T),
        "bias_quad": quad(np.broadcast_to(a["L0_cond2_bias"], (B, D))),
        "w_gate": a["L0_ffn_w_gate"], "w_up": a["L0_ffn_w_up"], "w_down": a["L0_ffn_w_down"],
        "down_idx": a["L0_ffn_down_reorder_index"].reshape(INNER, 1),
        "ident": np.eye(P, dtype=np.float32), "ones": ones, "rot": rot, "trig": trig, "mask": mask,
    }
    nc = bacc.Bacc("TRN2", target_bir_lowering=False, num_devices=1)
    arrays = {f"in_{k}": np.ascontiguousarray(v) for k, v in arrays.items()}
    aps = {k[3:]: nc.dram_tensor(k, v.shape, mybir.dt.from_np(v.dtype), kind="ExternalInput").ap() for k, v in arrays.items()}
    x1_scr = nc.dram_tensor("x1_scr", (T, NC, B, P), F32, kind="Internal").ap()
    q_scr = nc.dram_tensor("q_scr", (T, NC, B, P), F32, kind="Internal").ap()
    out = nc.dram_tensor("out_0", (B, T, D), F32, kind="ExternalOutput").ap()
    gru_attn_rk4_ffn(nc, **aps, x1_scr=x1_scr, q_scr=q_scr, out=out)
    r = run_bass_kernel_spmd(nc, [arrays], core_ids=[0])
    return r.results[0]["out_0"]


def constants(np):
    inv = 1.0 / 10000.0 ** (np.arange(0, DH, 2, dtype=np.float32) / np.float32(DH))
    fr = (np.arange(T, dtype=np.float32)[None, :] * inv.astype(np.float32)[:, None]).astype(np.float32)
    fr = np.concatenate([fr, fr])
    cos, sin = np.cos(fr.astype(np.float64)), np.sin(fr.astype(np.float64))
    sc = float(DH) ** -0.5
    trig = np.stack([cos * sc, sin * sc, cos, sin]).astype(np.float32)
    i, j = np.arange(P)[:, None] % T, np.arange(T)[None, :]
    mask = np.where(j > i, -np.finfo(np.float32).max, 0).astype(np.float32)
    half = DH // 2
    m = np.zeros((DH, DH), np.float32)
    m[np.arange(half), np.arange(half) + half] = -1
    m[np.arange(half) + half, np.arange(half)] = 1
    rot = np.stack([m.T, m])
    sel = np.repeat(np.eye(NC, dtype=np.float32), B, axis=1)
    ones = np.stack([np.full((P, P), 1.0 / D, np.float32), np.ones((P, P), np.float32)])
    return trig, mask, rot, sel, ones
```

```python
from contextlib import ExitStack

import concourse.bass as bass
from concourse import mybir

ALU = mybir.AluOpType
ACT = mybir.ActivationFunctionType
AX = mybir.AxisListType
F32 = mybir.dt.float32
BF16 = mybir.dt.bfloat16
U32 = mybir.dt.uint32
I32 = mybir.dt.int32

P = 128
B, T, D = 32, 64, 512
NC = D // P
GATES = 3
HEADS, DH = 16, 128
HP = HEADS // 2
TOK = B * T
BLK_B = 4
BLK = BLK_B * T
NBLK = B // BLK_B
PAIRS = BLK_B // 2
LN_TOK = 512
NLN = TOK // LN_TOK
INNER = 1408
IC = INNER // P
GU_N = 352
GU_T = INNER // GU_N
TILE_T = P // B
NTILE = T // TILE_T
PV_BANKS = (5, 2, 3)
LN_EPS = 1e-5
DT, EPS, ALPHA, BETA, CLAMP = 0.01, 0.08, 0.7, 0.8, 20.0
FP8_MAX = 448.0
FP8_TINY = 2.0 ** -6
ROUND_AT = 1.5 * 2.0 ** 20
EXP_BITS = 0x7F800000
WORDS = 48 * 1024 - 256


def rk4_weights():
    p, q, q2, q3, q4 = ([float(i == k) for i in range(5)] for k in range(5))

    def add(*terms):
        return [sum(c * v[k] for c, v in terms) for k in range(5)]
    a1, a2 = DT / 2 * EPS, DT * EPS
    ps2 = add((1, p), (a1, q), (-a1 * BETA, p))
    ps3 = add((1, p), (a1, q2), (-a1 * BETA, ps2))
    ps4 = add((1, p), (a2, q3), (-a2 * BETA, ps3))
    c = DT / 6 * EPS
    p_next = add((1, p), (c, q), (2 * c, q2), (2 * c, q3), (c, q4), (-c * BETA, p), (-2 * c * BETA, ps2), (-2 * c * BETA, ps3),
                 (-c * BETA, ps4))
    e1 = add((-1, p))
    s = 2 / DT
    minus = [add((-1, v), (-1, e1)) for v in (p, ps2, ps3)]
    minus.append(add((-1, ps4), (-1, e1), (-s, q), (s, q2), (2 * s, q3), (s, q4)))
    return minus, p_next


_MINUS, P_NEXT = rk4_weights()
MIX, STAGE_MIX = [1.0], []
for _row in _MINUS:
    _used = []
    for _k, _w in enumerate(_row):
        if _w != 0.0:
            _used.append((_k, len(MIX)))
            MIX.append(_w)
    STAGE_MIX.append(_used)

PREP_GU = (1, 1 + IC)
PREP_D = (PREP_GU[1], PREP_GU[1] + NC)
LEAD = 3
GROUP_STEPS = 93


def not_before(a, b):
    return not isinstance(a, int) or a >= b


def wait_if(eng, sem, value):
    if not isinstance(value, int) or value > 0:
        eng.wait_ge(sem, value)


def in_groups(eng, group):
    def tiles(g):
        def tile(a):
            i = g - 1 - a
            return i if not isinstance(g, int) or 0 <= i < NTILE else None
        return tile
    for g in range(LEAD):
        group(g, True, tiles(g))
    with eng.Fori(LEAD, NTILE - 1) as g:
        group(g, True, tiles(g))
    for g in range(NTILE - 1, NTILE + LEAD):
        group(g, g < NTILE, tiles(g))


class Steps:

    def __init__(self, eng, sem, base):
        self.eng, self.sem, self.base, self.n = eng, sem, base, 0

    def did(self, ins):
        ins.then_inc(self.sem, 1)
        self.n += 1
        return self.n

    def need(self, n):
        self.eng.wait_ge(self.sem, self.base + n)


class Words:

    def __init__(self, at, end):
        self.at, self.end = at, end

    def take(self, n):
        a = self.at
        self.at += n
        assert self.at <= self.end, (self.at, self.end)
        return a


def gru_attn_rk4_ffn(nc, xT, x, cond_quad, cond_T, W_ih, W_hh, bias_ih, bias_hh, sel, gamma, Wq, Wkv, Wo,
                     couplingT, bias_quad, w_gate, w_up, w_down, down_idx, ident, ones, rot, trig, mask,
                     x1_scr, q_scr, wgu_scr, wd_scr, scale_scr, out):
    with ExitStack() as ctx:
        mem = ctx.enter_context(nc.sbuf_tensor("mem", [P, WORDS], F32))
        ps = ctx.enter_context(nc.psum_tensor("ps", [P, 8, 512], F32))

        def sem(name):
            return ctx.enter_context(nc.semaphore(name))

        def f32(a, *dims):
            n = 1
            for d in dims:
                n *= d
            v = mem[:, a:a + n]
            if len(dims) == 2:
                v = v.rearrange("p (a b) -> p a b", a=dims[0])
            if len(dims) == 3:
                v = v.rearrange("p (a b c) -> p a b c", a=dims[0], b=dims[1])
            return v

        def bf16(a, *dims):
            n = 1
            for d in dims:
                n *= d
            v = mem[:, a:a + n // 2].bitcast(BF16)
            if len(dims) == 2:
                v = v.rearrange("p (a b) -> p a b", a=dims[0])
            return v

        w = Words(0, WORDS)
        a_hs = w.take(NC * TOK)
        hsT = f32(a_hs, NC, TOK)
        a_ih = w.take(NC * GATES * D)
        a_hh = w.take(NC * GATES * D)
        wih = f32(a_ih, NC, GATES * D)
        whh = f32(a_hh, NC, GATES * D)
        wq = f32(w.take(NC * HEADS * DH), NC, HEADS * DH)
        a_wo = w.take(HEADS * D)
        wo = f32(a_wo, HEADS, D)
        wkv = f32(w.take(NC * 2 * DH), NC, 2 * DH)
        a_p2 = w.at
        q_cos = f32(a_ih, BLK_B, HEADS * T)
        q_sin = f32(a_ih + HEADS * BLK, BLK_B, HEADS * T)
        aoT = f32(a_ih + 2 * HEADS * BLK, HEADS, BLK)
        rstd = f32(w.take(TOK), TOK)
        xnb = f32(w.take(NC * BLK), NC, BLK)
        probs = f32(w.take(PAIRS * HP * P), PAIRS, HP * P)
        pT = f32(w.take(HP * P), HP * P)
        xres = f32(w.take(PAIRS * D), PAIRS, D)
        a_k = w.take(3 * BLK)
        kc, kraw, kr, krr = f32(a_k, BLK), f32(a_k + BLK, BLK), f32(a_k + 2 * BLK, BLK), f32(w.take(BLK), BLK)
        vtok = f32(w.take(PAIRS * DH), PAIRS, DH)
        smax = f32(w.take(PAIRS * 2 * HP), PAIRS * 2, HP)
        ssum = f32(w.take(PAIRS * 2 * HP), PAIRS * 2, HP)
        gam = f32(w.take(NC), NC)
        row_scales = f32(w.take(2 * IC + NC), 2 * IC + NC)
        a_const = w.take(P + P + 2 * P + 4 * T + T)
        identf = f32(a_const, P)
        mean_w = f32(a_const + P, P)
        rots = f32(a_const + 2 * P, 2, P)
        trigs = f32(a_const + 4 * P, 4, T)
        masks = f32(a_const + 4 * P + 4 * T, T)
        g = Words(a_p2, a_const - 64)
        xt = [f32(g.take(NC * B), NC, B) for _ in range(2)]
        hT = [f32(g.take(NC * B), NC, B) for _ in range(2)]
        h_q = [f32(g.take(P), P) for _ in range(2)]
        rz = [f32(g.take(2 * P), 2, P) for _ in range(2)]
        rh, npre, nval, zh, omz, nz = (f32(g.take(P), P) for _ in range(6))
        a_bg = g.take(512 + 256 + 256 + 256 + 512 + 256 + 256 + 64)
        bg = f32(a_bg, 512)
        bres = f32(a_bg + 512 + 256 + 256 + 256, 512)
        bparts = [bf16(a_bg + 512 + 256 * i, 512) for i in range(3)]
        sel_f = f32(a_bg + 512 + 3 * 256 + 512, P)
        sel_b = bf16(a_bg + 512 + 3 * 256 + 512 + P, P)
        id_b1 = bf16(a_bg + 512 + 3 * 256 + 512 + 2 * P + 256, P)
        bstack = bf16(a_bg + 512 + 3 * 256 + 512 + 2 * P, 512)
        g = Words(a_wo, a_wo + HEADS * D)
        wraw = f32(g.take(2 * D), 2, D)
        wdraw = f32(g.take(INNER), INNER)
        wv = f32(g.take(INNER), INNER)
        wexp = f32(g.take(INNER), INNER)
        wq8 = bf16(g.take(INNER // 2), INNER)
        wst = bf16(g.take(INNER // 2), IC, P)
        idx = f32(g.take(1), 1)
        am, wsc, rs = (f32(g.take(1), 1) for _ in range(3))
        sq = f32(a_ih, NC, LN_TOK)
        var = f32(a_ih + NC * LN_TOK, LN_TOK)
        root = f32(a_ih + NC * LN_TOK + LN_TOK, LN_TOK)
        newt = f32(a_ih + NC * LN_TOK + 2 * LN_TOK, LN_TOK)

        w = Words(0, a_const - 64)
        ct = f32(w.take(NC * D), NC, D)
        wgT = bf16(w.take(NC * INNER // 2), NC, INNER)
        wuT = bf16(w.take(NC * INNER // 2), NC, INNER)
        wdT = bf16(w.take(IC * D // 2), IC, D)
        gs_row, us_row, ds_row = f32(w.take(INNER), INNER), f32(w.take(INNER), INNER), f32(w.take(D), D)
        id_b = bf16(w.take(P // 2), P)
        biasq = f32(w.take(P), P)
        mix = [f32(w.take(P), P) for _ in range(len(MIX))]
        drive = [f32(w.take(P), P) for _ in range(4)]
        qn = [f32(w.take(P), P) for _ in range(4)]
        pn = [f32(w.take(P), P) for _ in range(2)]
        emp = [f32(w.take(P), P) for _ in range(2)]
        qst = [f32(w.take(P), P) for _ in range(3)]
        qsT = f32(w.take(P), NC, B)
        thT = f32(w.take(P), NC, B)
        cube, ebuf, gbuf, dsum, qpre, w1, w2, w3, w4, w5 = (f32(w.take(P), P) for _ in range(10))
        qt = f32(w.take(D), D)
        x1t = f32(w.take(D), D)
        vq, eq = f32(w.take(D), D), f32(w.take(D), D)
        qx8 = bf16(w.take(D // 2), D)
        qxT = bf16(w.take(D // 2), NC, P)
        gsc = [f32(w.take(GU_N), GU_N) for _ in range(2)]
        usc = [f32(w.take(GU_N), GU_N) for _ in range(2)]
        sig = [f32(w.take(GU_N), GU_N) for _ in range(2)]
        tt = f32(w.take(INNER), INNER)
        vt, et = f32(w.take(INNER), INNER), f32(w.take(INNER), INNER)
        t8 = bf16(w.take(INNER // 2), INNER)
        t8T = bf16(w.take(INNER // 2), IC, P)
        ysc = f32(w.take(D), D)
        yout = f32(w.take(D), D)
        tam, tsx, trs, xam, xsx, xrs = (f32(w.take(1), 1) for _ in range(6))

        (w_gru, w_att, c_ld, xt_ld0, xt_ld1, h0_ld, st_ld, wraw_ld, idx_ld, wd_ld, x_ld, x1_wr, q_ld, x1_ld,
         o_wr, ct_ld) = (sem(n) for n in (
             "w_gru", "w_att", "c_ld", "xt_ld0", "xt_ld1", "h0_ld", "st_ld", "wraw_ld", "idx_ld", "wd_ld", "x_ld",
             "x1_wr", "q_ld", "x1_ld", "o_wr", "ct_ld"))
        xt_ld = [xt_ld0, xt_ld1]
        q_wr = [sem(f"q_wr{i}") for i in range(4)]
        drive_ld = [sem(f"drive_ld{i}") for i in range(4)]
        bias_split, gx_mm, gates_mm, rz_done, rh_done, npre_done, n_done, zh_done, omz_done, nz_done, h_done, hT_done, hs_cp = (
            sem(n) for n in ("bias_split", "gx_mm", "gates_mm", "rz_done", "rh_done", "npre_done", "n_done",
                             "zh_done", "omz_done", "nz_done", "h_done", "hT_done", "hs_cp"))
        mean_mm, xc_done, sq_done, var_mm, ve_done, root_done, ln_v = (
            sem(n) for n in ("mean_mm", "xc_done", "sq_done", "var_mm", "ve_done", "root_done", "ln_v"))
        (xn_done, k_mm, v_mm, q_mm, rot_mm, rot2_mm, kraw_cp, kc_done, ks_done, kr_done, krr_cp, v_cp, q_ev, s_mm,
         masked, max_done, shifted, exp_done, sum_done, inv_done, p_done, pT_mm, pT_cp, pv_mm, ao_cp, wo_mm,
         x1_done) = (sem(n) for n in (
             "xn_done", "k_mm", "v_mm", "q_mm", "rot_mm", "rot2_mm", "kraw_cp", "kc_done", "ks_done", "kr_done",
             "krr_cp", "v_cp", "q_ev", "s_mm", "masked", "max_done", "shifted", "exp_done", "sum_done", "inv_done",
             "p_done", "pT_mm", "pT_cp", "pv_mm", "ao_cp", "wo_mm", "x1_done"))
        w_v, w_rs, w_scaled, w_q8, w_tr, w_cp, wgu_wr, wd_wr, w_kept, idb_done, gather_go, stack_ld, ws_wr, ffn_ld = (
            sem(n) for n in ("w_v", "w_rs", "w_scaled", "w_q8", "w_tr", "w_cp", "wgu_wr", "wd_wr", "w_kept", "idb_done",
                             "gather_go", "stack_ld", "ws_wr", "ffn_ld"))
        rk_start = sem("rk_start")
        (rk_v, rk_mix, rk_qT, rk_th, rk_mm, rk_sq, rk_e, rk_q) = (
            sem(n) for n in ("rk_v", "rk_mix", "rk_qT", "rk_th", "rk_mm", "rk_sq", "rk_e", "rk_q"))
        (f_rq, f_vq, f_q8, f_qT, f_qTcp, f_g, f_u, f_gsc, f_usc, f_sig, f_gated, f_rt, f_vt, f_t8, f_tT, f_tTcp, f_y,
         f_out) = (sem(n) for n in (
             "f_rq", "f_vq", "f_q8", "f_qT", "f_qTcp", "f_g", "f_u", "f_gsc", "f_usc", "f_sig", "f_gated", "f_rt",
             "f_vt", "f_t8", "f_tT", "f_tTcp", "f_y", "f_out"))

        PRIMED = 1
        block = ctx.enter_context(nc.Block())
        N_CONST = 10

        @block.sync
        def _(sp):
            sp.dma_start(wih, W_ih.rearrange("p (c n) -> p c n", c=NC)).then_inc(w_gru, 16)
            gate_of = lambda a, lo, hi: a[lo:hi].rearrange("g j n -> j g n")
            sp.dma_start(bg[0:NC, 0:P], bias_ih[2]).then_inc(c_ld, 16)
            sp.dma_start(bg[0:NC, P:3 * P].rearrange("j (g n) -> j g n", g=2), gate_of(bias_ih, 0, 2)).then_inc(c_ld, 16)
            sp.dma_start(bg[0:NC, 3 * P:], bias_hh[2]).then_inc(c_ld, 16)
            sp.dma_start(bres[0:NC, 0:2 * P].rearrange("j (g n) -> j g n", g=2), gate_of(bias_hh, 0, 2)).then_inc(c_ld, 16)
            sp.dma_start(sel_f[0:3 * NC, :], sel).then_inc(c_ld, 16)
            sp.dma_start(xt[0], xT[0].rearrange("p (c b) -> p c b", c=NC)).then_inc(xt_ld[0], 16)
            sp.dma_start(xt[1], xT[1].rearrange("p (c b) -> p c b", c=NC)).then_inc(xt_ld[1], 16)
            sp.dma_start(hT[1], cond_T.rearrange("p (c b) -> p c b", c=NC)).then_inc(h0_ld, 16)
            sp.dma_start(h_q[1], cond_quad).then_inc(h0_ld, 16)
            sp.dma_start(whh, W_hh.rearrange("p (c n) -> p c n", c=NC)).then_inc(w_gru, 16)
            sp.dma_start(identf, ident).then_inc(c_ld, 16)
            sp.dma_start(mean_w, ones[0]).then_inc(c_ld, 16)
            sp.dma_start(rots, rot.rearrange("r p m -> p r m")).then_inc(c_ld, 16)
            sp.dma_start(trigs, trig.rearrange("r p m -> p r m")).then_inc(c_ld, 16)
            sp.dma_start(masks, mask).then_inc(c_ld, 16)
            sp.dma_start(wq, Wq.rearrange("p (c n) -> p c n", c=NC)).then_inc(w_att, 16)
            sp.dma_start(wkv, Wkv.rearrange("p (c n) -> p c n", c=NC)).then_inc(w_att, 16)
            def x_tile(i, par):
                sp.wait_ge(gx_mm, 2 * i + par - 1)
                sp.dma_start(xt[par], xT[bass.ds(2 * i + par, 1)].rearrange("a p (c b) -> p (a c) b", c=NC)).then_inc(xt_ld[par], 16)

            sp.dma_start(idx.bitcast(I32), down_idx[0:P, :]).then_inc(idx_ld, 16)
            sp.dma_start(wdraw, w_down[0:P, :]).then_inc(wd_ld, 16)
            sp.wait_ge(bias_split, 6)
            for k in range(3):
                sp.dma_start(bstack[NC * k:NC * k + NC, :], bparts[k][0:NC, :]).then_inc(stack_ld, 16)
            def x_tiles(i, rows):
                for par in range(2):
                    x_tile(i, par)
                    if rows == "gu":
                        k = i - 1 - PREP_GU[0]
                        sp.wait_ge(w_cp, PRIMED + 2 * k + par + 1)
                        sp.dma_start(wgu_scr[par, :, :, bass.ds(k * P, P)], wst[:, 0:NC, :]).then_inc(wgu_wr, 16)
                    if rows == "d" and par == 1:
                        k = i - 1 - PREP_D[0]
                        sp.wait_ge(w_cp, PRIMED + 2 * IC + k + 1)
                        sp.dma_start(wd_scr[:, :, bass.ds(k * P, P)], wst).then_inc(wd_wr, 16)

            def next_index(i):
                k = i - PREP_GU[0] + 1
                sp.wait_ge(wraw_ld, 32 * k)
                sp.dma_start(idx.bitcast(I32), down_idx[bass.ds(k * P, P), :]).then_inc(idx_ld, 16)

            def next_down_rows(i):
                k = i - PREP_D[0] + 1
                sp.wait_ge(w_scaled, PRIMED + 2 * IC + k)
                sp.dma_start(wdraw, w_down[bass.ds(k * P, P), :]).then_inc(wd_ld, 16)
            x_tiles(PREP_GU[0], None)
            next_index(PREP_GU[0])
            with sp.Fori(PREP_GU[0] + 1, PREP_GU[1] - 1) as i:
                x_tiles(i, "gu")
                next_index(i)
            x_tiles(PREP_GU[1] - 1, "gu")
            x_tiles(PREP_D[0], "gu")
            next_down_rows(PREP_D[0])
            with sp.Fori(PREP_D[0] + 1, PREP_D[1] - 1) as i:
                x_tiles(i, "d")
                next_down_rows(i)
            x_tiles(PREP_D[1] - 1, "d")
            x_tiles(PREP_D[1], "d")
            with sp.Fori(PREP_D[1] + 1, T // 2) as i:
                x_tiles(i, None)
            sp.wait_ge(hs_cp, PRIMED + T)
            sp.wait_ge(wgu_wr, PRIMED + 16 * 2 * IC)
            sp.wait_ge(wd_wr, PRIMED + 16 * NC)
            sp.wait_ge(idx_ld, 16 * IC)
            sp.wait_ge(wd_ld, 16 * NC)
            sp.dma_start(wo, Wo.rearrange("p (h n) -> p h n", h=HEADS)).then_inc(w_att, 16)
            sp.wait_ge(w_kept, 2 * IC + NC)
            sp.dma_start(scale_scr.rearrange("k p -> p k"), row_scales, allow_slow_non_contiguous=True).then_inc(ws_wr, 16)
            sp.dma_start(gam, gamma).then_inc(st_ld, 16)

            def x_rows(blk):
                for pr in range(PAIRS):
                    src = x[bass.ds(blk * BLK + pr * P, P), :]
                    sp.dma_start(xres[:, pr, :], src).then_inc(x_ld, 16)

            def x1_rows(blk):
                for pr in range(PAIRS):
                    sp.wait_ge(x1_done, PRIMED + PAIRS * blk + pr + 1)
                    for b2 in range(2):
                        dst = x1_scr[:, :, bass.ds(blk * BLK_B + 2 * pr + b2, 1), :]
                        src = xres[64 * b2:64 * b2 + 64, pr, :].rearrange("p (j a n) -> p j a n", j=NC, a=1)
                        sp.dma_start(dst, src).then_inc(x1_wr, 16)
            x_rows(0)
            with sp.Fori(0, NBLK - 1) as blk:
                x1_rows(blk)
                sp.wait_ge(x1_wr, 16 * 2 * PAIRS * (blk + 1))
                x_rows(blk + 1)
            x1_rows(NBLK - 1)
            sp.dma_start(ct, couplingT.rearrange("p (c n) -> p c n", c=NC)).then_inc(ct_ld, 16)
            sp.dma_start(biasq, bias_quad).then_inc(ct_ld, 16)
            sp.dma_start(qn[3], cond_quad).then_inc(ct_ld, 16)
            sp.dma_start(pn[1], cond_quad).then_inc(ct_ld, 16)

            sp.wait_ge(x1_wr, 16 * B)
            for s in range(4):
                sp.dma_start(drive[s], x1_scr[s].rearrange("j b n -> (j b) n")).then_inc(drive_ld[s], 16)
            sp.wait_ge(ws_wr, 16)
            sp.dma_start(wgT, wgu_scr[0]).then_inc(ffn_ld, 16)
            sp.dma_start(wuT, wgu_scr[1]).then_inc(ffn_ld, 16)
            sp.dma_start(wdT, wd_scr).then_inc(ffn_ld, 16)
            for row, lo, hi in ((gs_row, 0, IC), (us_row, IC, 2 * IC), (ds_row, 2 * IC, 2 * IC + NC)):
                sp.dma_start(row, scale_scr[lo:hi, :].rearrange("k p -> (k p)").partition_broadcast(P)).then_inc(ffn_ld, 16)

            def q_store(i, s):
                sp.wait_ge(rk_q, 4 * i + s + 1)
                sp.dma_start(q_scr[bass.ds(4 * i + s, 1)].rearrange("a j b n -> (a j b) n"), qn[s]).then_inc(q_wr[s], 16)
            def tile_loads(i):
                for s in range(TILE_T):
                    if s == 0:
                        sp.wait_ge(f_vq, PRIMED + i)
                    sp.wait_ge(q_wr[s], PRIMED + 16 * (i + 1))
                    sp.dma_start(qt[32 * s:32 * s + 32, :].rearrange("p (j n) -> p j n", j=NC),
                                 q_scr[bass.ds(i * TILE_T + s, 1)].rearrange("a j b n -> (a b) j n")).then_inc(q_ld, 16)

            def tile_x1(i):
                sp.wait_ge(f_out, PRIMED + i)
                for s in range(TILE_T):
                    sp.dma_start(x1t[32 * s:32 * s + 32, :].rearrange("p (j n) -> p j n", j=NC),
                                 x1_scr[bass.ds(i * TILE_T + s, 1)].rearrange("a j b n -> (a b) j n")).then_inc(x1_ld, 16)

            def tile_store(i):
                sp.wait_ge(f_out, PRIMED + i + 1)
                for s in range(TILE_T):
                    sp.dma_start(out[:, bass.ds(i * TILE_T + s, 1), :].rearrange("b a n -> (b a) n"),
                                 yout[32 * s:32 * s + 32, :]).then_inc(o_wr, 16)

            def next_drive(i, s):
                sp.dma_start(drive[s], x1_scr[bass.ds(4 * i + 4 + s, 1)].rearrange("a j b n -> (a j b) n")).then_inc(drive_ld[s], 16)

            def group(g, rk, drives):
                for s in range(4):
                    if rk:
                        q_store(g, s)
                        if drives:
                            next_drive(g, s)
                    if s == 2 and not_before(g - 3, 0) and g - 3 < NTILE:
                        tile_store(g - 3)
                        if g - 2 < NTILE:
                            tile_x1(g - 2)
                    if s == 2 and isinstance(g, int) and g == 2:
                        tile_x1(0)
                if rk:
                    tile_loads(g)
            for g in range(LEAD):
                group(g, True, True)
            with sp.Fori(LEAD, NTILE - 1) as g:
                for s in range(4):
                    q_store(g, s)
                    next_drive(g, s)
                    if s == 2:
                        tile_store(g - 3)
                        tile_x1(g - 2)
                tile_loads(g)
            group(NTILE - 1, True, False)
            for g in range(NTILE, NTILE + LEAD):
                group(g, False, False)
            sp.wait_ge(o_wr, PRIMED + 16 * TILE_T * NTILE)

        @block.gpsimd
        def _(pool):
            for s_ in (hs_cp, x1_done, f_vq, f_out, w_tr, w_cp, wgu_wr, wd_wr, w_scaled, o_wr, *q_wr):
                pool.sem_inc(s_, PRIMED)
            def keep_state(i, par):
                t = 2 * i + par
                pool.wait_ge(hT_done, t + 1)
                pool.tensor_copy(hsT.rearrange("p c (b t) -> p c b t", t=T)[:, :, :, bass.ds(t, 1)],
                                 hT[par].rearrange("p c (b a) -> p c b a", a=1)).then_inc(hs_cp, 1)

            def gather(n):
                pool.wait_ge(idx_ld, 16 * (n + 1))
                pool.wait_ge(w_scaled, PRIMED + 2 * n)
                pool.sem_inc(gather_go, 1)
                for k, src in enumerate((w_gate, w_up)):
                    pool.indirect_dma_start(out=wraw[:, k, :], out_offset=None, in_=src,
                                            in_offset=bass.IndirectOffsetOnAxis(ap=idx.bitcast(U32), axis=0)).then_inc(wraw_ld, 16)
            gather(0)
            keep_state(0, 0)
            keep_state(0, 1)
            with pool.Fori(1, IC) as i:
                keep_state(i, 0)
                keep_state(i, 1)
                gather(i)
            with pool.Fori(IC, T // 2) as i:
                keep_state(i, 0)
                keep_state(i, 1)

        @block.tensor
        def _(pe):
            pe.wait_ge(stack_ld, 48)
            pe.wait_ge(bias_split, 6)
            pe.wait_ge(w_gru, 16 * 2)

            def x_part(t, par, prev):
                pe.wait_ge(xt_ld[par], 8 * (t - par) + 16)
                if prev:
                    pe.wait_ge(npre_done, t - 1)
                pe.matmul(ps[:, par, :], sel_b[0:3 * NC, :], bstack[0:3 * NC, :], start=True, stop=False, skip_group_check=True)
                for c in range(NC):
                    for j in range(NC):
                        mm = pe.matmul(ps[32 * j:32 * j + 32, par, 0:3 * P].rearrange("p (g n) -> p g n", g=3), xt[par][:, c, :],
                                       wih[:, c, :].rearrange("p (g j n) -> p g j n", g=3, j=NC)[:, :, j, :],
                                       start=False, stop=False, skip_group_check=True, tile_position=(0, 32 * j))
                mm.then_inc(gx_mm, 1)

            def h_part(t, par):
                for c in range(NC):
                    for j in range(NC):
                        mm = pe.matmul(ps[32 * j:32 * j + 32, par, P:4 * P].rearrange("p (g n) -> p g n", g=3), hT[1 - par][:, c, :],
                                       whh[:, c, :].rearrange("p (g j n) -> p g j n", g=3, j=NC)[:, :, j, :],
                                       start=False, stop=(c == NC - 1), skip_group_check=True, tile_position=(0, 32 * j))
                mm.then_inc(gates_mm, 1)
            x_part(0, 0, False)
            x_part(1, 1, False)
            pe.wait_ge(h0_ld, 32)
            h_part(0, 0)
            def turn_rows(n, chunks):
                pe.wait_ge(w_q8, n + 1)
                pe.wait_ge(w_cp, PRIMED + n)
                for c in range(chunks):
                    mm = pe.transpose(ps[:, 2 + c // 8, :].bitcast(BF16)[:, (c % 8) * P:(c % 8 + 1) * P], wq8[:, c * P:(c + 1) * P], id_b1)
                mm.then_inc(w_tr, 1)

            def pair_of_steps(i, prep):
                for par in range(2):
                    x_part(2 * i + par, par, True)
                    if prep == "gu":
                        turn_rows(2 * (i - 1 - PREP_GU[0]) + par, NC)
                    if prep == "d" and par == 1:
                        turn_rows(2 * IC + i - 1 - PREP_D[0], IC)
                    pe.wait_ge(hT_done, 2 * i - 1 + par)
                    h_part(2 * i - 1 + par, 1 - par)
            pe.wait_ge(idb_done, 1)
            pair_of_steps(PREP_GU[0], None)
            with pe.Fori(PREP_GU[0] + 1, PREP_GU[1] + 1) as i:
                pair_of_steps(i, "gu")
            with pe.Fori(PREP_D[0] + 1, PREP_D[1] + 1) as i:
                pair_of_steps(i, "d")
            with pe.Fori(PREP_D[1] + 1, T // 2) as i:
                pair_of_steps(i, None)
            pe.wait_ge(hT_done, T - 1)
            h_part(T - 1, 1)

            pe.wait_ge(hs_cp, PRIMED + T)
            pe.wait_ge(c_ld, 16 * N_CONST)
            with pe.Fori(0, NLN) as i:
                for c in range(NC):
                    mm = pe.matmul(ps[:, 0, :], mean_w, hsT[:, c, bass.ds(i * LN_TOK, LN_TOK)], start=(c == 0), stop=(c == NC - 1))
                mm.then_inc(mean_mm, 1)
                pe.wait_ge(sq_done, i + 1)
                for c in range(NC):
                    mm = pe.matmul(ps[:, 1, :], mean_w, sq[:, c, :], start=(c == 0), stop=(c == NC - 1))
                mm.then_inc(var_mm, 1)
                pe.wait_ge(ve_done, i + 1)

            def out_proj(blk):
                pe.wait_ge(x1_done, PRIMED + PAIRS * blk)
                for pr in range(PAIRS):
                    pe.wait_ge(ao_cp, 4 * (PAIRS * blk + pr + 1))
                    for h in range(HEADS):
                        mm = pe.matmul(ps[:, 6 + pr, :], aoT[:, h, pr * P:pr * P + P], wo[:, h, :], start=(h == 0), stop=(h == HEADS - 1))
                    mm.then_inc(wo_mm, 1)

            def q_heads(blk, h0, h1):
                for h in range(h0, h1):
                    bank = h % 2
                    if h >= 2:
                        pe.wait_ge(q_ev, 2 * (HEADS * blk + h - 1))
                    for c in range(NC):
                        mm = pe.matmul(ps[:, bank, 0:BLK], wq[:, c, h * DH:(h + 1) * DH], xnb[:, c, :], start=(c == 0), stop=(c == NC - 1))
                    mm.then_inc(q_mm, 1)

            def attn_block(blk, first):
                pe.wait_ge(xn_done, blk + 1)
                if not first:
                    pe.wait_ge(x1_done, PRIMED + PAIRS * (blk - 1))
                    pe.wait_ge(pT_cp, 2 * PAIRS * blk)
                    pe.wait_ge(ao_cp, 4 * PAIRS * blk)
                for c in range(NC):
                    mm = pe.matmul(ps[:, 7, 0:BLK], wkv[:, c, 0:DH], xnb[:, c, :], start=(c == 0), stop=(c == NC - 1))
                mm.then_inc(k_mm, 1)
                for pr in range(PAIRS):
                    for c in range(NC):
                        mm = pe.matmul(ps[:, 5, pr * DH:(pr + 1) * DH], xnb[:, c, pr * P:pr * P + P], wkv[:, c, DH:], start=(c == 0), stop=(c == NC - 1))
                mm.then_inc(v_mm, 1)
                q_heads(blk, 0, 6)
                pe.wait_ge(kraw_cp, blk + 1)
                pe.matmul(ps[:, 7, 0:BLK], rots[:, 0, :], kraw, start=True, stop=True).then_inc(rot_mm, 1)
                q_heads(blk, 6, 12)
                pe.wait_ge(kr_done, blk + 1)
                pe.matmul(ps[:, 7, BLK:2 * BLK], rots[:, 1, :], kr, start=True, stop=True).then_inc(rot2_mm, 1)
                q_heads(blk, 12, HEADS)
                pe.wait_ge(krr_cp, blk + 1)
                pe.wait_ge(q_ev, 2 * HEADS * (blk + 1))
                pe.wait_ge(v_cp, blk + 1)
                for pr in range(PAIRS):
                    for b2 in range(2):
                        if pr:
                            pe.wait_ge(masked, 2 * PAIRS * blk + 2 * pr - 1 + b2)
                        b = 2 * pr + b2
                        for hp in range(HP):
                            o = ps[:, 2 + 2 * b2 + hp // 4, (hp % 4) * P:(hp % 4 + 1) * P]
                            pe.matmul(o, q_cos[:, b, hp * P:(hp + 1) * P], kr[:, pr * P:(pr + 1) * P], start=True, stop=False)
                            mm = pe.matmul(o, q_sin[:, b, hp * P:(hp + 1) * P], krr[:, pr * P:(pr + 1) * P], start=False, stop=True)
                        mm.then_inc(s_mm, 1)
                if not first:
                    out_proj(blk - 1)
                for pr in range(PAIRS):
                    pe.wait_ge(p_done, 2 * (PAIRS * blk + pr + 1))
                    for half in range(2):
                        n = 2 * pr + half
                        if n >= 2:
                            pe.wait_ge(pT_cp, 2 * PAIRS * blk + n - 1)
                        for hp in range(4 * half, 4 * half + 4):
                            mm = pe.transpose(ps[:, half, (hp % 4) * P:(hp % 4 + 1) * P], probs[:, pr, hp * P:(hp + 1) * P], identf)
                        mm.then_inc(pT_mm, 1)
                    pe.wait_ge(pT_cp, 2 * PAIRS * blk + 2 * pr + 2)
                    pe.wait_ge(masked, 2 * PAIRS * (blk + 1))
                    for half in range(2):
                        for b2 in range(2):
                            n = 4 * pr + 2 * half + b2
                            if n >= 3:
                                pe.wait_ge(ao_cp, 4 * PAIRS * blk + n - 2)
                            pe.matmul(ps[:, PV_BANKS[n % 3], :], vtok[64 * b2:64 * b2 + 64, pr, :], pT[64 * b2:64 * b2 + 64, half * 512:(half + 1) * 512],
                                      start=True, stop=True).then_inc(pv_mm, 1)
            pe.wait_ge(w_att, 48)
            attn_block(0, True)
            with pe.Fori(1, NBLK) as blk:
                attn_block(blk, False)
            out_proj(NBLK - 1)

            def mm_mix(o, m, src, first):
                pe.matmul(o, mix[m], src, start=first, stop=False, skip_group_check=True)

            def stage(t, s, st):
                o = ps[:, st % 2, 0:P]
                if st == 0:
                    pe.wait_ge(rk_e, t + 1)
                pe.wait_ge(rk_qT, 4 * t + st) if st else None
                mm_mix(o, 0, emp[s % 2], True)
                for k, m in STAGE_MIX[st]:
                    src = (pn[(s - 1) % 2], qn[(s - 1) % 4], *qst)[k]
                    if k == st + 1 and st:
                        pe.wait_ge(rk_qT, 4 * t + st + 1)
                    mm_mix(o, m, src, False)
                pe.wait_ge(rk_th, 4 * t + st + 1)
                for c in range(NC):
                    for j in range(NC):
                        mm = pe.matmul(ps[32 * j:32 * j + 32, st % 2, 0:P], thT[:, c, :], ct[:, c, j * P:(j + 1) * P],
                                       start=False, stop=(c == NC - 1), skip_group_check=True, tile_position=(0, 32 * j))
                mm.then_inc(rk_mm, 1)

            def product(i, m, k):
                done = (f_gsc, f_usc)[k]
                wait_if(pe, done, GU_T * i + m - 1)
                for c in range(NC):
                    mm = pe.matmul(ps[:, 2 + 2 * (m % 2) + k, 0:GU_N], qxT[:, c, :], (wgT, wuT)[k][:, c, m * GU_N:(m + 1) * GU_N],
                                   start=(c == 0), stop=(c == NC - 1))
                mm.then_inc((f_g, f_u)[k], 1)

            def slot(k, tile):
                i = tile(0)
                if i is not None:
                    if k == 9:
                        pe.wait_ge(f_q8, i + 1)
                        for c in range(NC):
                            mm = pe.transpose(ps[:, 6, 0:2 * P].bitcast(BF16)[:, c * P:(c + 1) * P], qx8[:, c * P:(c + 1) * P], id_b)
                        mm.then_inc(f_qT, 1)
                    if k == 10:
                        pe.wait_ge(f_qTcp, i + 1)
                    if k >= 10:
                        product(i, (k - 10) // 2, k % 2)
                i = tile(1)
                if i is not None:
                    if k < 2:
                        product(i, 3, k)
                    if k == 13:
                        pe.wait_ge(f_t8, i + 1)
                        for c in range(IC):
                            mm = pe.transpose(ps[:, 6 + c // 8, :].bitcast(BF16)[:, (c % 8) * P:(c % 8 + 1) * P], t8[:, c * P:(c + 1) * P], id_b)
                        mm.then_inc(f_tT, 1)
                    if k == 14:
                        pe.wait_ge(f_tTcp, 2 * i + 2)
                    if k >= 14:
                        down(i, k - 14)
                i = tile(2)
                if i is not None and k < 2:
                    down(i, 2 + k)

            def down(i, part):
                for c in range(3 * part, min(3 * part + 3, IC)):
                    mm = pe.matmul(ps[:, 7, :], t8T[:, c, :], wdT[:, c, :], start=(c == 0), stop=(c == IC - 1))
                if part == 3:
                    mm.then_inc(f_y, 1)

            def group(g, rk, tile):
                for k in range(16):
                    if rk:
                        stage(4 * g + k // 4, k // 4, k % 4)
                    slot(k, tile)
            pe.wait_ge(ct_ld, 16 * 4)
            pe.wait_ge(rk_mix, len(MIX))
            pe.wait_ge(ffn_ld, 16 * 6)
            in_groups(pe, group)

        @block.scalar
        def _(act):
            def gru_step(t, par):
                act.wait_ge(gates_mm, t + 1)
                act.activation(rz[par], ps[:, par, P:3 * P].rearrange("p (g n) -> p g n", g=2), ACT.Sigmoid).then_inc(rz_done, 1)
                act.wait_ge(npre_done, t + 1)
                act.activation(nval, npre, ACT.Tanh).then_inc(n_done, 1)
            def scaled_rows(n, src, width, chunks):
                act.wait_ge(w_rs, n + 1)
                act.activation(wv[:, 0:width], src, ACT.Copy, scale=rs[:, 0:1]).then_inc(w_scaled, 1)

            def rows_out(n, chunks, stored, count):
                act.wait_ge(w_tr, PRIMED + n + 1)
                act.wait_ge(stored, count)
                if chunks > 8:
                    act.activation(wst[:, 8:chunks, :], ps[:, 3, :].bitcast(BF16)[:, 0:(chunks - 8) * P].rearrange("p (c n) -> p c n", n=P),
                                   ACT.Copy)
                m = min(chunks, 8)
                act.activation(wst[:, 0:m, :], ps[:, 2, :].bitcast(BF16)[:, 0:m * P].rearrange("p (c n) -> p c n", n=P),
                               ACT.Copy).then_inc(w_cp, 1)
            act.wait_ge(c_ld, 16 * N_CONST)
            act.activation(id_b1, identf, ACT.Copy).then_inc(idb_done, 1)
            gru_step(0, 0)
            gru_step(1, 1)
            with act.Fori(PREP_GU[0], PREP_GU[1]) as i:
                for par in range(2):
                    n = 2 * (i - PREP_GU[0]) + par
                    scaled_rows(n, wraw[:, par, :], D, NC)
                    gru_step(2 * i + par, par)
                    rows_out(n, NC, wgu_wr, PRIMED + 16 * n)
            with act.Fori(PREP_D[0], PREP_D[1]) as i:
                n = 2 * IC + i - PREP_D[0]
                scaled_rows(n, wdraw, INNER, IC)
                gru_step(2 * i, 0)
                gru_step(2 * i + 1, 1)
                if True:
                    act.wait_ge(wgu_wr, PRIMED + 16 * 2 * IC)
                rows_out(n, IC, wd_wr, PRIMED + 16 * (i - PREP_D[0]))
            with act.Fori(PREP_D[1], T // 2) as i:
                gru_step(2 * i, 0)
                gru_step(2 * i + 1, 1)

            with act.Fori(0, NLN) as i:
                act.wait_ge(xc_done, i + 1)
                act.activation(sq, hsT[:, :, bass.ds(i * LN_TOK, LN_TOK)], ACT.Square).then_inc(sq_done, 1)
                act.wait_ge(ve_done, i + 1)
                act.activation(root, var, ACT.Sqrt).then_inc(root_done, 1)

            def attn_block(blk):
                act.wait_ge(k_mm, blk + 1)
                act.activation(kraw, ps[:, 7, 0:BLK], ACT.Copy).then_inc(kraw_cp, 1)
                act.wait_ge(v_mm, blk + 1)
                act.activation(vtok, ps[:, 5, 0:PAIRS * DH].rearrange("p (a n) -> p a n", a=PAIRS), ACT.Copy).then_inc(v_cp, 1)
                act.wait_ge(rot2_mm, blk + 1)
                act.activation(krr, ps[:, 7, BLK:2 * BLK], ACT.Copy).then_inc(krr_cp, 1)
                for n in range(2 * PAIRS):
                    act.wait_ge(shifted, 2 * PAIRS * blk + n + 1)
                    pb = probs[:, n // 2, :].rearrange("p (h b j) -> p h b j", h=HP, b=2)[:, :, n % 2, :]
                    act.activation(pb, pb, ACT.Exp).then_inc(exp_done, 1)
                for pr in range(PAIRS):
                    for half in range(2):
                        act.wait_ge(pT_mm, 2 * (PAIRS * blk + pr) + half + 1)
                        if pr and half == 0:
                            act.wait_ge(pv_mm, 4 * (PAIRS * blk + pr))
                        act.activation(pT[:, half * 512:(half + 1) * 512], ps[:, half, :], ACT.Copy).then_inc(pT_cp, 1)
                    for half in range(2):
                        for b2 in range(2):
                            act.wait_ge(pv_mm, 4 * (PAIRS * blk + pr) + 2 * half + b2 + 1)
                            tk = (2 * pr + b2) * T
                            act.activation(aoT[:, 8 * half:8 * half + 8, tk:tk + T],
                                           ps[:, PV_BANKS[(4 * pr + 2 * half + b2) % 3], :].rearrange("p (h t) -> p h t", h=8), ACT.Copy).then_inc(ao_cp, 1)
            with act.Fori(0, NBLK) as blk:
                attn_block(blk)

            def stage(t, s, st):
                n = 4 * t + st
                act.wait_ge(rk_qT, n + 1)
                act.activation(thT, qsT, ACT.Tanh).then_inc(rk_th, 1)
                src = qn[(s - 1) % 4] if st == 0 else qst[st - 1]
                act.activation(cube, src, ACT.Square, scale=3.0 ** -0.5).then_inc(rk_sq, 1)

            def silu_part(i, m):
                act.wait_ge(f_gsc, GU_T * i + m + 1)
                wait_if(act, f_gated, GU_T * i + m - 1)
                act.activation(sig[m % 2], gsc[m % 2], ACT.Sigmoid).then_inc(f_sig, 1)

            def slot(k, tile):
                i = tile(0)
                if i is not None:
                    if k == 5:
                        act.wait_ge(f_rq, i + 1)
                        act.activation(vq, qt, ACT.Copy, scale=xrs).then_inc(f_vq, 1)
                    if k == 9:
                        act.wait_ge(f_qT, i + 1)
                        act.activation(qxT, ps[:, 6, 0:2 * P].bitcast(BF16).rearrange("p (c n) -> p c n", c=NC), ACT.Copy).then_inc(f_qTcp, 1)
                    if k in (12, 14):
                        silu_part(i, (k - 12) // 2)
                i = tile(1)
                if i is not None:
                    if k in (0, 2):
                        silu_part(i, 2 + k // 2)
                    if k == 6:
                        act.wait_ge(f_rt, i + 1)
                        act.activation(vt, tt, ACT.Copy, scale=trs).then_inc(f_vt, 1)
                    if k == 13:
                        act.wait_ge(f_tT, i + 1)
                        act.activation(t8T[:, 0:8, :], ps[:, 6, :].bitcast(BF16).rearrange("p (c n) -> p c n", c=8), ACT.Copy).then_inc(f_tTcp, 1)
                        act.activation(t8T[:, 8:IC, :], ps[:, 7, :].bitcast(BF16)[:, 0:(IC - 8) * P].rearrange("p (c n) -> p c n", c=IC - 8),
                                       ACT.Copy).then_inc(f_tTcp, 1)

            def group(g, rk, tile):
                for k in range(16):
                    if rk:
                        stage(4 * g + k // 4, k // 4, k % 4)
                    slot(k, tile)
            in_groups(act, group)

        @block.vector
        def _(dve):
            def bcast(row, nb):
                return row.unsqueeze(1).to_broadcast([P, nb, T])

            dve.wait_ge(c_ld, 16 * N_CONST)
            b4, r4 = bg[0:NC, :], bres[0:NC, :]
            dve.tensor_copy(sel_b[0:3 * NC, :], sel_f[0:3 * NC, :]).then_inc(bias_split, 1)
            dve.tensor_tensor(b4[:, P:3 * P], b4[:, P:3 * P], r4[:, 0:2 * P], ALU.add).then_inc(bias_split, 1)
            dve.wait_ge(bias_split, 2)
            dve.tensor_copy(bparts[0][0:NC, :], b4).then_inc(bias_split, 1)
            dve.wait_ge(bias_split, 3)
            dve.tensor_tensor(r4, b4, bparts[0][0:NC, :], ALU.subtract).then_inc(bias_split, 1)
            dve.wait_ge(bias_split, 4)
            dve.tensor_copy(bparts[1][0:NC, :], r4).then_inc(bias_split, 1)
            dve.wait_ge(bias_split, 5)
            dve.tensor_tensor(bparts[2][0:NC, :], r4, bparts[1][0:NC, :], ALU.subtract).then_inc(bias_split, 1)

            def grid_of(v, x_, e):
                v.need(v.did(dve.tensor_scalar(e.bitcast(U32), x_.bitcast(U32), EXP_BITS, None, ALU.bitwise_and)))
                return v.did(dve.tensor_scalar(e, e, FP8_TINY, ROUND_AT, ALU.max, ALU.mult))

            def weight_scale(n, col, src):
                v = Steps(dve, w_v, W_STEPS * n)
                v.need(v.did(dve.tensor_reduce(am, src, AX.X, ALU.max, apply_absolute_value=True)))
                scaled = v.did(dve.tensor_scalar(wsc, am, 1.0 / FP8_MAX, None, ALU.mult))
                dve.tensor_scalar(row_scales[:, bass.ds(col, 1)], am, 1.0 / FP8_MAX, None, ALU.mult).then_inc(w_kept, 1)
                v.need(scaled)
                dve.reciprocal(rs, wsc).then_inc(w_rs, 1)

            def weight_round(n, width):
                v = Steps(dve, w_v, W_STEPS * n + 2)
                x_, e = wv[:, 0:width], wexp[:, 0:width]
                dve.wait_ge(w_scaled, PRIMED + n + 1)
                v.need(grid_of(v, x_, e))
                v.need(v.did(dve.tensor_tensor(x_, x_, e, ALU.add)))
                dve.wait_ge(w_tr, PRIMED + n)
                dve.tensor_tensor(wq8[:, 0:width], x_, e, ALU.subtract).then_inc(w_q8, 1)
                assert v.n + 2 == W_STEPS
            W_STEPS = 5

            dve.wait_ge(h0_ld, 32)

            def gru_pair(i, prep):
                for par in range(2):
                    t = 2 * i + par
                    if prep == "gu":
                        n = 2 * (i - PREP_GU[0]) + par
                        dve.wait_ge(wraw_ld, 32 * (i - PREP_GU[0] + 1))
                        weight_scale(n, i - PREP_GU[0] + IC * par, wraw[:, par, :])
                        weight_round(n, D)
                    if prep == "d":
                        n = 2 * IC + i - PREP_D[0]
                        if par == 0:
                            dve.wait_ge(wd_ld, 16 * (i - PREP_D[0] + 1))
                            weight_scale(n, n, wdraw)
                        else:
                            weight_round(n, INNER)
                    r, z = rz[par][:, 0, :], rz[par][:, 1, :]
                    dve.wait_ge(rz_done, t + 1)
                    dve.tensor_tensor(rh, r, ps[:, par, 3 * P:4 * P], ALU.mult).then_inc(rh_done, 1)
                    dve.wait_ge(rh_done, t + 1)
                    dve.tensor_tensor(npre, rh, ps[:, par, 0:P], ALU.add).then_inc(npre_done, 1)
                    dve.tensor_tensor(zh, z, h_q[1 - par], ALU.mult).then_inc(zh_done, 1)
                    dve.tensor_scalar(omz, z, -1.0, 1.0, ALU.mult, ALU.add).then_inc(omz_done, 1)
                    dve.wait_ge(n_done, t + 1)
                    dve.wait_ge(omz_done, t + 1)
                    dve.tensor_tensor(nz, omz, nval, ALU.mult).then_inc(nz_done, 1)
                    dve.wait_ge(zh_done, t + 1)
                    dve.wait_ge(nz_done, t + 1)
                    dve.tensor_tensor(h_q[par], nz, zh, ALU.add).then_inc(h_done, 1)
                    dve.wait_ge(h_done, t + 1)
                    dve.wait_ge(hs_cp, PRIMED + t)
                    dve.transpose(hT[par].rearrange("p c b -> p (c b)"), h_q[par]).then_inc(hT_done, 1)
            gru_pair(0, None)
            with dve.Fori(PREP_GU[0], PREP_GU[1]) as i:
                gru_pair(i, "gu")
            with dve.Fori(PREP_D[0], PREP_D[1]) as i:
                gru_pair(i, "d")
            with dve.Fori(PREP_D[1], T // 2) as i:
                gru_pair(i, None)

            with dve.Fori(0, NLN) as i:
                v = Steps(dve, ln_v, 5 * i)
                dve.wait_ge(mean_mm, i + 1)
                for c in range(NC):
                    one = hsT[:, c, bass.ds(i * LN_TOK, LN_TOK)]
                    mm = dve.tensor_tensor(one, one, ps[:, 0, :], ALU.subtract)
                mm.then_inc(xc_done, 1)
                dve.wait_ge(var_mm, i + 1)
                dve.tensor_scalar(var, ps[:, 1, :], LN_EPS, None, ALU.add).then_inc(ve_done, 1)
                dve.wait_ge(root_done, i + 1)
                v.need(v.did(dve.reciprocal(newt, root)))
                v.need(v.did(dve.tensor_tensor(root, newt, newt, ALU.mult)))
                v.need(v.did(dve.tensor_tensor(root, root, var, ALU.mult)))
                v.need(v.did(dve.tensor_scalar(root, root, -0.5, 1.5, ALU.mult, ALU.add)))
                v.did(dve.tensor_tensor(rstd[:, bass.ds(i * LN_TOK, LN_TOK)], newt, root, ALU.mult))
                assert v.n == 5

            def norm(blk):
                for c in range(NC):
                    mm = dve.scalar_tensor_tensor(out=xnb[:, c, :], in0=hsT[:, c, bass.ds(blk * BLK, BLK)], scalar=gam[:, c:c + 1],
                                                  in1=rstd[:, bass.ds(blk * BLK, BLK)], op0=ALU.mult, op1=ALU.mult)
                mm.then_inc(xn_done, 1)

            def by_time(a):
                return a.rearrange("p (b t) -> p b t", t=T)

            def q_out(blk, h0, h1):
                for h in range(h0, h1):
                    dve.wait_ge(q_mm, HEADS * blk + h + 1)
                    for dst, tr in ((q_cos, 0), (q_sin, 1)):
                        dve.tensor_tensor(dst[:, :, h * T:(h + 1) * T], by_time(ps[:, h % 2, 0:BLK]), bcast(trigs[:, tr, :], BLK_B),
                                          ALU.mult).then_inc(q_ev, 1)

            def softmax(blk, pr):
                def of(n):
                    return probs[:, pr, :].rearrange("p (h b j) -> p h b j", h=HP, b=2)[:, :, n % 2, :]

                def row(a, n):
                    return a[:, n, :].unsqueeze(2).to_broadcast([P, HP, T])

                def at(n):
                    return 2 * PAIRS * blk + n + 1
                two = (2 * pr, 2 * pr + 1)
                for n in two:
                    dve.wait_ge(s_mm, at(n))
                    own = ps[:, 2 + 2 * (n % 2):4 + 2 * (n % 2), :].rearrange("p a (h b j) -> p (a h) b j", b=2, j=T)[:, :, n % 2, :]
                    dve.tensor_tensor(of(n), own, bcast(masks, HP), ALU.add).then_inc(masked, 1)
                for n in two:
                    dve.wait_ge(masked, at(n))
                    dve.tensor_reduce(smax[:, n, :], of(n), AX.X, ALU.max).then_inc(max_done, 1)
                for n in two:
                    dve.wait_ge(max_done, at(n))
                    dve.tensor_tensor(of(n), of(n), row(smax, n), ALU.subtract).then_inc(shifted, 1)
                for n in two:
                    dve.wait_ge(exp_done, at(n))
                    dve.tensor_reduce(ssum[:, n, :], of(n), AX.X, ALU.add).then_inc(sum_done, 1)
                for n in two:
                    dve.wait_ge(sum_done, at(n))
                    dve.reciprocal(ssum[:, n, :], ssum[:, n, :]).then_inc(inv_done, 1)
                for n in two:
                    dve.wait_ge(inv_done, at(n))
                    dve.tensor_tensor(of(n), of(n), row(ssum, n), ALU.mult).then_inc(p_done, 1)

            def residual(blk):
                for pr in range(PAIRS):
                    dve.wait_ge(wo_mm, PAIRS * blk + pr + 1)
                    dve.wait_ge(x_ld, 16 * PAIRS * (blk + 1))
                    dve.tensor_tensor(xres[:, pr, :], ps[:, 6 + pr, :], xres[:, pr, :], ALU.add).then_inc(x1_done, 1)

            def attn_block(blk, first, last):
                dve.wait_ge(kraw_cp, blk + 1)
                dve.tensor_tensor(by_time(kc), by_time(kraw), bcast(trigs[:, 2, :], BLK_B), ALU.mult).then_inc(kc_done, 1)
                q_out(blk, 0, 6)
                dve.wait_ge(rot_mm, blk + 1)
                dve.tensor_tensor(by_time(kr), by_time(ps[:, 7, 0:BLK]), bcast(trigs[:, 3, :], BLK_B), ALU.mult).then_inc(ks_done, 1)
                dve.wait_ge(kc_done, blk + 1)
                dve.wait_ge(ks_done, blk + 1)
                dve.tensor_tensor(kr, kr, kc, ALU.add).then_inc(kr_done, 1)
                q_out(blk, 6, HEADS)
                for pr in range(PAIRS):
                    softmax(blk, pr)
                if not last:
                    norm(blk + 1)
                if not first:
                    residual(blk - 1)
            dve.wait_ge(st_ld, 16)
            dve.wait_ge(ln_v, 5 * NLN)
            norm(0)
            attn_block(0, True, False)
            with dve.Fori(1, NBLK - 1) as blk:
                attn_block(blk, False, False)
            attn_block(NBLK - 1, False, True)
            residual(NBLK - 1)

            dve.wait_ge(x1_wr, 16 * B)
            dve.wait_ge(ct_ld, 16 * 4)
            for m, weight in enumerate(MIX):
                dve.tensor_scalar(mix[m], identf, float(weight), None, ALU.mult).then_inc(rk_mix, 1)
            dve.tensor_copy(id_b, identf).then_inc(rk_start, 1)
            dve.tensor_scalar(biasq, biasq, -ALPHA / BETA, None, ALU.add).then_inc(rk_start, 1)
            dve.tensor_scalar(pn[1], pn[1], -ALPHA / BETA, None, ALU.add).then_inc(rk_start, 1)
            dve.wait_ge(drive_ld[0], 16)
            dve.wait_ge(rk_start, 3)
            dve.tensor_tensor(dsum, drive[0], biasq, ALU.add).then_inc(rk_start, 1)
            dve.wait_ge(rk_start, 4)
            dve.tensor_tensor(emp[0], dsum, pn[1], ALU.subtract).then_inc(rk_e, 1)
            dve.transpose(qsT.rearrange("p c b -> p (c b)"), qn[3]).then_inc(rk_qT, 1)
            dve.wait_ge(ffn_ld, 16 * 6)

            def stage(v, g, s, st, last, fill):
                t = 4 * g + s
                n = 4 * t + st
                q, p = qn[(s - 1) % 4], pn[(s - 1) % 2]
                qs = q if st == 0 else qst[st - 1]
                a = (DT / 2, DT / 2, DT, DT / 6)[st]
                stt = dve.scalar_tensor_tensor
                end = last and s == 3
                if st == 0:
                    v.did(dve.tensor_scalar(w1, p, float(P_NEXT[0]), None, ALU.mult))
                if st == 2 and not end:
                    dve.wait_ge(drive_ld[(s + 1) % 4], 16 * (g + 1 + (s == 3)))
                    v.did(dve.tensor_tensor(dsum, drive[(s + 1) % 4], biasq, ALU.add))
                dve.wait_ge(rk_sq, n + 1)
                e = v.did(stt(out=ebuf, in0=cube, scalar=1.0, in1=qs, op0=ALU.subtract, op1=ALU.mult))
                if st == 0:
                    v.need(e - 1)
                wn = v.did(stt(out=(w2, w3, w4, w5)[st], in0=qs, scalar=float(P_NEXT[1 + st]), in1=(w1, w2, w3, w4)[st], op0=ALU.mult, op1=ALU.add))
                v.need(e)
                if st < 3:
                    gs = v.did(stt(out=gbuf, in0=ebuf, scalar=-a, in1=q, op0=ALU.mult, op1=ALU.add))
                else:
                    gs = v.did(dve.tensor_scalar(gbuf, ebuf, -a, None, ALU.mult))
                    v.need(wn)
                    pc = v.did(dve.tensor_scalar(pn[s % 2], w5, CLAMP - ALPHA / BETA, -CLAMP - ALPHA / BETA, ALU.min, ALU.max))
                    v.need(pc)
                    if not end:
                        dve.tensor_tensor(emp[(s + 1) % 2], dsum, pn[s % 2], ALU.subtract).then_inc(rk_e, 1)
                fill()
                v.need(gs)
                dve.wait_ge(rk_mm, n + 1)
                dst = qst[st] if st < 3 else qpre
                v.need(v.did(stt(out=dst, in0=ps[:, st % 2, 0:P], scalar=a, in1=gbuf, op0=ALU.mult, op1=ALU.add)))
                if st == 3:
                    wait_if(dve, q_wr[s], PRIMED + 16 * g)
                    dve.tensor_scalar(qn[s], qpre, CLAMP, -CLAMP, ALU.min, ALU.max).then_inc(rk_q, 1)
                    dve.wait_ge(rk_q, t + 1)
                    dst = qn[s]
                if not (end and st == 3):
                    dve.transpose(qsT.rearrange("p c b -> p (c b)"), dst).then_inc(rk_qT, 1)

            HALVES = ((0, INNER // 2), (INNER // 2, INNER))

            def slot(v, k, tile):
                i = tile(0)
                if i is not None:
                    if k == 3:
                        dve.wait_ge(q_ld, 16 * TILE_T * (i + 1))
                        v.did(dve.tensor_reduce(xam, qt, AX.X, ALU.max, apply_absolute_value=True))
                    if k == 4:
                        v.need(v.did(dve.tensor_scalar(xsx, xam, 1.0 / FP8_MAX, None, ALU.mult)))
                        dve.reciprocal(xrs, xsx).then_inc(f_rq, 1)
                    if k == 6:
                        dve.wait_ge(f_vq, PRIMED + i + 1)
                        grid_of(v, vq, eq)
                    if k == 7:
                        v.did(dve.tensor_tensor(vq, vq, eq, ALU.add))
                    if k == 8:
                        dve.tensor_tensor(qx8, vq, eq, ALU.subtract).then_inc(f_q8, 1)
                    for m in range(GU_T):
                        gated_part(v, i, m, k - 11 - 2 * m)
                i = tile(1)
                if i is not None:
                    for m in range(GU_T):
                        gated_part(v, i, m, 16 + k - 11 - 2 * m)
                    if k == 4:
                        v.did(dve.tensor_reduce(tam, tt, AX.X, ALU.max, apply_absolute_value=True))
                i2 = tile(2)
                if i2 is not None:
                    if k == 3:
                        dve.wait_ge(f_y, i2 + 1)
                        v.did(dve.scalar_tensor_tensor(out=ysc, in0=ps[:, 7, :], scalar=tsx, in1=ds_row, op0=ALU.mult, op1=ALU.mult))
                    if k == 4:
                        dve.wait_ge(x1_ld, 16 * TILE_T * (i2 + 1))
                        wait_if(dve, o_wr, PRIMED + 16 * TILE_T * i2)
                        dve.tensor_tensor(yout, ysc, x1t, ALU.add).then_inc(f_out, 1)
                if i is not None:
                    if k == 5:
                        v.need(v.did(dve.tensor_scalar(tsx, tam, 1.0 / FP8_MAX, None, ALU.mult)))
                        dve.reciprocal(trs, tsx).then_inc(f_rt, 1)
                    if k == 7:
                        dve.wait_ge(f_vt, i + 1)
                        v.did(dve.tensor_scalar(et.bitcast(U32), vt.bitcast(U32), EXP_BITS, None, ALU.bitwise_and))
                    if k == 8:
                        v.did(dve.tensor_scalar(et, et, FP8_TINY, ROUND_AT, ALU.max, ALU.mult))
                    if k in (9, 10):
                        lo, hi = HALVES[k - 9]
                        v.did(dve.tensor_tensor(vt[:, lo:hi], vt[:, lo:hi], et[:, lo:hi], ALU.add))
                    if k in (11, 12):
                        lo, hi = HALVES[k - 11]
                        ins = dve.tensor_tensor(t8[:, lo:hi], vt[:, lo:hi], et[:, lo:hi], ALU.subtract)
                        ins.then_inc(f_t8, 1) if k == 12 else v.did(ins)

            def gated_part(v, i, m, phase):
                b, cols = m % 2, slice(m * GU_N, (m + 1) * GU_N)
                if phase == 0:
                    dve.wait_ge(f_g, GU_T * i + m + 1)
                    dve.scalar_tensor_tensor(out=gsc[b], in0=ps[:, 2 + 2 * b, 0:GU_N], scalar=xsx, in1=gs_row[:, cols],
                                             op0=ALU.mult, op1=ALU.mult).then_inc(f_gsc, 1)
                if phase == 1:
                    dve.wait_ge(f_u, GU_T * i + m + 1)
                    dve.scalar_tensor_tensor(out=usc[b], in0=ps[:, 3 + 2 * b, 0:GU_N], scalar=xsx, in1=us_row[:, cols],
                                             op0=ALU.mult, op1=ALU.mult).then_inc(f_usc, 1)
                    dve.wait_ge(f_usc, GU_T * i + m + 1)
                    v.did(dve.tensor_tensor(usc[b], gsc[b], usc[b], ALU.mult))
                if phase == 2:
                    dve.wait_ge(f_sig, GU_T * i + m + 1)
                    dve.tensor_tensor(tt[:, cols], sig[b], usc[b], ALU.mult).then_inc(f_gated, 1)

            counts = {}

            def group(g, rk, tile):
                base = 0
                if not isinstance(g, int):
                    base = counts["lead"] + (g - LEAD) * GROUP_STEPS
                else:
                    base = counts["lead"] if g < NTILE - 1 and g >= LEAD else counts.get("next", 0)
                v = Steps(dve, rk_v, base)
                for k in range(16):
                    if rk:
                        stage(v, g, k // 4, k % 4, isinstance(g, int) and g == NTILE - 1, lambda: slot(v, k, tile))
                    else:
                        v.did(dve.tensor_copy(w1[:, 0:1], xsx))
                        v.need(v.n)
                        slot(v, k, tile)
                if isinstance(g, int):
                    counts["next"] = counts.get("next", 0) + v.n
                    if g == LEAD - 1:
                        counts["lead"] = counts["next"]
                else:
                    assert v.n == GROUP_STEPS, v.n
                    counts["next"] += (NTILE - 1 - LEAD) * GROUP_STEPS
            in_groups(dve, group)


def kernel(**inputs):
    import numpy as np
    import concourse.bacc as bacc
    from concourse.bass_utils import run_bass_kernel_spmd

    a = {k: np.asarray(v) for k, v in inputs.items()}

    def by_block(w_):
        return w_.reshape(NC, NC, 32, -1).transpose(0, 2, 1, 3).reshape(P, -1)

    def quad(m):
        return m.reshape(B, NC, P).transpose(1, 0, 2).reshape(P, P)

    wih = a["L0_cond_W_ih"].reshape(D, GATES, D)[:, [2, 0, 1]].reshape(D, -1)
    b_ih, b_hh = a["L0_cond_b_ih"], a["L0_cond_b_hh"]
    x_ = a["x"]
    trig, mask, rot, sel, ones = constants(np)
    arrays = {
        "xT": x_.reshape(B, T, NC, P).transpose(1, 3, 2, 0).reshape(T, P, NC * B),
        "x": x_.reshape(TOK, D),
        "cond_quad": quad(a["cond_2048"]),
        "cond_T": by_block(a["cond_2048"].T),
        "W_ih": wih.reshape(NC, P, -1).transpose(1, 0, 2).reshape(P, -1),
        "W_hh": by_block(a["L0_cond_W_hh"]),
        "bias_ih": b_ih.reshape(GATES, NC, P), "bias_hh": b_hh.reshape(GATES, NC, P),
        "sel": sel,
        "gamma": by_block(a["L0_attn_gamma"][:, None]),
        "Wq": by_block(a["L0_attn_Wq"]), "Wkv": by_block(a["L0_attn_Wkv"]),
        "Wo": a["L0_attn_Wo"].reshape(HEADS, DH, D).transpose(1, 0, 2).reshape(P, -1),
        "couplingT": by_block(a["L0_cond2_coupling"].T),
        "bias_quad": quad(np.broadcast_to(a["L0_cond2_bias"], (B, D))),
        "w_gate": a["L0_ffn_w_gate"], "w_up": a["L0_ffn_w_up"], "w_down": a["L0_ffn_w_down"],
        "down_idx": a["L0_ffn_down_reorder_index"].reshape(INNER, 1),
        "ident": np.eye(P, dtype=np.float32), "ones": ones, "rot": rot, "trig": trig, "mask": mask,
    }
    nc = bacc.Bacc("TRN2", target_bir_lowering=False, num_devices=1)
    arrays = {f"in_{k}": np.ascontiguousarray(v) for k, v in arrays.items()}
    aps = {k[3:]: nc.dram_tensor(k, v.shape, mybir.dt.from_np(v.dtype), kind="ExternalInput").ap() for k, v in arrays.items()}
    x1_scr = nc.dram_tensor("x1_scr", (T, NC, B, P), F32, kind="Internal").ap()
    q_scr = nc.dram_tensor("q_scr", (T, NC, B, P), F32, kind="Internal").ap()
    wgu_scr = nc.dram_tensor("wgu_scr", (2, P, NC, INNER), BF16, kind="Internal").ap()
    wd_scr = nc.dram_tensor("wd_scr", (P, IC, D), BF16, kind="Internal").ap()
    scale_scr = nc.dram_tensor("scale_scr", (2 * IC + NC, P), F32, kind="Internal").ap()
    out = nc.dram_tensor("out_0", (B, T, D), F32, kind="ExternalOutput").ap()
    gru_attn_rk4_ffn(nc, **aps, x1_scr=x1_scr, q_scr=q_scr, wgu_scr=wgu_scr,
                     wd_scr=wd_scr, scale_scr=scale_scr, out=out)
    r = run_bass_kernel_spmd(nc, [arrays], core_ids=[0])
    return r.results[0]["out_0"]


def constants(np):
    inv = 1.0 / 10000.0 ** (np.arange(0, DH, 2, dtype=np.float32) / np.float32(DH))
    fr = (np.arange(T, dtype=np.float32)[None, :] * inv.astype(np.float32)[:, None]).astype(np.float32)
    fr = np.concatenate([fr, fr])
    cos, sin = np.cos(fr.astype(np.float64)), np.sin(fr.astype(np.float64))
    sc = float(DH) ** -0.5
    trig = np.stack([cos * sc, sin * sc, cos, sin]).astype(np.float32)
    i, j = np.arange(P)[:, None] % T, np.arange(T)[None, :]
    mask = np.where(j > i, -np.finfo(np.float32).max, 0).astype(np.float32)
    half = DH // 2
    m = np.zeros((DH, DH), np.float32)
    m[np.arange(half), np.arange(half) + half] = -1
    m[np.arange(half) + half, np.arange(half)] = 1
    rot = np.stack([m.T, m])
    sel = np.tile(np.repeat(np.eye(NC, dtype=np.float32), B, axis=1), (3, 1))
    ones = np.stack([np.full((P, P), 1.0 / D, np.float32), np.ones((P, P), np.float32)])
    return trig, mask, rot, sel, ones
```

```python
from contextlib import ExitStack

import concourse.bass as bass
from concourse import mybir

ALU = mybir.AluOpType
ACT = mybir.ActivationFunctionType
AX = mybir.AxisListType
F32 = mybir.dt.float32
BF16 = mybir.dt.bfloat16
U32 = mybir.dt.uint32
I32 = mybir.dt.int32

P = 128
B, T, D = 32, 64, 512
NC = D // P
GATES = 3
HEADS, DH = 16, 128
HP = HEADS // 2
TOK = B * T
BLK_B = 4
BLK = BLK_B * T
NBLK = B // BLK_B
PAIRS = BLK_B // 2
LN_TOK = 512
NLN = TOK // LN_TOK
INNER = 1408
IC = INNER // P
GU_N = 352
GU_T = INNER // GU_N
TILE_T = P // B
NTILE = T // TILE_T
Q_BANKS = 4
PV_BANKS = (5, 2, 3)
LN_EPS = 1e-5
DT, EPS, ALPHA, BETA, CLAMP = 0.01, 0.08, 0.7, 0.8, 20.0
FP8_MAX = 448.0
FP8_TINY = 2.0 ** -6
ROUND_AT = 1.5 * 2.0 ** 20
EXP_BITS = 0x7F800000
WORDS = 48 * 1024 - 256


def rk4_weights():
    p, q, q2, q3, q4 = ([float(i == k) for i in range(5)] for k in range(5))

    def add(*terms):
        return [sum(c * v[k] for c, v in terms) for k in range(5)]
    a1, a2 = DT / 2 * EPS, DT * EPS
    ps2 = add((1, p), (a1, q), (-a1 * BETA, p))
    ps3 = add((1, p), (a1, q2), (-a1 * BETA, ps2))
    ps4 = add((1, p), (a2, q3), (-a2 * BETA, ps3))
    c = DT / 6 * EPS
    p_next = add((1, p), (c, q), (2 * c, q2), (2 * c, q3), (c, q4), (-c * BETA, p), (-2 * c * BETA, ps2), (-2 * c * BETA, ps3),
                 (-c * BETA, ps4))
    e1 = add((-1, p))
    s = 2 / DT
    minus = [add((-1, v), (-1, e1)) for v in (p, ps2, ps3)]
    minus.append(add((-1, ps4), (-1, e1), (-s, q), (s, q2), (2 * s, q3), (s, q4)))
    return minus, p_next


_MINUS, P_NEXT = rk4_weights()
MIX, STAGE_MIX = [1.0], []
for _row in _MINUS:
    _used = []
    for _k, _w in enumerate(_row):
        if _w != 0.0:
            _used.append((_k, len(MIX)))
            MIX.append(_w)
    STAGE_MIX.append(_used)

PREP_GU = (1, 1 + IC)
PREP_D = (PREP_GU[1], PREP_GU[1] + NC)
LEAD = 3
GROUP_STEPS = 88


def wait_if(eng, sem, value):
    if not isinstance(value, int) or value > 0:
        eng.wait_ge(sem, value)


def in_groups(eng, group):
    def tiles(g):
        def tile(a):
            i = g - 1 - a
            return i if not isinstance(g, int) or 0 <= i < NTILE else None
        return tile
    for g in range(LEAD):
        group(g, True, tiles(g))
    with eng.Fori(LEAD, NTILE - 1) as g:
        group(g, True, tiles(g))
    for g in range(NTILE - 1, NTILE + LEAD):
        group(g, g < NTILE, tiles(g))


class Steps:

    def __init__(self, eng, sem, base):
        self.eng, self.sem, self.base, self.n = eng, sem, base, 0

    def did(self, ins):
        ins.then_inc(self.sem, 1)
        self.n += 1
        return self.n

    def need(self, n):
        self.eng.wait_ge(self.sem, self.base + n)


class Words:

    def __init__(self, at, end):
        self.at, self.end = at, end

    def take(self, n):
        a = self.at
        self.at += n
        assert self.at <= self.end, (self.at, self.end)
        return a


def gru_attn_rk4_ffn(nc, xT, x, cond_quad, cond_T, W_ih, W_hh, bias_ih, bias_hh, sel, gamma, Wq, Wkv, Wo,
                     couplingT, bias_quad, w_gate, w_up, w_down, down_idx, ident, mean_of, trig, mask,
                     x1_scr, q_scr, wgu_scr, wd_scr, scale_scr, out):
    with ExitStack() as ctx:
        mem = ctx.enter_context(nc.sbuf_tensor("mem", [P, WORDS], F32))
        ps = ctx.enter_context(nc.psum_tensor("ps", [P, 8, 512], F32))

        def sem(name):
            return ctx.enter_context(nc.semaphore(name))

        def f32(a, *dims):
            n = 1
            for d in dims:
                n *= d
            v = mem[:, a:a + n]
            if len(dims) == 2:
                v = v.rearrange("p (a b) -> p a b", a=dims[0])
            if len(dims) == 3:
                v = v.rearrange("p (a b c) -> p a b c", a=dims[0], b=dims[1])
            return v

        def bf16(a, *dims):
            n = 1
            for d in dims:
                n *= d
            v = mem[:, a:a + n // 2].bitcast(BF16)
            if len(dims) == 2:
                v = v.rearrange("p (a b) -> p a b", a=dims[0])
            return v

        w = Words(0, WORDS)
        a_hs = w.take(NC * TOK)
        hsT = f32(a_hs, NC, TOK)
        a_ih = w.take(NC * GATES * D)
        a_hh = w.take(NC * GATES * D)
        wih = f32(a_ih, NC, GATES * D)
        whh = f32(a_hh, NC, GATES * D)
        wq = f32(w.take(NC * HEADS * DH), NC, HEADS * DH)
        a_wo = w.take(HEADS * D)
        wo = f32(a_wo, HEADS, D)
        wkv = f32(w.take(NC * 2 * DH), NC, 2 * DH)
        a_p2 = w.at
        q_rot = f32(a_ih, BLK_B, HEADS * T)
        turned = [f32(a_ih + HEADS * BLK + i * BLK, BLK) for i in range(2)]
        aoT = f32(a_ih + 2 * HEADS * BLK, HEADS, BLK)
        rstd = f32(w.take(TOK), TOK)
        xnb = f32(w.take(NC * BLK), NC, BLK)
        probs = f32(w.take(PAIRS * HP * P), PAIRS, HP * P)
        pT = f32(w.take(HP * P), HP * P)
        xres = f32(w.take(PAIRS * D), PAIRS, D)
        kr, kturned = f32(w.take(BLK), BLK), f32(w.take(BLK), BLK)
        vtok = f32(w.take(PAIRS * DH), PAIRS, DH)
        smax = f32(w.take(PAIRS * 2 * HP), PAIRS * 2, HP)
        ssum = f32(w.take(PAIRS * 2 * HP), PAIRS * 2, HP)
        gam = f32(w.take(NC), NC)
        row_scales = f32(w.take(2 * IC + NC), 2 * IC + NC)
        a_const = w.take(P + P + 4 * T + T)
        identf = f32(a_const, P)
        mean_w = f32(a_const + P, P)
        trigs = f32(a_const + 2 * P, 4, T)
        masks = f32(a_const + 2 * P + 4 * T, T)
        g = Words(a_p2, a_const - 64)
        xt = [f32(g.take(NC * B), NC, B) for _ in range(2)]
        hT = [f32(g.take(NC * B), NC, B) for _ in range(2)]
        h_q = [f32(g.take(P), P) for _ in range(2)]
        rz = [f32(g.take(2 * P), 2, P) for _ in range(2)]
        rh, npre, nval, zh, omz, nz = (f32(g.take(P), P) for _ in range(6))
        a_bg = g.take(512 + 256 + 256 + 256 + 512 + 256 + 256 + 64)
        bg = f32(a_bg, 512)
        bres = f32(a_bg + 512 + 256 + 256 + 256, 512)
        bparts = [bf16(a_bg + 512 + 256 * i, 512) for i in range(3)]
        sel_f = f32(a_bg + 512 + 3 * 256 + 512, P)
        sel_b = bf16(a_bg + 512 + 3 * 256 + 512 + P, P)
        id_b1 = bf16(a_bg + 512 + 3 * 256 + 512 + 2 * P + 256, P)
        bstack = bf16(a_bg + 512 + 3 * 256 + 512 + 2 * P, 512)
        g = Words(a_wo, a_wo + HEADS * D)
        wraw = f32(g.take(2 * D), 2, D)
        wdraw = f32(g.take(INNER), INNER)
        wv = f32(g.take(INNER), INNER)
        wexp = f32(g.take(INNER), INNER)
        wq8 = bf16(g.take(INNER // 2), INNER)
        wst = bf16(g.take(INNER // 2), IC, P)
        idx = f32(g.take(1), 1)
        am, wsc, rs = (f32(g.take(1), 1) for _ in range(3))
        g = Words(a_ih, a_ih + 2 * NC * GATES * D)
        sq = [f32(g.take(NC * LN_TOK), NC, LN_TOK) for _ in range(2)]
        g = Words(a_ih + HEADS * BLK + 2 * BLK, a_ih + 2 * HEADS * BLK)
        var = [f32(g.take(LN_TOK), LN_TOK) for _ in range(NLN)]
        newt = [f32(g.take(LN_TOK), LN_TOK) for _ in range(2)]

        w = Words(0, a_const - 64)
        ct = f32(w.take(NC * D), NC, D)
        wgT = bf16(w.take(NC * INNER // 2), NC, INNER)
        wuT = bf16(w.take(NC * INNER // 2), NC, INNER)
        a_wgu_end = w.at
        wdT = bf16(w.take(IC * D // 2), IC, D)
        gs_row, us_row, ds_row = f32(w.take(INNER), INNER), f32(w.take(INNER), INNER), f32(w.take(D), D)
        id_b = bf16(w.take(P // 2), P)
        biasq = f32(w.take(P), P)
        mix = [f32(w.take(P), P) for _ in range(len(MIX))]
        drive = [f32(w.take(P), P) for _ in range(4)]
        qn = [f32(w.take(P), P) for _ in range(4)]
        pn = [f32(w.take(P), P) for _ in range(2)]
        emp = [f32(w.take(P), P) for _ in range(2)]
        qst = [f32(w.take(P), P) for _ in range(3)]
        qsT = f32(w.take(P), NC, B)
        thT = f32(w.take(P), NC, B)
        cube, ebuf, gbuf, dsum, qpre, w1, w2, w3, w4, w5 = (f32(w.take(P), P) for _ in range(10))
        qt = f32(w.take(D), D)
        x1t = f32(w.take(D), D)
        vq, eq = f32(w.take(D), D), f32(w.take(D), D)
        qx8 = bf16(w.take(D // 2), D)
        qxT = bf16(w.take(D // 2), NC, P)
        gsc = [f32(w.take(GU_N), GU_N) for _ in range(2)]
        usc = [f32(w.take(GU_N), GU_N) for _ in range(2)]
        sig = [f32(w.take(GU_N), GU_N) for _ in range(2)]
        tt = f32(w.take(INNER), INNER)
        vt, et = f32(w.take(INNER), INNER), f32(w.take(INNER), INNER)
        t8 = bf16(w.take(INNER // 2), INNER)
        t8T = bf16(w.take(INNER // 2), IC, P)
        ysc = f32(w.take(D), D)
        yout = f32(w.take(D), D)
        tam2 = f32(w.take(2), 2)
        tam, tsx, trs, xam, xsx, xrs = (f32(w.take(1), 1) for _ in range(6))

        (wih_ld, whh_ld, w_att, b_ld, c_ld, xt_ld0, xt_ld1, h0_ld, st_ld, wg_ld, wu_ld, idx_ld, wd_ld, x_ld, x1_wr, q_ld, x1_ld,
         o_wr, ct_ld) = (sem(n) for n in (
             "wih_ld", "whh_ld", "w_att", "b_ld", "c_ld", "xt_ld0", "xt_ld1", "h0_ld", "st_ld", "wg_ld", "wu_ld", "idx_ld", "wd_ld", "x_ld",
             "x1_wr", "q_ld", "x1_ld", "o_wr", "ct_ld"))
        xt_ld, wraw_ld = [xt_ld0, xt_ld1], [wg_ld, wu_ld]
        q_wr = [sem(f"q_wr{i}") for i in range(4)]
        drive_ld = [sem(f"drive_ld{i}") for i in range(4)]
        bias_split, gx_mm, gates_mm, rz_done, rh_done, npre_done, n_done, zh_done, omz_done, nz_done, h_done, hT_done, hs_cp = (
            sem(n) for n in ("bias_split", "gx_mm", "gates_mm", "rz_done", "rh_done", "npre_done", "n_done",
                             "zh_done", "omz_done", "nz_done", "h_done", "hT_done", "hs_cp"))
        mean_mm, xc_done, sq_done, var_mm, ve_done, root_done, ln_v = (
            sem(n) for n in ("mean_mm", "xc_done", "sq_done", "var_mm", "ve_done", "root_done", "ln_v"))
        (xn_done, k_mm, v_mm, q_mm, k_parts, kr_done, v_cp, q_ev, qr_done, s_mm,
         masked, max_done, shifted, exp_done, sum_done, inv_done, p_done, pT_mm, pT_cp, pv_mm, ao_cp, wo_mm,
         x1_done) = (sem(n) for n in (
             "xn_done", "k_mm", "v_mm", "q_mm", "k_parts", "kr_done",
             "v_cp", "q_ev", "qr_done", "s_mm", "masked", "max_done", "shifted", "exp_done", "sum_done", "inv_done",
             "p_done", "pT_mm", "pT_cp", "pv_mm", "ao_cp", "wo_mm", "x1_done"))
        w_v, w_rs, w_scaled, w_q8, w_tr, w_cp, wgu_wr, wd_wr, w_kept, idb_done, gather_go, stack_ld, ws_wr, ffn_ld = (
            sem(n) for n in ("w_v", "w_rs", "w_scaled", "w_q8", "w_tr", "w_cp", "wgu_wr", "wd_wr", "w_kept", "idb_done",
                             "gather_go", "stack_ld", "ws_wr", "ffn_ld"))
        rk_start = sem("rk_start")
        (rk_v, rk_mix, rk_qT, rk_th, rk_mm, rk_sq, rk_e, rk_q) = (
            sem(n) for n in ("rk_v", "rk_mix", "rk_qT", "rk_th", "rk_mm", "rk_sq", "rk_e", "rk_q"))
        (f_rq, f_vq, f_q8, f_qT, f_qTcp, f_g, f_u, f_gsc, f_usc, f_sig, f_gated, f_rt, f_vt, f_t8, f_tT, f_tTcp, f_y,
         f_out, f_xe, f_xa, f_te, f_ta, f_ysc) = (sem(n) for n in (
             "f_rq", "f_vq", "f_q8", "f_qT", "f_qTcp", "f_g", "f_u", "f_gsc", "f_usc", "f_sig", "f_gated", "f_rt",
             "f_vt", "f_t8", "f_tT", "f_tTcp", "f_y", "f_out", "f_xe", "f_xa", "f_te", "f_ta", "f_ysc"))

        PRIMED = 1
        block = ctx.enter_context(nc.Block())
        N_BIAS, N_CONST = 5, 4

        @block.sync
        def _(sp):
            gate_of = lambda a, lo, hi: a[lo:hi].rearrange("g j n -> j g n")
            sp.dma_start(bg[0:NC, 0:P], bias_ih[2]).then_inc(b_ld, 16)
            sp.dma_start(bg[0:NC, P:3 * P].rearrange("j (g n) -> j g n", g=2), gate_of(bias_ih, 0, 2)).then_inc(b_ld, 16)
            sp.dma_start(bg[0:NC, 3 * P:], bias_hh[2]).then_inc(b_ld, 16)
            sp.dma_start(bres[0:NC, 0:2 * P].rearrange("j (g n) -> j g n", g=2), gate_of(bias_hh, 0, 2)).then_inc(b_ld, 16)
            sp.dma_start(sel_f[0:3 * NC, :], sel).then_inc(b_ld, 16)
            sp.dma_start(xt[0], xT[0].rearrange("p (c b) -> p c b", c=NC)).then_inc(xt_ld[0], 16)
            sp.dma_start(xt[1], xT[1].rearrange("p (c b) -> p c b", c=NC)).then_inc(xt_ld[1], 16)
            sp.dma_start(hT[1], cond_T.rearrange("p (c b) -> p c b", c=NC)).then_inc(h0_ld, 16)
            sp.dma_start(h_q[1], cond_quad).then_inc(h0_ld, 16)
            sp.dma_start(wih, W_ih.rearrange("p (c n) -> p c n", c=NC)).then_inc(wih_ld, 16)
            sp.wait_ge(bias_split, 6)
            for k in range(3):
                sp.dma_start(bstack[NC * k:NC * k + NC, :], bparts[k][0:NC, :]).then_inc(stack_ld, 16)
            sp.dma_start(whh, W_hh.rearrange("p (c n) -> p c n", c=NC)).then_inc(whh_ld, 16)
            sp.dma_start(idx.bitcast(I32), down_idx[0:P, :]).then_inc(idx_ld, 16)
            sp.dma_start(identf, ident).then_inc(c_ld, 16)
            sp.dma_start(mean_w, mean_of).then_inc(c_ld, 16)
            sp.dma_start(trigs, trig.rearrange("r p m -> p r m")).then_inc(c_ld, 16)
            sp.dma_start(masks, mask).then_inc(c_ld, 16)
            sp.dma_start(wdraw, w_down[0:P, :]).then_inc(wd_ld, 16)

            def x_tile(i, par):
                sp.wait_ge(gx_mm, 2 * i + par - 1)
                sp.dma_start(xt[par], xT[bass.ds(2 * i + par, 1)].rearrange("a p (c b) -> p (a c) b", c=NC)).then_inc(xt_ld[par], 16)

            def x_tiles(i, now, before):
                x_tile(i, 0)
                x_tile(i, 1)
                for par in range(2):
                    if before == "gu":
                        k = i - 1 - PREP_GU[0]
                        sp.wait_ge(w_cp, PRIMED + 2 * k + par + 1)
                        sp.dma_start(wgu_scr[par, :, :, bass.ds(k * P, P)], wst[:, 0:NC, :]).then_inc(wgu_wr, 16)
                    if now == "down" and par == 1:
                        k = i - PREP_D[0] + 1
                        sp.wait_ge(w_scaled, PRIMED + 2 * IC + k)
                        sp.dma_start(wdraw, w_down[bass.ds(k * P, P), :]).then_inc(wd_ld, 16)
                    if before == "d" and par == 1:
                        k = i - 1 - PREP_D[0]
                        sp.wait_ge(w_cp, PRIMED + 2 * IC + k + 1)
                        sp.dma_start(wd_scr[:, :, bass.ds(k * P, P)], wst).then_inc(wd_wr, 16)
                    if now == "index" and par == 0:
                        k = i - PREP_GU[0] + 1
                        for ld in wraw_ld:
                            sp.wait_ge(ld, 16 * k)
                        sp.dma_start(idx.bitcast(I32), down_idx[bass.ds(k * P, P), :]).then_inc(idx_ld, 16)
            x_tiles(PREP_GU[0], "index", None)
            sp.dma_start(wq, Wq.rearrange("p (c n) -> p c n", c=NC)).then_inc(w_att, 16)
            sp.dma_start(wkv, Wkv.rearrange("p (c n) -> p c n", c=NC)).then_inc(w_att, 16)
            with sp.Fori(PREP_GU[0] + 1, PREP_GU[1] - 1) as i:
                x_tiles(i, "index", "gu")
            x_tiles(PREP_GU[1] - 1, None, "gu")
            x_tiles(PREP_D[0], "down", "gu")
            with sp.Fori(PREP_D[0] + 1, PREP_D[1] - 1) as i:
                x_tiles(i, "down", "d")
            x_tiles(PREP_D[1] - 1, None, "d")
            x_tiles(PREP_D[1], None, "d")
            with sp.Fori(PREP_D[1] + 1, T // 2) as i:
                x_tiles(i, None, None)
            sp.wait_ge(hs_cp, PRIMED + T)
            sp.wait_ge(wgu_wr, PRIMED + 16 * 2 * IC)
            sp.wait_ge(wd_wr, PRIMED + 16 * NC)
            sp.wait_ge(idx_ld, 16 * IC)
            sp.wait_ge(wd_ld, 16 * NC)
            sp.dma_start(wo, Wo.rearrange("p (h n) -> p h n", h=HEADS)).then_inc(w_att, 16)
            sp.wait_ge(w_kept, 2 * IC + NC)
            sp.dma_start(scale_scr.rearrange("k p -> p k"), row_scales, allow_slow_non_contiguous=True).then_inc(ws_wr, 16)
            sp.dma_start(gam, gamma).then_inc(st_ld, 16)

            def x_rows(blk):
                for pr in range(PAIRS):
                    src = x[bass.ds(blk * BLK + pr * P, P), :]
                    sp.dma_start(xres[:, pr, :], src).then_inc(x_ld, 16)

            def x1_rows(blk):
                for pr in range(PAIRS):
                    sp.wait_ge(x1_done, PRIMED + PAIRS * blk + pr + 1)
                    for b2 in range(2):
                        dst = x1_scr[:, :, bass.ds(blk * BLK_B + 2 * pr + b2, 1), :]
                        src = xres[64 * b2:64 * b2 + 64, pr, :].rearrange("p (j a n) -> p j a n", j=NC, a=1)
                        sp.dma_start(dst, src).then_inc(x1_wr, 16)
            x_rows(0)
            with sp.Fori(0, NBLK - 1) as blk:
                x1_rows(blk)
                sp.wait_ge(x1_wr, 16 * 2 * PAIRS * (blk + 1))
                x_rows(blk + 1)
            assert a_wgu_end <= a_ih
            sp.wait_ge(xn_done, NBLK)
            sp.dma_start(ct, couplingT.rearrange("p (c n) -> p c n", c=NC)).then_inc(ct_ld, 16)
            sp.wait_ge(ws_wr, 16)
            sp.dma_start(wgT, wgu_scr[0]).then_inc(ffn_ld, 16)
            sp.dma_start(wuT, wgu_scr[1]).then_inc(ffn_ld, 16)
            x1_rows(NBLK - 1)
            sp.dma_start(biasq, bias_quad).then_inc(ct_ld, 16)
            sp.dma_start(qn[3], cond_quad).then_inc(ct_ld, 16)
            sp.dma_start(pn[1], cond_quad).then_inc(ct_ld, 16)

            sp.wait_ge(x1_wr, 16 * B)
            for s in range(4):
                sp.dma_start(drive[s], x1_scr[s].rearrange("j b n -> (j b) n")).then_inc(drive_ld[s], 16)
            sp.dma_start(wdT, wd_scr).then_inc(ffn_ld, 16)
            for row, lo, hi in ((gs_row, 0, IC), (us_row, IC, 2 * IC), (ds_row, 2 * IC, 2 * IC + NC)):
                sp.dma_start(row, scale_scr[lo:hi, :].rearrange("k p -> (k p)").partition_broadcast(P)).then_inc(ffn_ld, 16)

            def q_store(i, s):
                sp.wait_ge(rk_q, 4 * i + s + 1)
                sp.dma_start(q_scr[bass.ds(4 * i + s, 1)].rearrange("a j b n -> (a j b) n"), qn[s]).then_inc(q_wr[s], 16)
            def tile_loads(i):
                for s in range(TILE_T):
                    if s == 0:
                        sp.wait_ge(f_vq, PRIMED + i)
                    sp.wait_ge(q_wr[s], PRIMED + 16 * (i + 1))
                    sp.dma_start(qt[32 * s:32 * s + 32, :].rearrange("p (j n) -> p j n", j=NC),
                                 q_scr[bass.ds(i * TILE_T + s, 1)].rearrange("a j b n -> (a b) j n")).then_inc(q_ld, 16)

            def tile_x1(i):
                sp.wait_ge(f_out, PRIMED + i)
                for s in range(TILE_T):
                    sp.dma_start(x1t[32 * s:32 * s + 32, :].rearrange("p (j n) -> p j n", j=NC),
                                 x1_scr[bass.ds(i * TILE_T + s, 1)].rearrange("a j b n -> (a b) j n")).then_inc(x1_ld, 16)

            def tile_store(i):
                sp.wait_ge(f_out, PRIMED + i + 1)
                for s in range(TILE_T):
                    sp.dma_start(out[:, bass.ds(i * TILE_T + s, 1), :].rearrange("b a n -> (b a) n"),
                                 yout[32 * s:32 * s + 32, :]).then_inc(o_wr, 16)

            def next_drive(i, s):
                sp.dma_start(drive[s], x1_scr[bass.ds(4 * i + 4 + s, 1)].rearrange("a j b n -> (a j b) n")).then_inc(drive_ld[s], 16)

            def group(g, drives, out_tile, x1_tile):
                for s in range(4):
                    if g is not None:
                        q_store(g, s)
                    if drives:
                        next_drive(g, s)
                    if s == 2 and out_tile is not None:
                        tile_store(out_tile)
                    if s == 2 and x1_tile is not None:
                        tile_x1(x1_tile)
                if g is not None:
                    tile_loads(g)
            for g in range(LEAD):
                group(g, True, None, 0 if g == LEAD - 1 else None)
            with sp.Fori(LEAD, NTILE - 1) as g:
                group(g, True, g - LEAD, g - LEAD + 1)
            group(NTILE - 1, False, NTILE - 1 - LEAD, NTILE - LEAD)
            for i in range(NTILE - LEAD, NTILE):
                group(None, False, i, i + 1 if i + 1 < NTILE else None)
            sp.wait_ge(o_wr, PRIMED + 16 * TILE_T * NTILE)

        def tile_sums(eng, k, tile):
            i = tile(0)
            if i is not None and k == 7:
                eng.wait_ge(f_xe, i + 1)
                eng.tensor_tensor(vq, vq, eq, ALU.add).then_inc(f_xa, 1)
                eng.wait_ge(f_xa, i + 1)
                wait_if(eng, f_qT, i)
                eng.tensor_tensor(qx8, vq, eq, ALU.subtract).then_inc(f_q8, 1)
            i = tile(2)
            if i is not None and k == 8:
                eng.wait_ge(f_ysc, i + 1)
                eng.wait_ge(x1_ld, 16 * TILE_T * (i + 1))
                wait_if(eng, o_wr, PRIMED + 16 * TILE_T * i)
                eng.tensor_tensor(yout, ysc, x1t, ALU.add).then_inc(f_out, 1)
            i = tile(1)
            if i is not None and k == 10:
                eng.wait_ge(f_te, i + 1)
                eng.tensor_tensor(vt, vt, et, ALU.add).then_inc(f_ta, 1)
                eng.wait_ge(f_ta, i + 1)
                wait_if(eng, f_tT, i)
                eng.tensor_tensor(t8, vt, et, ALU.subtract).then_inc(f_t8, 1)

        @block.gpsimd
        def _(pool):
            for s_ in (hs_cp, x1_done, f_vq, f_out, w_tr, w_cp, wgu_wr, wd_wr, w_scaled, o_wr, *q_wr):
                pool.sem_inc(s_, PRIMED)
            def keep_state(i, par):
                t = 2 * i + par
                pool.wait_ge(hT_done, t + 1)
                pool.tensor_copy(hsT.rearrange("p c (b t) -> p c b t", t=T)[:, :, :, bass.ds(t, 1)],
                                 hT[par].rearrange("p c (b a) -> p c b a", a=1)).then_inc(hs_cp, 1)

            def gather(n, k):
                pool.wait_ge(idx_ld, 16 * (n + 1))
                wait_if(pool, w_scaled, 2 * n - 1 + k + PRIMED)
                pool.sem_inc(gather_go, 1)
                pool.indirect_dma_start(out=wraw[:, k, :], out_offset=None, in_=(w_gate, w_up)[k],
                                        in_offset=bass.IndirectOffsetOnAxis(ap=idx.bitcast(U32), axis=0)).then_inc(wraw_ld[k], 16)
            gather(0, 0)
            gather(0, 1)
            keep_state(0, 0)
            keep_state(0, 1)
            with pool.Fori(1, IC) as i:
                for par in range(2):
                    keep_state(i, par)
                    gather(i, par)
            with pool.Fori(IC, T // 2) as i:
                keep_state(i, 0)
                keep_state(i, 1)

            def group(g, rk, tile):
                if rk:
                    for k in range(16):
                        tile_sums(pool, k, tile)
            in_groups(pool, group)

        @block.tensor
        def _(pe):
            pe.wait_ge(stack_ld, 48)
            pe.wait_ge(bias_split, 6)
            pe.wait_ge(wih_ld, 16)

            def x_part(t, par, prev):
                pe.wait_ge(xt_ld[par], 8 * (t - par) + 16)
                if prev:
                    pe.wait_ge(npre_done, t - 1)
                pe.matmul(ps[:, par, :], sel_b[0:3 * NC, :], bstack[0:3 * NC, :], start=True, stop=False, skip_group_check=True)
                for c in range(NC):
                    for j in range(NC):
                        mm = pe.matmul(ps[32 * j:32 * j + 32, par, 0:3 * P].rearrange("p (g n) -> p g n", g=3), xt[par][:, c, :],
                                       wih[:, c, :].rearrange("p (g j n) -> p g j n", g=3, j=NC)[:, :, j, :],
                                       start=False, stop=False, skip_group_check=True, tile_position=(0, 32 * j))
                mm.then_inc(gx_mm, 1)

            def h_part(t, par):
                for c in range(NC):
                    for j in range(NC):
                        mm = pe.matmul(ps[32 * j:32 * j + 32, par, P:4 * P].rearrange("p (g n) -> p g n", g=3), hT[1 - par][:, c, :],
                                       whh[:, c, :].rearrange("p (g j n) -> p g j n", g=3, j=NC)[:, :, j, :],
                                       start=False, stop=(c == NC - 1), skip_group_check=True, tile_position=(0, 32 * j))
                mm.then_inc(gates_mm, 1)
            x_part(0, 0, False)
            x_part(1, 1, False)
            pe.wait_ge(h0_ld, 32)
            pe.wait_ge(whh_ld, 16)
            h_part(0, 0)
            pe.wait_ge(hT_done, 1)
            h_part(1, 1)
            def turn_rows(n, chunks):
                pe.wait_ge(w_q8, n + 1)
                pe.wait_ge(w_cp, PRIMED + n)
                for c in range(chunks):
                    mm = pe.transpose(ps[:, 2 + c // 8, :].bitcast(BF16)[:, (c % 8) * P:(c % 8 + 1) * P], wq8[:, c * P:(c + 1) * P], id_b1)
                mm.then_inc(w_tr, 1)

            def pair_of_steps(i, before):
                for par in range(2):
                    if before == "gu":
                        turn_rows(2 * (i - 1 - PREP_GU[0]) + par, NC)
                    if before == "d" and par == 1:
                        turn_rows(2 * IC + i - 1 - PREP_D[0], IC)
                    x_part(2 * i + par, par, True)
                    pe.wait_ge(hT_done, 2 * i + par)
                    h_part(2 * i + par, par)
            pe.wait_ge(idb_done, 1)
            pair_of_steps(PREP_GU[0], None)
            with pe.Fori(PREP_GU[0] + 1, PREP_GU[1] + 1) as i:
                pair_of_steps(i, "gu")
            with pe.Fori(PREP_D[0] + 1, PREP_D[1] + 1) as i:
                pair_of_steps(i, "d")
            with pe.Fori(PREP_D[1] + 1, T // 2) as i:
                pair_of_steps(i, None)

            pe.wait_ge(hs_cp, PRIMED + T)
            pe.wait_ge(c_ld, 16 * N_CONST)
            def mean(i):
                if i >= 2:
                    pe.wait_ge(xc_done, i - 1)
                for c in range(NC):
                    mm = pe.matmul(ps[:, i % 2, :], mean_w, hsT[:, c, i * LN_TOK:(i + 1) * LN_TOK], start=(c == 0), stop=(c == NC - 1))
                mm.then_inc(mean_mm, 1)

            def variance(i):
                if i >= 2:
                    pe.wait_ge(ve_done, i - 1)
                pe.wait_ge(sq_done, i + 1)
                for c in range(NC):
                    mm = pe.matmul(ps[:, 2 + i % 2, :], mean_w, sq[i % 2][:, c, :], start=(c == 0), stop=(c == NC - 1))
                mm.then_inc(var_mm, 1)
            mean(0)
            for i in range(1, NLN):
                mean(i)
                variance(i - 1)
            variance(NLN - 1)
            pe.wait_ge(ve_done, NLN)

            def out_proj(blk, part):
                pr, h0 = part // 2, part % 2 * HP
                if h0 == 0:
                    pe.wait_ge(x1_done, PRIMED + PAIRS * (blk - 1) + pr + 1)
                    pe.wait_ge(ao_cp, 4 * (PAIRS * blk + pr + 1))
                for h in range(h0, h0 + HP):
                    mm = pe.matmul(ps[:, 6 + pr, :], aoT[:, h, pr * P:pr * P + P], wo[:, h, :], start=(h == 0), stop=(h == HEADS - 1))
                if h0:
                    mm.then_inc(wo_mm, 1)

            def q_heads(blk):
                for h in range(HEADS):
                    if h >= Q_BANKS:
                        pe.wait_ge(q_ev, 3 * (HEADS * blk + h - Q_BANKS + 1))
                    for c in range(NC):
                        mm = pe.matmul(ps[:, h % Q_BANKS, 0:BLK], wq[:, c, h * DH:(h + 1) * DH], xnb[:, c, :], start=(c == 0), stop=(c == NC - 1))
                    mm.then_inc(q_mm, 1)

            def attn_block(blk, first):
                pe.wait_ge(xn_done, blk + 1)
                if not first:
                    pe.wait_ge(x1_done, PRIMED + PAIRS * (blk - 1))
                    pe.wait_ge(pT_cp, 2 * PAIRS * blk)
                    pe.wait_ge(ao_cp, 4 * PAIRS * blk)
                for c in range(NC):
                    mm = pe.matmul(ps[:, 7, 0:BLK], wkv[:, c, 0:DH], xnb[:, c, :], start=(c == 0), stop=(c == NC - 1))
                mm.then_inc(k_mm, 1)
                for pr in range(PAIRS):
                    for c in range(NC):
                        mm = pe.matmul(ps[:, 5, pr * DH:(pr + 1) * DH], xnb[:, c, pr * P:pr * P + P], wkv[:, c, DH:], start=(c == 0), stop=(c == NC - 1))
                mm.then_inc(v_mm, 1)
                q_heads(blk)
                pe.wait_ge(kr_done, blk + 1)

                def before(part):
                    if not first:
                        out_proj(blk - 1, part)

                def scores(pr):
                    for b2 in range(2):
                        if pr:
                            pe.wait_ge(masked, 2 * PAIRS * blk + 2 * pr - 1 + b2)
                        b = 2 * pr + b2
                        for hp in range(HP):
                            o = ps[:, 2 + 2 * b2 + hp // 4, (hp % 4) * P:(hp % 4 + 1) * P]
                            mm = pe.matmul(o, q_rot[:, b, hp * P:(hp + 1) * P], kr[:, pr * P:(pr + 1) * P], start=True, stop=True)
                        mm.then_inc(s_mm, 1)

                def turned_probs(pr):
                    pe.wait_ge(p_done, 2 * (PAIRS * blk + pr + 1))
                    for half in range(2):
                        n = 2 * pr + half
                        if n >= 2:
                            pe.wait_ge(pT_cp, 2 * PAIRS * blk + n - 1)
                        for hp in range(4 * half, 4 * half + 4):
                            mm = pe.transpose(ps[:, half, (hp % 4) * P:(hp % 4 + 1) * P], probs[:, pr, hp * P:(hp + 1) * P], identf)
                        mm.then_inc(pT_mm, 1)

                def values(pr):
                    pe.wait_ge(pT_cp, 2 * PAIRS * blk + 2 * pr + 2)
                    pe.wait_ge(masked, 2 * PAIRS * (blk + 1))
                    for half in range(2):
                        for b2 in range(2):
                            n = 4 * pr + 2 * half + b2
                            if n >= 3:
                                pe.wait_ge(ao_cp, 4 * PAIRS * blk + n - 2)
                            pe.matmul(ps[:, PV_BANKS[n % 3], :], vtok[64 * b2:64 * b2 + 64, pr, :], pT[64 * b2:64 * b2 + 64, half * 512:(half + 1) * 512],
                                      start=True, stop=True).then_inc(pv_mm, 1)
                before(0)
                pe.wait_ge(qr_done, HEADS * (blk + 1))
                pe.wait_ge(v_cp, blk + 1)
                scores(0)
                before(1)
                scores(1)
                turned_probs(0)
                before(2)
                values(0)
                turned_probs(1)
                before(3)
                values(1)
            pe.wait_ge(w_att, 48)
            attn_block(0, True)
            with pe.Fori(1, NBLK) as blk:
                attn_block(blk, False)
            for part in range(2 * PAIRS):
                out_proj(NBLK - 1, part)

            def mm_mix(o, m, src, first):
                pe.matmul(o, mix[m], src, start=first, stop=False, skip_group_check=True)

            def mix_into(t, s, st, newest):
                o = ps[:, st % 2, 0:P]
                if newest:
                    pe.wait_ge(rk_qT, 4 * t + st + 1)
                elif st == 0:
                    pe.wait_ge(rk_e, t + 1)
                else:
                    pe.wait_ge(rk_qT, 4 * t + st)
                if not newest:
                    mm_mix(o, 0, emp[s % 2], True)
                for k, m in STAGE_MIX[st]:
                    src = (pn[(s - 1) % 2], qn[(s - 1) % 4], *qst)[k]
                    if newest == (k == st + 1):
                        mm_mix(o, m, src, False)

            def stage(g, s, st, last):
                t = 4 * g + s
                if st == 3:
                    mix_into(t, s, st, True)
                pe.wait_ge(rk_th, 4 * t + st + 1)
                for c in range(NC):
                    for j in range(NC):
                        mm = pe.matmul(ps[32 * j:32 * j + 32, st % 2, 0:P], thT[:, c, :], ct[:, c, j * P:(j + 1) * P],
                                       start=False, stop=(c == NC - 1), skip_group_check=True, tile_position=(0, 32 * j))
                mm.then_inc(rk_mm, 1)
                if st < 3:
                    mix_into(t, s, st + 1, False)
                elif not (last and s == 3):
                    mix_into(t + 1, (s + 1) % 4, 0, False)

            def product(i, m, k):
                done = (f_gsc, f_usc)[k]
                wait_if(pe, done, GU_T * i + m - 1)
                for c in range(NC):
                    mm = pe.matmul(ps[:, 2 + 2 * (m % 2) + k, 0:GU_N], qxT[:, c, :], (wgT, wuT)[k][:, c, m * GU_N:(m + 1) * GU_N],
                                   start=(c == 0), stop=(c == NC - 1))
                mm.then_inc((f_g, f_u)[k], 1)

            def slot(k, tile):
                i = tile(0)
                if i is not None:
                    if k == 9:
                        pe.wait_ge(f_q8, i + 1)
                        for c in range(NC):
                            mm = pe.transpose(ps[:, 6, 0:2 * P].bitcast(BF16)[:, c * P:(c + 1) * P], qx8[:, c * P:(c + 1) * P], id_b)
                        mm.then_inc(f_qT, 1)
                    if k == 10:
                        pe.wait_ge(f_qTcp, i + 1)
                    if k >= 10:
                        product(i, (k - 10) // 2, k % 2)
                i = tile(1)
                if i is not None:
                    if k < 2:
                        product(i, 3, k)
                    if k == 15:
                        pe.wait_ge(f_t8, i + 1)
                        wait_if(pe, f_ysc, i)
                        for c in range(IC):
                            mm = pe.transpose(ps[:, 6 + c // 8, :].bitcast(BF16)[:, (c % 8) * P:(c % 8 + 1) * P], t8[:, c * P:(c + 1) * P], id_b)
                        mm.then_inc(f_tT, 1)
                i = tile(2)
                if i is not None:
                    if k == 2:
                        pe.wait_ge(f_tTcp, 2 * i + 2)
                    if 2 <= k < 6:
                        down(i, k - 2)

            def down(i, part):
                for c in range(3 * part, min(3 * part + 3, IC)):
                    mm = pe.matmul(ps[:, 7, :], t8T[:, c, :], wdT[:, c, :], start=(c == 0), stop=(c == IC - 1))
                if part == 3:
                    mm.then_inc(f_y, 1)

            def group(g, rk, tile):
                if isinstance(g, int) and g == 1:
                    pe.wait_ge(ffn_ld, 16 * 6)
                for k in range(16):
                    if rk:
                        stage(g, k // 4, k % 4, isinstance(g, int) and g == NTILE - 1)
                    slot(k, tile)
            pe.wait_ge(ct_ld, 16 * 4)
            pe.wait_ge(rk_mix, len(MIX))
            mix_into(0, 0, 0, False)
            in_groups(pe, group)

        @block.scalar
        def _(act):
            def gru_step(t, par):
                act.wait_ge(gates_mm, t + 1)
                act.activation(rz[par], ps[:, par, P:3 * P].rearrange("p (g n) -> p g n", g=2), ACT.Sigmoid).then_inc(rz_done, 1)
                act.wait_ge(npre_done, t + 1)
                act.activation(nval, npre, ACT.Tanh).then_inc(n_done, 1)
            def scaled_rows(n, src, width):
                act.wait_ge(w_rs, n + 1)
                act.activation(wv[:, 0:width], src, ACT.Copy, scale=rs[:, 0:1]).then_inc(w_scaled, 1)

            def chunks_of(bank, m):
                return ps[:, bank, :].bitcast(BF16)[:, 0:m * P].rearrange("p (c n) -> p c n", n=P)

            def gate_up_out(n):
                act.wait_ge(w_tr, PRIMED + n + 1)
                act.wait_ge(wgu_wr, PRIMED + 16 * n)
                act.activation(wst[:, 0:NC, :], chunks_of(2, NC), ACT.Copy).then_inc(w_cp, 1)

            def down_out(k):
                act.wait_ge(w_tr, PRIMED + 2 * IC + k + 1)
                act.wait_ge(wgu_wr, PRIMED + 16 * 2 * IC)
                act.wait_ge(wd_wr, PRIMED + 16 * k)
                act.activation(wst[:, 8:IC, :], chunks_of(3, IC - 8), ACT.Copy)
                act.activation(wst[:, 0:8, :], chunks_of(2, 8), ACT.Copy).then_inc(w_cp, 1)
            act.wait_ge(c_ld, 16 * N_CONST)
            act.activation(id_b1, identf, ACT.Copy).then_inc(idb_done, 1)
            def gru_pair(i, now, before):
                gru_step(2 * i, 0)
                if now == "gu":
                    scaled_rows(2 * (i - PREP_GU[0]), wraw[:, 0, :], D)
                if now == "d":
                    scaled_rows(2 * IC + i - PREP_D[0], wdraw, INNER)
                if before == "gu":
                    gate_up_out(2 * (i - 1 - PREP_GU[0]) + 1)
                if before == "d":
                    down_out(i - 1 - PREP_D[0])
                gru_step(2 * i + 1, 1)
                if now == "gu":
                    scaled_rows(2 * (i - PREP_GU[0]) + 1, wraw[:, 1, :], D)
                    gate_up_out(2 * (i - PREP_GU[0]))

            gru_pair(0, None, None)
            gru_pair(PREP_GU[0], "gu", None)
            with act.Fori(PREP_GU[0] + 1, PREP_GU[1]) as i:
                gru_pair(i, "gu", "gu")
            gru_pair(PREP_D[0], "d", "gu")
            with act.Fori(PREP_D[0] + 1, PREP_D[1]) as i:
                gru_pair(i, "d", "d")
            gru_pair(PREP_D[1], None, "d")
            with act.Fori(PREP_D[1] + 1, T // 2) as i:
                gru_pair(i, None, None)

            for i in range(NLN):
                act.wait_ge(xc_done, i + 1)
                if i >= 2:
                    act.wait_ge(var_mm, i - 1)
                act.activation(sq[i % 2], hsT[:, :, i * LN_TOK:(i + 1) * LN_TOK], ACT.Square).then_inc(sq_done, 1)
                if i >= 1:
                    act.wait_ge(ve_done, i)
                    act.activation(rstd[:, (i - 1) * LN_TOK:i * LN_TOK], var[i - 1], ACT.Sqrt).then_inc(root_done, 1)
            act.wait_ge(ve_done, NLN)
            act.activation(rstd[:, (NLN - 1) * LN_TOK:], var[NLN - 1], ACT.Sqrt).then_inc(root_done, 1)

            def attn_block(blk):
                act.wait_ge(v_mm, blk + 1)
                act.activation(vtok, ps[:, 5, 0:PAIRS * DH].rearrange("p (a n) -> p a n", a=PAIRS), ACT.Copy).then_inc(v_cp, 1)
                for n in range(2 * PAIRS):
                    act.wait_ge(shifted, 2 * PAIRS * blk + n + 1)
                    pb = probs[:, n // 2, :].rearrange("p (h b j) -> p h b j", h=HP, b=2)[:, :, n % 2, :]
                    act.activation(pb, pb, ACT.Exp).then_inc(exp_done, 1)
                for pr in range(PAIRS):
                    for half in range(2):
                        act.wait_ge(pT_mm, 2 * (PAIRS * blk + pr) + half + 1)
                        if pr and half == 0:
                            act.wait_ge(pv_mm, 4 * (PAIRS * blk + pr))
                        act.activation(pT[:, half * 512:(half + 1) * 512], ps[:, half, :], ACT.Copy).then_inc(pT_cp, 1)
                    for half in range(2):
                        for b2 in range(2):
                            act.wait_ge(pv_mm, 4 * (PAIRS * blk + pr) + 2 * half + b2 + 1)
                            tk = (2 * pr + b2) * T
                            act.activation(aoT[:, 8 * half:8 * half + 8, tk:tk + T],
                                           ps[:, PV_BANKS[(4 * pr + 2 * half + b2) % 3], :].rearrange("p (h t) -> p h t", h=8), ACT.Copy).then_inc(ao_cp, 1)
            with act.Fori(0, NBLK) as blk:
                attn_block(blk)

            def stage(t, s, st):
                n = 4 * t + st
                act.wait_ge(rk_qT, n + 1)
                act.activation(thT, qsT, ACT.Tanh).then_inc(rk_th, 1)
                src = qn[(s - 1) % 4] if st == 0 else qst[st - 1]
                act.activation(cube, src, ACT.Square, scale=3.0 ** -0.5).then_inc(rk_sq, 1)

            def silu_part(i, m):
                act.wait_ge(f_gsc, GU_T * i + m + 1)
                wait_if(act, f_gated, GU_T * i + m - 1)
                act.activation(sig[m % 2], gsc[m % 2], ACT.Sigmoid).then_inc(f_sig, 1)

            def slot(k, tile):
                i = tile(0)
                if i is not None:
                    if k == 5:
                        act.wait_ge(f_rq, i + 1)
                        wait_if(act, f_q8, i)
                        act.activation(vq, qt, ACT.Copy, scale=xrs).then_inc(f_vq, 1)
                    if k == 9:
                        act.wait_ge(f_qT, i + 1)
                        act.activation(qxT, ps[:, 6, 0:2 * P].bitcast(BF16).rearrange("p (c n) -> p c n", c=NC), ACT.Copy).then_inc(f_qTcp, 1)
                    if k in (12, 14):
                        silu_part(i, (k - 12) // 2)
                i = tile(1)
                if i is not None:
                    if k in (0, 2):
                        silu_part(i, 2 + k // 2)
                    if k == 8:
                        act.wait_ge(f_rt, i + 1)
                        wait_if(act, f_t8, i)
                        act.activation(vt, tt, ACT.Copy, scale=trs).then_inc(f_vt, 1)
                i = tile(2)
                if i is not None:
                    if k == 0:
                        act.wait_ge(f_tT, i + 1)
                        wait_if(act, f_y, i)
                        act.activation(t8T[:, 0:8, :], ps[:, 6, :].bitcast(BF16).rearrange("p (c n) -> p c n", c=8), ACT.Copy).then_inc(f_tTcp, 1)
                    if k == 1:
                        act.activation(t8T[:, 8:IC, :], ps[:, 7, :].bitcast(BF16)[:, 0:(IC - 8) * P].rearrange("p (c n) -> p c n", c=IC - 8),
                                       ACT.Copy).then_inc(f_tTcp, 1)

            def group(g, rk, tile):
                for k in range(16):
                    if rk:
                        stage(4 * g + k // 4, k // 4, k % 4)
                    slot(k, tile)
            in_groups(act, group)

        @block.vector
        def _(dve):
            def bcast(row, nb):
                return row.unsqueeze(1).to_broadcast([P, nb, T])

            dve.wait_ge(b_ld, 16 * N_BIAS)
            b4, r4 = bg[0:NC, :], bres[0:NC, :]
            dve.tensor_copy(sel_b[0:3 * NC, :], sel_f[0:3 * NC, :]).then_inc(bias_split, 1)
            dve.tensor_tensor(b4[:, P:3 * P], b4[:, P:3 * P], r4[:, 0:2 * P], ALU.add).then_inc(bias_split, 1)
            dve.wait_ge(bias_split, 2)
            dve.tensor_copy(bparts[0][0:NC, :], b4).then_inc(bias_split, 1)
            dve.wait_ge(bias_split, 3)
            dve.tensor_tensor(r4, b4, bparts[0][0:NC, :], ALU.subtract).then_inc(bias_split, 1)
            dve.wait_ge(bias_split, 4)
            dve.tensor_copy(bparts[1][0:NC, :], r4).then_inc(bias_split, 1)
            dve.wait_ge(bias_split, 5)
            dve.tensor_tensor(bparts[2][0:NC, :], r4, bparts[1][0:NC, :], ALU.subtract).then_inc(bias_split, 1)

            def grid_of(v, x_, e):
                v.need(v.did(dve.tensor_scalar(e.bitcast(U32), x_.bitcast(U32), EXP_BITS, None, ALU.bitwise_and)))
                return v.did(dve.tensor_scalar(e, e, FP8_TINY, ROUND_AT, ALU.max, ALU.mult))

            def weight_scale(n, col, src):
                v = Steps(dve, w_v, W_STEPS * n)
                v.need(v.did(dve.tensor_reduce(am, src, AX.X, ALU.max, apply_absolute_value=True)))
                scaled = v.did(dve.tensor_scalar(wsc, am, 1.0 / FP8_MAX, None, ALU.mult))
                dve.tensor_scalar(row_scales[:, bass.ds(col, 1)], am, 1.0 / FP8_MAX, None, ALU.mult).then_inc(w_kept, 1)
                v.need(scaled)
                dve.reciprocal(rs, wsc).then_inc(w_rs, 1)

            def round_add(n, width):
                v = Steps(dve, w_v, W_STEPS * n + 2)
                x_, e = wv[:, 0:width], wexp[:, 0:width]
                dve.wait_ge(w_scaled, PRIMED + n + 1)
                v.need(grid_of(v, x_, e))
                v.did(dve.tensor_tensor(x_, x_, e, ALU.add))
                assert v.n + 2 == W_STEPS

            def round_off(n, width):
                dve.wait_ge(w_v, W_STEPS * (n + 1))
                dve.wait_ge(w_tr, PRIMED + n)
                dve.tensor_tensor(wq8[:, 0:width], wv[:, 0:width], wexp[:, 0:width], ALU.subtract).then_inc(w_q8, 1)
            W_STEPS = 5

            dve.wait_ge(h0_ld, 32)

            def gru_pair(i, now, before):
                for par in range(2):
                    t = 2 * i + par
                    n = 2 * (i - PREP_GU[0]) + par
                    if (before, now)[par] == "gu":
                        round_add(n - 1, D)
                        round_off(n - 1, D)
                    if now == "gu":
                        dve.wait_ge(wraw_ld[par], 16 * (i - PREP_GU[0] + 1))
                        weight_scale(n, i - PREP_GU[0] + IC * par, wraw[:, par, :])
                    n = 2 * IC + i - PREP_D[0]
                    if before == "d" and par == 0:
                        round_off(n - 1, INNER)
                    if now == "d":
                        if par == 0:
                            dve.wait_ge(wd_ld, 16 * (i - PREP_D[0] + 1))
                            weight_scale(n, n, wdraw)
                        else:
                            round_add(n, INNER)
                    r, z = rz[par][:, 0, :], rz[par][:, 1, :]
                    dve.wait_ge(rz_done, t + 1)
                    dve.tensor_tensor(rh, r, ps[:, par, 3 * P:4 * P], ALU.mult).then_inc(rh_done, 1)
                    dve.wait_ge(rh_done, t + 1)
                    dve.tensor_tensor(npre, rh, ps[:, par, 0:P], ALU.add).then_inc(npre_done, 1)
                    dve.tensor_tensor(zh, z, h_q[1 - par], ALU.mult).then_inc(zh_done, 1)
                    dve.tensor_scalar(omz, z, -1.0, 1.0, ALU.mult, ALU.add).then_inc(omz_done, 1)
                    dve.wait_ge(n_done, t + 1)
                    dve.wait_ge(omz_done, t + 1)
                    dve.tensor_tensor(nz, omz, nval, ALU.mult).then_inc(nz_done, 1)
                    dve.wait_ge(zh_done, t + 1)
                    dve.wait_ge(nz_done, t + 1)
                    dve.tensor_tensor(h_q[par], nz, zh, ALU.add).then_inc(h_done, 1)
                    dve.wait_ge(h_done, t + 1)
                    dve.wait_ge(hs_cp, PRIMED + t)
                    dve.transpose(hT[par].rearrange("p c b -> p (c b)"), h_q[par]).then_inc(hT_done, 1)
            gru_pair(0, None, None)
            gru_pair(PREP_GU[0], "gu", None)
            with dve.Fori(PREP_GU[0] + 1, PREP_GU[1]) as i:
                gru_pair(i, "gu", "gu")
            gru_pair(PREP_D[0], "d", "gu")
            with dve.Fori(PREP_D[0] + 1, PREP_D[1]) as i:
                gru_pair(i, "d", "d")
            gru_pair(PREP_D[1], None, "d")
            with dve.Fori(PREP_D[1] + 1, T // 2) as i:
                gru_pair(i, None, None)

            def centred(i):
                dve.wait_ge(mean_mm, i + 1)
                for c in range(NC):
                    one = hsT[:, c, i * LN_TOK:(i + 1) * LN_TOK]
                    mm = dve.tensor_tensor(one, one, ps[:, i % 2, :], ALU.subtract)
                mm.then_inc(xc_done, 1)

            def spread(i):
                dve.wait_ge(var_mm, i + 1)
                dve.tensor_scalar(var[i], ps[:, 2 + i % 2, :], LN_EPS, None, ALU.add).then_inc(ve_done, 1)

            def inverse_root(i):
                v = Steps(dve, ln_v, LN_STEPS * i)
                a, out_ = newt[1], rstd[:, i * LN_TOK:(i + 1) * LN_TOK]
                dve.wait_ge(root_done, i + 1)
                v.need(v.did(dve.reciprocal(newt[0], out_)))
                v.need(v.did(dve.tensor_tensor(a, newt[0], newt[0], ALU.mult)))
                v.need(v.did(dve.tensor_tensor(a, a, var[i], ALU.mult)))
                v.need(v.did(dve.tensor_scalar(a, a, -0.5, 1.5, ALU.mult, ALU.add)))
                v.need(v.did(dve.tensor_tensor(out_, newt[0], a, ALU.mult)))
                assert v.n == LN_STEPS
            LN_STEPS = 5
            centred(0)
            for i in range(1, NLN):
                centred(i)
                spread(i - 1)

            def norm(blk):
                for c in range(NC):
                    mm = dve.scalar_tensor_tensor(out=xnb[:, c, :], in0=hsT[:, c, bass.ds(blk * BLK, BLK)], scalar=gam[:, c:c + 1],
                                                  in1=rstd[:, bass.ds(blk * BLK, BLK)], op0=ALU.mult, op1=ALU.mult)
                mm.then_inc(xn_done, 1)

            def by_time(a):
                return a.rearrange("p (b t) -> p b t", t=T)

            def rotated(dst, share, src, tr, done):
                dve.tensor_tensor(dst, src, bcast(trigs[:, tr, :], BLK_B), ALU.mult).then_inc(done, 1)
                for a, b in ((0, DH // 2), (DH // 2, 0)):
                    dve.tensor_tensor(share[b:b + DH // 2], src[a:a + DH // 2], bcast(trigs[:, tr + 1, :], BLK_B)[a:a + DH // 2],
                                      ALU.mult).then_inc(done, 1)

            def q_out(blk):
                for h in range(HEADS + 1):
                    if h < HEADS:
                        dve.wait_ge(q_mm, HEADS * blk + h + 1)
                        if h >= 2:
                            dve.wait_ge(qr_done, HEADS * blk + h - 1)
                        rotated(q_rot[:, :, h * T:(h + 1) * T], by_time(turned[h % 2]), by_time(ps[:, h % Q_BANKS, 0:BLK]), 0, q_ev)
                    if h >= 1:
                        dve.wait_ge(q_ev, 3 * (HEADS * blk + h))
                        one = q_rot[:, :, (h - 1) * T:h * T]
                        dve.tensor_tensor(one, one, by_time(turned[(h - 1) % 2]), ALU.add).then_inc(qr_done, 1)

            def softmax(blk, pr):
                def of(n):
                    return probs[:, pr, :].rearrange("p (h b j) -> p h b j", h=HP, b=2)[:, :, n % 2, :]

                def row(a, n):
                    return a[:, n, :].unsqueeze(2).to_broadcast([P, HP, T])

                def at(n):
                    return 2 * PAIRS * blk + n + 1
                two = (2 * pr, 2 * pr + 1)
                for n in two:
                    dve.wait_ge(s_mm, at(n))
                    own = ps[:, 2 + 2 * (n % 2):4 + 2 * (n % 2), :].rearrange("p a (h b j) -> p (a h) b j", b=2, j=T)[:, :, n % 2, :]
                    dve.tensor_tensor(of(n), own, bcast(masks, HP), ALU.add).then_inc(masked, 1)
                for n in two:
                    dve.wait_ge(masked, at(n))
                    dve.tensor_reduce(smax[:, n, :], of(n), AX.X, ALU.max).then_inc(max_done, 1)
                for n in two:
                    dve.wait_ge(max_done, at(n))
                    dve.tensor_tensor(of(n), of(n), row(smax, n), ALU.subtract).then_inc(shifted, 1)
                for n in two:
                    dve.wait_ge(exp_done, at(n))
                    dve.tensor_reduce(ssum[:, n, :], of(n), AX.X, ALU.add).then_inc(sum_done, 1)
                for n in two:
                    dve.wait_ge(sum_done, at(n))
                    dve.reciprocal(ssum[:, n, :], ssum[:, n, :]).then_inc(inv_done, 1)
                for n in two:
                    dve.wait_ge(inv_done, at(n))
                    dve.tensor_tensor(of(n), of(n), row(ssum, n), ALU.mult).then_inc(p_done, 1)

            def residual(blk):
                for pr in range(PAIRS):
                    dve.wait_ge(wo_mm, PAIRS * blk + pr + 1)
                    dve.wait_ge(x_ld, 16 * PAIRS * (blk + 1))
                    dve.tensor_tensor(xres[:, pr, :], ps[:, 6 + pr, :], xres[:, pr, :], ALU.add).then_inc(x1_done, 1)

            def attn_block(blk, first, last):
                dve.wait_ge(k_mm, blk + 1)
                rotated(by_time(kr), by_time(kturned), by_time(ps[:, 7, 0:BLK]), 2, k_parts)
                dve.wait_ge(k_parts, 3 * (blk + 1))
                dve.tensor_tensor(kr, kr, kturned, ALU.add).then_inc(kr_done, 1)
                q_out(blk)
                for pr in range(PAIRS):
                    softmax(blk, pr)
                if first:
                    for i in range(1, NLN):
                        inverse_root(i)
                if not last:
                    norm(blk + 1)
                if not first:
                    residual(blk - 1)
            dve.wait_ge(st_ld, 16)
            inverse_root(0)
            norm(0)
            spread(NLN - 1)
            attn_block(0, True, False)
            with dve.Fori(1, NBLK - 1) as blk:
                attn_block(blk, False, False)
            attn_block(NBLK - 1, False, True)
            residual(NBLK - 1)

            dve.wait_ge(x1_wr, 16 * B)
            dve.wait_ge(ct_ld, 16 * 4)
            for m, weight in enumerate(MIX):
                dve.tensor_scalar(mix[m], identf, float(weight), None, ALU.mult).then_inc(rk_mix, 1)
            dve.tensor_copy(id_b, identf).then_inc(rk_start, 1)
            dve.tensor_scalar(biasq, biasq, -ALPHA / BETA, None, ALU.add).then_inc(rk_start, 1)
            dve.tensor_scalar(pn[1], pn[1], -ALPHA / BETA, None, ALU.add).then_inc(rk_start, 1)
            dve.wait_ge(drive_ld[0], 16)
            dve.wait_ge(rk_start, 3)
            dve.tensor_tensor(dsum, drive[0], biasq, ALU.add).then_inc(rk_start, 1)
            dve.wait_ge(rk_start, 4)
            dve.tensor_tensor(emp[0], dsum, pn[1], ALU.subtract).then_inc(rk_e, 1)
            dve.transpose(qsT.rearrange("p c b -> p (c b)"), qn[3]).then_inc(rk_qT, 1)

            def stage(v, g, s, st, last, fill):
                t = 4 * g + s
                n = 4 * t + st
                q, p = qn[(s - 1) % 4], pn[(s - 1) % 2]
                qs = q if st == 0 else qst[st - 1]
                a = (DT / 2, DT / 2, DT, DT / 6)[st]
                stt = dve.scalar_tensor_tensor
                end = last and s == 3
                if st == 0:
                    v.did(dve.tensor_scalar(w1, p, float(P_NEXT[0]), None, ALU.mult))
                fill()
                if st == 2 and not end:
                    dve.wait_ge(drive_ld[(s + 1) % 4], 16 * (g + 1 + (s == 3)))
                    v.did(dve.tensor_tensor(dsum, drive[(s + 1) % 4], biasq, ALU.add))
                dve.wait_ge(rk_sq, n + 1)
                e = v.did(stt(out=ebuf, in0=cube, scalar=1.0, in1=qs, op0=ALU.subtract, op1=ALU.mult))
                if st == 0:
                    v.need(e - 1)
                wn = v.did(stt(out=(w2, w3, w4, w5)[st], in0=qs, scalar=float(P_NEXT[1 + st]), in1=(w1, w2, w3, w4)[st], op0=ALU.mult, op1=ALU.add))
                v.need(e)
                if st < 3:
                    gs = v.did(stt(out=gbuf, in0=ebuf, scalar=-a, in1=q, op0=ALU.mult, op1=ALU.add))
                else:
                    gs = v.did(dve.tensor_scalar(gbuf, ebuf, -a, None, ALU.mult))
                    v.need(wn)
                    pc = v.did(dve.tensor_scalar(pn[s % 2], w5, CLAMP - ALPHA / BETA, -CLAMP - ALPHA / BETA, ALU.min, ALU.max))
                    v.need(pc)
                    if not end:
                        dve.tensor_tensor(emp[(s + 1) % 2], dsum, pn[s % 2], ALU.subtract).then_inc(rk_e, 1)
                v.need(gs)
                dve.wait_ge(rk_mm, n + 1)
                dst = qst[st] if st < 3 else qpre
                v.need(v.did(stt(out=dst, in0=ps[:, st % 2, 0:P], scalar=a, in1=gbuf, op0=ALU.mult, op1=ALU.add)))
                if st == 3:
                    wait_if(dve, q_wr[s], PRIMED + 16 * g)
                    dve.tensor_scalar(qn[s], qpre, CLAMP, -CLAMP, ALU.min, ALU.max).then_inc(rk_q, 1)
                    dve.wait_ge(rk_q, t + 1)
                    dst = qn[s]
                if not (end and st == 3):
                    dve.transpose(qsT.rearrange("p c b -> p (c b)"), dst).then_inc(rk_qT, 1)

            HALVES = ((0, INNER // 2), (INNER // 2, INNER))

            def slot(v, k, tile, rk):
                i = tile(0)
                if i is not None:
                    if k == 4:
                        dve.wait_ge(q_ld, 16 * TILE_T * (i + 1))
                        v.did(dve.tensor_reduce(xam, qt, AX.X, ALU.max, apply_absolute_value=True))
                    if k == 5:
                        v.need(v.did(dve.tensor_scalar(xsx, xam, 1.0 / FP8_MAX, None, ALU.mult)))
                        dve.reciprocal(xrs, xsx).then_inc(f_rq, 1)
                    if k == 6:
                        dve.wait_ge(f_vq, PRIMED + i + 1)
                        v.did(dve.tensor_scalar(eq.bitcast(U32), vq.bitcast(U32), EXP_BITS, None, ALU.bitwise_and))
                    if k == 7:
                        dve.tensor_scalar(eq, eq, FP8_TINY, ROUND_AT, ALU.max, ALU.mult).then_inc(f_xe, 1)
                    for m in range(GU_T):
                        gated_part(v, i, m, k - 12 - 2 * m)
                i = tile(1)
                if i is not None:
                    for m in range(GU_T):
                        gated_part(v, i, m, 16 + k - 12 - 2 * m)
                    if k in (5, 6):
                        lo, hi = HALVES[k - 5]
                        v.did(dve.tensor_reduce(tam2[:, k - 5:k - 4], tt[:, lo:hi], AX.X, ALU.max, apply_absolute_value=True))
                    if k == 7:
                        v.did(dve.tensor_reduce(tam, tam2, AX.X, ALU.max))
                i2 = tile(2)
                if i2 is not None:
                    if k == 7:
                        dve.wait_ge(f_y, i2 + 1)
                        dve.wait_ge(f_out, PRIMED + i2)
                        dve.scalar_tensor_tensor(out=ysc, in0=ps[:, 7, :], scalar=tsx, in1=ds_row, op0=ALU.mult, op1=ALU.mult).then_inc(f_ysc, 1)
                if i is not None:
                    if k == 8:
                        wait_if(dve, f_ysc, i)
                        v.need(v.did(dve.tensor_scalar(tsx, tam, 1.0 / FP8_MAX, None, ALU.mult)))
                        dve.reciprocal(trs, tsx).then_inc(f_rt, 1)
                    if k == 9:
                        dve.wait_ge(f_vt, i + 1)
                        v.did(dve.tensor_scalar(et.bitcast(U32), vt.bitcast(U32), EXP_BITS, None, ALU.bitwise_and))
                    if k == 10:
                        dve.tensor_scalar(et, et, FP8_TINY, ROUND_AT, ALU.max, ALU.mult).then_inc(f_te, 1)
                if not rk:
                    tile_sums(dve, k, tile)

            def gated_part(v, i, m, phase):
                b, cols = m % 2, slice(m * GU_N, (m + 1) * GU_N)
                if phase == 0:
                    dve.wait_ge(f_g, GU_T * i + m + 1)
                    dve.scalar_tensor_tensor(out=gsc[b], in0=ps[:, 2 + 2 * b, 0:GU_N], scalar=xsx, in1=gs_row[:, cols],
                                             op0=ALU.mult, op1=ALU.mult).then_inc(f_gsc, 1)
                if phase == 1:
                    dve.wait_ge(f_u, GU_T * i + m + 1)
                    dve.scalar_tensor_tensor(out=usc[b], in0=ps[:, 3 + 2 * b, 0:GU_N], scalar=xsx, in1=us_row[:, cols],
                                             op0=ALU.mult, op1=ALU.mult).then_inc(f_usc, 1)
                    dve.wait_ge(f_usc, GU_T * i + m + 1)
                    v.did(dve.tensor_tensor(usc[b], gsc[b], usc[b], ALU.mult))
                if phase == 2:
                    dve.wait_ge(f_sig, GU_T * i + m + 1)
                    dve.tensor_tensor(tt[:, cols], sig[b], usc[b], ALU.mult).then_inc(f_gated, 1)

            counts = {}

            def group(g, rk, tile):
                if not isinstance(g, int):
                    base = counts["lead"] + (g - LEAD) * GROUP_STEPS
                else:
                    base = counts.get("next", 0)
                v = Steps(dve, rk_v, base)
                if isinstance(g, int) and g == 1:
                    dve.wait_ge(ffn_ld, 16 * 6)
                for k in range(16):
                    if rk:
                        stage(v, g, k // 4, k % 4, isinstance(g, int) and g == NTILE - 1, lambda: slot(v, k, tile, rk))
                    else:
                        v.need(v.n)
                        slot(v, k, tile, rk)
                if isinstance(g, int):
                    counts["next"] = counts.get("next", 0) + v.n
                    if g == LEAD - 1:
                        counts["lead"] = counts["next"]
                else:
                    assert v.n == GROUP_STEPS, v.n
                    counts["next"] += (NTILE - 1 - LEAD) * GROUP_STEPS
            in_groups(dve, group)


def kernel(**inputs):
    import numpy as np
    import concourse.bacc as bacc
    from concourse.bass_utils import run_bass_kernel_spmd

    a = {k: np.asarray(v) for k, v in inputs.items()}

    def by_block(w_):
        return w_.reshape(NC, NC, 32, -1).transpose(0, 2, 1, 3).reshape(P, -1)

    def quad(m):
        return m.reshape(B, NC, P).transpose(1, 0, 2).reshape(P, P)

    wih = a["L0_cond_W_ih"].reshape(D, GATES, D)[:, [2, 0, 1]].reshape(D, -1)
    b_ih, b_hh = a["L0_cond_b_ih"], a["L0_cond_b_hh"]
    x_ = a["x"]
    trig, mask, sel, mean_of = constants(np)
    arrays = {
        "xT": x_.reshape(B, T, NC, P).transpose(1, 3, 2, 0).reshape(T, P, NC * B),
        "x": x_.reshape(TOK, D),
        "cond_quad": quad(a["cond_2048"]),
        "cond_T": by_block(a["cond_2048"].T),
        "W_ih": wih.reshape(NC, P, -1).transpose(1, 0, 2).reshape(P, -1),
        "W_hh": by_block(a["L0_cond_W_hh"]),
        "bias_ih": b_ih.reshape(GATES, NC, P), "bias_hh": b_hh.reshape(GATES, NC, P),
        "sel": sel,
        "gamma": by_block(a["L0_attn_gamma"][:, None]),
        "Wq": by_block(a["L0_attn_Wq"]), "Wkv": by_block(a["L0_attn_Wkv"]),
        "Wo": a["L0_attn_Wo"].reshape(HEADS, DH, D).transpose(1, 0, 2).reshape(P, -1),
        "couplingT": by_block(a["L0_cond2_coupling"].T),
        "bias_quad": quad(np.broadcast_to(a["L0_cond2_bias"], (B, D))),
        "w_gate": a["L0_ffn_w_gate"], "w_up": a["L0_ffn_w_up"], "w_down": a["L0_ffn_w_down"],
        "down_idx": a["L0_ffn_down_reorder_index"].reshape(INNER, 1),
        "ident": np.eye(P, dtype=np.float32), "mean_of": mean_of, "trig": trig, "mask": mask,
    }
    nc = bacc.Bacc("TRN2", target_bir_lowering=False, num_devices=1)
    arrays = {f"in_{k}": np.ascontiguousarray(v) for k, v in arrays.items()}
    aps = {k[3:]: nc.dram_tensor(k, v.shape, mybir.dt.from_np(v.dtype), kind="ExternalInput").ap() for k, v in arrays.items()}
    x1_scr = nc.dram_tensor("x1_scr", (T, NC, B, P), F32, kind="Internal").ap()
    q_scr = nc.dram_tensor("q_scr", (T, NC, B, P), F32, kind="Internal").ap()
    wgu_scr = nc.dram_tensor("wgu_scr", (2, P, NC, INNER), BF16, kind="Internal").ap()
    wd_scr = nc.dram_tensor("wd_scr", (P, IC, D), BF16, kind="Internal").ap()
    scale_scr = nc.dram_tensor("scale_scr", (2 * IC + NC, P), F32, kind="Internal").ap()
    out = nc.dram_tensor("out_0", (B, T, D), F32, kind="ExternalOutput").ap()
    gru_attn_rk4_ffn(nc, **aps, x1_scr=x1_scr, q_scr=q_scr, wgu_scr=wgu_scr,
                     wd_scr=wd_scr, scale_scr=scale_scr, out=out)
    r = run_bass_kernel_spmd(nc, [arrays], core_ids=[0])
    return r.results[0]["out_0"]


def constants(np):
    inv = 1.0 / 10000.0 ** (np.arange(0, DH, 2, dtype=np.float32) / np.float32(DH))
    fr = (np.arange(T, dtype=np.float32)[None, :] * inv.astype(np.float32)[:, None]).astype(np.float32)
    fr = np.concatenate([fr, fr])
    cos, sin = np.cos(fr.astype(np.float64)), np.sin(fr.astype(np.float64))
    sc = float(DH) ** -0.5
    sin[DH // 2:] *= -1
    trig = np.stack([cos * sc, sin * sc, cos, sin]).astype(np.float32)
    i, j = np.arange(P)[:, None] % T, np.arange(T)[None, :]
    mask = np.where(j > i, -np.finfo(np.float32).max, 0).astype(np.float32)
    sel = np.tile(np.repeat(np.eye(NC, dtype=np.float32), B, axis=1), (3, 1))
    mean_of = np.full((P, P), 1.0 / D, np.float32)
    return trig, mask, sel, mean_of
```
